# Optimizing a Trainium2 kernel written in Bass

```python
import numpy as np
import jax
import jax.numpy as jnp

def _softmax(x, axis=-1):
    return jax.nn.softmax(x, axis=axis)

def _gelu(x):
    return jax.nn.gelu(x, approximate=True)

def _silu(x):
    return jax.nn.silu(x)

def _sigmoid(x):
    return jax.nn.sigmoid(x)

def _layernorm(x, axis=-1, eps=1e-05):
    m = jnp.mean(x, axis=axis, keepdims=True)
    v = jnp.var(x, axis=axis, keepdims=True)
    return (x - m) / jnp.sqrt(v + eps)

def _scatter_add(tgt, idx, src, axis=0):
    return tgt.at[idx].add(src)

def _segment_sum(src, seg, n):
    return jax.ops.segment_sum(src, seg, n)
kernel_name = 'mk_gnn_resnorm_d4_gnn_r32_f1be43'

def setup_inputs(seed: int=0):
    np.random.seed(seed)
    _w = jnp.asarray

    def _rec_inputs():
        import jax
        import jax.numpy as jnp
        _gk = jax.random.key(seed)
        x = -0.0008691 + 1 * jax.random.normal(jax.random.fold_in(_gk, 1), (3125, 128), jnp.float32)
        src = jax.random.randint(jax.random.fold_in(_gk, 2), (50000,), 0, 3125, jnp.int32)
        dst = jax.random.randint(jax.random.fold_in(_gk, 3), (50000,), 0, 3125, jnp.int32)
        _o = jnp.argsort(dst, stable=True)
        src = src[_o]
        dst = dst[_o]
        edge_attr_128 = -8.513e-05 + 0.999844 * jax.random.normal(jax.random.fold_in(_gk, 12), (50000, 128), jnp.float32)
        edge_weight = jax.random.uniform(jax.random.fold_in(_gk, 14), (50000,), jnp.float32, 0.0, 0.999998)
        return (x, src, dst, edge_attr_128, edge_weight)
    x, src, dst, edge_attr_128, edge_weight = _rec_inputs()

    def _L0_gnn_setup():
        import jax, jax.numpy as jnp
        import numpy as np
        N, E, D, G, H, O = (10000, 20000, 128, 128, 512, 128)

        def mish(x):
            return x * jnp.tanh(jax.nn.softplus(x))
        key = jax.random.key(seed)
        ks = jax.random.split(key, 10)
        nodes = jax.random.normal(ks[0], (N, D), dtype=jnp.float32)
        edges = jax.random.normal(ks[1], (E, D), dtype=jnp.float32)
        globals_g = jax.random.normal(ks[2], (1, G), dtype=jnp.float32)
        senders = jax.random.randint(ks[3], (E,), 0, N)
        receivers = jax.random.randint(ks[4], (E,), 0, N)
        lim_e = np.sqrt(6.0 / (D + D)).astype(np.float32)
        W_e_k = jax.random.uniform(ks[5], (D, D), jnp.float32, -lim_e, lim_e)
        W_e_b = jnp.zeros((D,), jnp.float32)
        eps = jnp.zeros((1, 1), jnp.float32)
        lim1 = np.sqrt(6.0 / (D + G + H)).astype(np.float32)
        W1 = jax.random.uniform(ks[6], (D + G, H), jnp.float32, -lim1, lim1)
        b1 = jnp.zeros((H,), jnp.float32)
        lim2 = np.sqrt(6.0 / (H + O)).astype(np.float32)
        W2 = jax.random.uniform(ks[7], (H, O), jnp.float32, -lim2, lim2)
        b2 = jnp.zeros((O,), jnp.float32)
        return {'nodes': nodes, 'edges': edges, 'globals_g': globals_g, 'W_e_k': W_e_k, 'W_e_b': W_e_b, 'eps': eps, 'W1': W1, 'b1': b1, 'W2': W2, 'b2': b2, 'senders': senders, 'receivers': receivers}
    _L0_gnn_all = _L0_gnn_setup()
    _L0_gnn_in = {k: v for k, v in _L0_gnn_all.items() if k in ('globals_g', 'W_e_k', 'W_e_b', 'eps', 'W1', 'b1', 'W2', 'b2')}
    del _L0_gnn_all

    def _L1_gnn_setup():
        import jax, jax.numpy as jnp
        import numpy as np
        N_NODES = 50000
        N_EDGES = 25000
        D = 128

        def _sage_conv(h, src, dst, W_self, W_neigh, b, n_nodes):
            msg = h[src]
            agg = jax.ops.segment_sum(msg, dst, num_segments=n_nodes)
            deg = jax.ops.segment_sum(jnp.ones((src.shape[0],), h.dtype), dst, num_segments=n_nodes)
            h_neigh = agg / jnp.maximum(deg, 1.0)[:, None]
            return h @ W_self + h_neigh @ W_neigh + b
        key = jax.random.key(seed)
        ks = jax.random.split(key, 8)
        scale = 1.0 / np.sqrt(D)
        return {'x': jax.random.normal(ks[0], (N_NODES, D), jnp.float32), 'src': jax.random.randint(ks[1], (N_EDGES,), 0, N_NODES, jnp.int64 if jax.config.jax_enable_x64 else jnp.int32), 'dst': jax.random.randint(ks[2], (N_EDGES,), 0, N_NODES, jnp.int64 if jax.config.jax_enable_x64 else jnp.int32), 'W_self0': jax.random.normal(ks[3], (D, D), jnp.float32) * scale, 'W_neigh0': jax.random.normal(ks[4], (D, D), jnp.float32) * scale, 'b0': jnp.zeros((D,), jnp.float32), 'W_self1': jax.random.normal(ks[5], (D, D), jnp.float32) * scale, 'W_neigh1': jax.random.normal(ks[6], (D, D), jnp.float32) * scale, 'b1': jnp.zeros((D,), jnp.float32)}
    _L1_gnn_all = _L1_gnn_setup()
    _L1_gnn_in = {k: v for k, v in _L1_gnn_all.items() if k in ('W_self0', 'W_neigh0', 'b0', 'W_self1', 'W_neigh1', 'b1')}
    del _L1_gnn_all

    def _L2_gnn_setup():
        import jax, jax.numpy as jnp
        import numpy as np
        N_NODES = 3125
        N_EDGES = 25000
        DIM = 128
        BN_EPS = 1e-05
        L2_EPS = 1e-12
        key = jax.random.key(seed)
        k1, k2, k3, k4 = jax.random.split(key, 4)
        x = jax.random.normal(k1, (N_NODES, DIM), dtype=jnp.float32)
        W = jax.random.normal(k2, (DIM, DIM), dtype=jnp.float32) * (1.0 / np.sqrt(DIM))
        gamma = jnp.ones((DIM,), dtype=jnp.float32)
        beta = jnp.zeros((DIM,), dtype=jnp.float32)
        src = jax.random.randint(k3, (N_EDGES,), 0, N_NODES, dtype=jnp.int64)
        dst = jax.random.randint(k4, (N_EDGES,), 0, N_NODES, dtype=jnp.int64)
        return {'x': x, 'W': W, 'gamma': gamma, 'beta': beta, 'src': src, 'dst': dst}
    _L2_gnn_all = _L2_gnn_setup()
    _L2_gnn_in = {k: v for k, v in _L2_gnn_all.items() if k in ('W', 'gamma', 'beta')}
    del _L2_gnn_all

    def _L3_gnn_setup():
        import jax, jax.numpy as jnp
        import numpy as np
        N, E = (50000, 25000)
        IN_DIM = 128
        OUT_DIM = 128
        H = 8
        D = OUT_DIM // H
        LN_EPS = 1e-05
        key = jax.random.key(seed)
        ks = jax.random.split(key, 16)
        s_in = 1.0 / np.sqrt(IN_DIM)
        s_out = 1.0 / np.sqrt(OUT_DIM)
        return {'x': jax.random.normal(ks[0], (N, IN_DIM), dtype=jnp.float32), 'edge_index': jax.random.randint(ks[1], (2, E), 0, N, dtype=jnp.int32), 'edge_attr': jax.random.uniform(ks[2], (E,), dtype=jnp.float32), 'Wq': jax.random.normal(ks[3], (H, IN_DIM, D), dtype=jnp.float32) * s_in, 'bq': jnp.zeros((H, D), dtype=jnp.float32), 'Wk': jax.random.normal(ks[4], (H, IN_DIM, D), dtype=jnp.float32) * s_in, 'bk': jnp.zeros((H, D), dtype=jnp.float32), 'Wv': jax.random.normal(ks[5], (H, IN_DIM, D), dtype=jnp.float32) * s_in, 'bv': jnp.zeros((H, D), dtype=jnp.float32), 'We': jax.random.normal(ks[6], (H, D), dtype=jnp.float32), 'Wskip': jax.random.normal(ks[7], (H, IN_DIM, D), dtype=jnp.float32) * s_in, 'bskip': jnp.zeros((H, D), dtype=jnp.float32), 'Wo': jax.random.normal(ks[8], (OUT_DIM, OUT_DIM), dtype=jnp.float32) * s_out, 'bo': jnp.zeros((OUT_DIM,), dtype=jnp.float32), 'gamma': jnp.ones((OUT_DIM,), dtype=jnp.float32), 'beta': jnp.zeros((OUT_DIM,), dtype=jnp.float32)}
    _L3_gnn_all = _L3_gnn_setup()
    _L3_gnn_in = {k: v for k, v in _L3_gnn_all.items() if k in ('Wq', 'bq', 'Wk', 'bk', 'Wv', 'bv', 'We', 'Wskip', 'bskip', 'Wo', 'bo', 'gamma', 'beta')}
    del _L3_gnn_all
    return {'x': x, 'src': src, 'dst': dst, 'edge_attr_128': edge_attr_128, 'edge_weight': edge_weight, 'L0_gnn_globals_g': _L0_gnn_in['globals_g'], 'L0_gnn_W_e_k': _L0_gnn_in['W_e_k'], 'L0_gnn_W_e_b': _L0_gnn_in['W_e_b'], 'L0_gnn_eps': _L0_gnn_in['eps'], 'L0_gnn_W1': _L0_gnn_in['W1'], 'L0_gnn_b1': _L0_gnn_in['b1'], 'L0_gnn_W2': _L0_gnn_in['W2'], 'L0_gnn_b2': _L0_gnn_in['b2'], 'L1_gnn_W_self0': _L1_gnn_in['W_self0'], 'L1_gnn_W_neigh0': _L1_gnn_in['W_neigh0'], 'L1_gnn_b0': _L1_gnn_in['b0'], 'L1_gnn_W_self1': _L1_gnn_in['W_self1'], 'L1_gnn_W_neigh1': _L1_gnn_in['W_neigh1'], 'L1_gnn_b1': _L1_gnn_in['b1'], 'L2_gnn_W': _L2_gnn_in['W'], 'L2_gnn_gamma': _L2_gnn_in['gamma'], 'L2_gnn_beta': _L2_gnn_in['beta'], 'L3_gnn_Wq': _L3_gnn_in['Wq'], 'L3_gnn_bq': _L3_gnn_in['bq'], 'L3_gnn_Wk': _L3_gnn_in['Wk'], 'L3_gnn_bk': _L3_gnn_in['bk'], 'L3_gnn_Wv': _L3_gnn_in['Wv'], 'L3_gnn_bv': _L3_gnn_in['bv'], 'L3_gnn_We': _L3_gnn_in['We'], 'L3_gnn_Wskip': _L3_gnn_in['Wskip'], 'L3_gnn_bskip': _L3_gnn_in['bskip'], 'L3_gnn_Wo': _L3_gnn_in['Wo'], 'L3_gnn_bo': _L3_gnn_in['bo'], 'L3_gnn_gamma': _L3_gnn_in['gamma'], 'L3_gnn_beta': _L3_gnn_in['beta']}

def reference(x, src, dst, edge_attr_128, edge_weight, L0_gnn_globals_g, L0_gnn_W_e_k, L0_gnn_W_e_b, L0_gnn_eps, L0_gnn_W1, L0_gnn_b1, L0_gnn_W2, L0_gnn_b2, L1_gnn_W_self0, L1_gnn_W_neigh0, L1_gnn_b0, L1_gnn_W_self1, L1_gnn_W_neigh1, L1_gnn_b1, L2_gnn_W, L2_gnn_gamma, L2_gnn_beta, L3_gnn_Wq, L3_gnn_bq, L3_gnn_Wk, L3_gnn_bk, L3_gnn_Wv, L3_gnn_bv, L3_gnn_We, L3_gnn_Wskip, L3_gnn_bskip, L3_gnn_Wo, L3_gnn_bo, L3_gnn_gamma, L3_gnn_beta):
    import jax
    import jax.numpy as jnp

    def _L0_gnn_ref(nodes, edges, globals_g, W_e_k, W_e_b, eps, W1, b1, W2, b2, senders, receivers):
        import jax, jax.numpy as jnp
        import numpy as np
        N, E, D, G, H, O = (10000, 20000, 128, 128, 512, 128)

        def mish(x):
            return x * jnp.tanh(jax.nn.softplus(x))
        n = nodes.shape[0]
        sent = nodes[senders]
        e = mish(sent + edges @ W_e_k + W_e_b)
        agg = jax.ops.segment_sum(e, receivers, num_segments=n)
        h = (1.0 + eps) * nodes + agg
        g = jnp.broadcast_to(globals_g, (n, globals_g.shape[-1]))
        h = jnp.concatenate([h, g], axis=-1)
        h = jax.nn.relu(h @ W1 + b1) @ W2 + b2
        return h

    def _L1_gnn_ref(x, src, dst, W_self0, W_neigh0, b0, W_self1, W_neigh1, b1):
        import jax, jax.numpy as jnp
        import numpy as np
        N_NODES = 50000
        N_EDGES = 25000
        D = 128

        def _sage_conv(h, src, dst, W_self, W_neigh, b, n_nodes):
            msg = h[src]
            agg = jax.ops.segment_sum(msg, dst, num_segments=n_nodes)
            deg = jax.ops.segment_sum(jnp.ones((src.shape[0],), h.dtype), dst, num_segments=n_nodes)
            h_neigh = agg / jnp.maximum(deg, 1.0)[:, None]
            return h @ W_self + h_neigh @ W_neigh + b
        n = x.shape[0]
        h = jax.nn.relu(_sage_conv(x, src, dst, W_self0, W_neigh0, b0, n))
        h = jax.nn.relu(_sage_conv(h, src, dst, W_self1, W_neigh1, b1, n))
        norm = jnp.sqrt(jnp.sum(h * h, axis=1, keepdims=True))
        return h / jnp.maximum(norm, 1e-12)

    def _L2_gnn_ref(x, W, gamma, beta, src, dst):
        import jax, jax.numpy as jnp
        import numpy as np
        N_NODES = 3125
        N_EDGES = 25000
        DIM = 128
        BN_EPS = 1e-05
        L2_EPS = 1e-12
        n = x.shape[0]
        ones = jnp.ones(src.shape[0], dtype=x.dtype)
        deg_out = jnp.clip(jax.ops.segment_sum(ones, src, num_segments=n), 1.0)
        deg_in = jnp.clip(jax.ops.segment_sum(ones, dst, num_segments=n), 1.0)
        h = x * jax.lax.rsqrt(deg_out)[:, None]
        agg = jax.ops.segment_sum(h[src], dst, num_segments=n)
        h = agg @ W
        h = h * jax.lax.rsqrt(deg_in)[:, None]
        mean = jnp.mean(h, axis=0)
        var = jnp.mean(jnp.square(h - mean), axis=0)
        h = (h - mean) * jax.lax.rsqrt(var + BN_EPS) * gamma + beta
        h = jax.nn.relu(h)
        norm = jnp.clip(jnp.linalg.norm(h, axis=1, keepdims=True), L2_EPS)
        return h / norm

    def _L3_gnn_ref(x, edge_index, edge_attr, Wq, bq, Wk, bk, Wv, bv, We, Wskip, bskip, Wo, bo, gamma, beta):
        import jax, jax.numpy as jnp
        import numpy as np
        N, E = (50000, 25000)
        IN_DIM = 128
        OUT_DIM = 128
        H = 8
        D = OUT_DIM // H
        LN_EPS = 1e-05
        n = x.shape[0]
        h, _, d = Wq.shape
        src, dst = (edge_index[0], edge_index[1])
        q = jnp.einsum('ni,hid->nhd', x, Wq) + bq
        k = jnp.einsum('ni,hid->nhd', x, Wk) + bk
        v = jnp.einsum('ni,hid->nhd', x, Wv) + bv
        e = edge_attr[:, None, None] * We[None, :, :]
        ke = k[src] + e
        alpha = jnp.einsum('ehd,ehd->eh', q[dst], ke) / jnp.sqrt(jnp.asarray(d, x.dtype))
        m = jax.ops.segment_max(alpha, dst, num_segments=n)
        m = jnp.where(jnp.isfinite(m), m, 0.0)
        ex = jnp.exp(alpha - m[dst])
        denom = jax.ops.segment_sum(ex, dst, num_segments=n)
        w = ex / jnp.maximum(denom[dst], 1e-16)
        agg = jax.ops.segment_sum(w[:, :, None] * (v[src] + e), dst, num_segments=n)
        skip = jnp.einsum('ni,hid->nhd', x, Wskip) + bskip
        heads_cat = (agg + skip).reshape(n, h * d)
        out = heads_cat @ Wo + bo
        out = out + x
        mu = out.mean(-1, keepdims=True)
        var = out.var(-1, keepdims=True)
        out = (out - mu) * jax.lax.rsqrt(var + LN_EPS) * gamma + beta
        return out
    edge_index = jnp.stack([src, dst])
    x = _layernorm(x + _L0_gnn_ref(x, edge_attr_128, L0_gnn_globals_g, L0_gnn_W_e_k, L0_gnn_W_e_b, L0_gnn_eps, L0_gnn_W1, L0_gnn_b1, L0_gnn_W2, L0_gnn_b2, src, dst), axis=-1)
    x = _layernorm(x + _L1_gnn_ref(x, src, dst, L1_gnn_W_self0, L1_gnn_W_neigh0, L1_gnn_b0, L1_gnn_W_self1, L1_gnn_W_neigh1, L1_gnn_b1), axis=-1)
    x = _layernorm(x + _L2_gnn_ref(x, L2_gnn_W, L2_gnn_gamma, L2_gnn_beta, src, dst), axis=-1)
    x = _layernorm(x + _L3_gnn_ref(x, edge_index, edge_weight, L3_gnn_Wq, L3_gnn_bq, L3_gnn_Wk, L3_gnn_bk, L3_gnn_Wv, L3_gnn_bv, L3_gnn_We, L3_gnn_Wskip, L3_gnn_bskip, L3_gnn_Wo, L3_gnn_bo, L3_gnn_gamma, L3_gnn_beta), axis=-1)
    return x

_drawn_inputs = setup_inputs


def setup_inputs(seed=0):
    import zlib

    import numpy as np

    out = dict(_drawn_inputs(seed))
    spreads = {'L0_gnn_W_e_b': (0.0, 0.1),
     'L0_gnn_b1': (0.0, 0.341),
     'L0_gnn_b2': (0.0, 0.356),
     'L1_gnn_b0': (0.0, 0.8),
     'L1_gnn_b1': (0.0, 0.8),
     'L2_gnn_gamma': (1.0, 0.6),
     'L2_gnn_beta': (0.0, 0.8),
     'L3_gnn_bq': (0.0, 2.0),
     'L3_gnn_bk': (0.0, 2.0),
     'L3_gnn_bv': (0.0, 0.1),
     'L3_gnn_bskip': (0.0, 0.1),
     'L3_gnn_bo': (0.0, 0.1),
     'L3_gnn_gamma': (1.0, 0.2),
     'L3_gnn_beta': (0.0, 0.1)}
    factors = {}
    for name, (base, spread) in spreads.items():
        noise = np.random.default_rng([zlib.crc32(name.encode()), seed]).standard_normal(out[name].shape)
        drawn = base * np.exp(spread * noise) if base else spread * noise
        out[name] = jnp.asarray(drawn.astype(out[name].dtype))
    for name, factor in factors.items():
        out[name] = (out[name] * factor).astype(out[name].dtype)
    return out
```

```python
import concourse.bass as bass
from concourse import mybir
from contextlib import ExitStack

F32 = mybir.dt.float32
I32 = mybir.dt.int32
U32 = mybir.dt.uint32
BF16 = mybir.dt.bfloat16
ALU = mybir.AluOpType
ACT = mybir.ActivationFunctionType
AX = mybir.AxisListType

P = 128
D = 128
N, E = 3125, 50000
NT = -(-N // P)
NP = NT * P
TB = 7
NB = 56
ET = TB * NB
EP = ET * P
BW = TB * P
TK = 4
TP = ET // TK
H, HD = 8, 16
QW = D + H
MW = D + 2 * H
RW = MW + H
SW = MW + H + 1
ES = 4
KS = 8
RS = 2
BANK = 512
PT = BANK // MW
TM = TB // PT * PT
NS = 5
BIG = 1.0e30
assert TM == TB - 1 and NB % KS == 0 and KS % ES == 0 and NT % NS == 0 and EP >= E and ET == TK * TP


def pipelined(eng, count, slots, sections, head=1):
    deepest = max(lag for lag, _ in sections)
    assert deepest <= slots and count % slots == 0
    for step in range(head * slots):
        for lag, do in sections:
            if step >= lag:
                do(step - lag, (step - lag) % slots, (step - lag) // slots)
    with eng.Fori(head, count // slots) as i:
        for k in range(slots):
            for lag, do in sections:
                do(i * slots + (k - lag), (k - lag) % slots, i + (k - lag) // slots)
    for step in range(count, count + deepest):
        for lag, do in sections:
            if step - lag < count:
                do(step - lag, (step - lag) % slots, (step - lag) // slots)


class Products:

    def __init__(self, sem, stage, slots, names):
        self.slots = slots
        self.of = {name: sem(f"{stage}_{name}") for name in (names + " held").split()}

    def credit(self, eng):
        for s in self.of.values():
            eng.sem_inc(s, self.slots)

    def __getitem__(self, name):
        return self.of[name]

    def ready(self, eng, name, n):
        eng.wait_ge(self.of[name], n + (1 + self.slots))

    def hold(self, eng):
        eng.sem_inc(self.of["held"], 1)

    def free(self, eng, name, n, slots=None):
        eng.wait_ge(self.of[name], n + (1 + self.slots - (slots or self.slots)))


def gnn_kernel(nc, xp, srccol, dstcol, dstflat, dsthead, lasthead, headtail, wcol, edgesT, wmat, wrow, wbc, gvec, out):
    ctx = ExitStack()
    with ctx:
        def sb(name, shape, dt=F32):
            return ctx.enter_context(nc.sbuf_tensor(name, shape, dt))

        stage_sems = []
        gathered = [nc.alloc_semaphore(f"gathered{s}") for s in range(KS)]
        before = [0] * KS

        def wait_rows(eng, s, r, copies=1):
            eng.wait_ge(gathered[s], (r + 1) * (16 * copies) + before[s])

        def count_rows(slots, items, copies=1):
            for s in range(slots):
                before[s] += items // slots * copies * 16
        picked = nc.alloc_semaphore("picked")

        def sem(name):
            stage_sems.append(nc.alloc_semaphore(name))
            return stage_sems[-1]

        def end_stage():
            with nc.Block() as block:
                @block.sync
                def _(sp):
                    for s in stage_sems:
                        sp.sem_clear(s)
            for s in stage_sems:
                nc.release_semaphore(s)
            stage_sems.clear()

        def dram(name, shape, dt=F32):
            return nc.dram_tensor(name, shape, dt, kind="Internal").ap()

        tab = [dram(f"table{i}", [NP, D]) for i in range(4)]
        sums = [dram(f"sums{i}", [EP + P, D]) for i in range(4)]
        kv_table = dram("kv_table", [NP, 2 * D])
        q_table = dram("q_table", [NP, QW])
        q_starts = dram("q_starts", [EP + NP, QW])
        sums_att = dram("sums_att", [EP + P, RW])

        x_now = sb("x_now", [P, NT, D])
        h_now = sb("h_now", [P, NT, D])
        wm = sb("wm", [P, 23, D])
        wr = sb("wr", [1, 8, D])
        bc = sb("bc", [P, 7, D])
        W_E, W_1, W_1G, W_2, W_S0, W_N0, W_S1, W_N1, W_L2, W_Q, W_O = 0, 1, 5, 9, 13, 14, 15, 16, 17, 18, 22
        R_B2, R_S0, R_S1, R_Q, R_O = 0, 1, 2, 3, 7
        B_EB, B_G2, B_B2, B_WE, B_G3, B_B3, B_B1 = range(7)
        ident = sb("ident", [P, P])
        ones = sb("ones", [P, P])
        iota = sb("iota", [P, P])
        tri = sb("tri", [P, P])
        iota_hi = sb("iota_hi", [P, NT])
        src_i = sb("src_i", [P, ET], I32)
        dst_i = sb("dst_i", [P, ET], I32)
        w_col = sb("w_col", [P, ET])
        key_rel = sb("key_rel", [TP, NT, TK])
        key_same = sb("key_same", [TP, TK, 3])
        deg_in = sb("deg_in", [P, NT])
        deg_out = sb("deg_out", [P, NT])
        end_row = sb("end_row", [P, NT], U32)
        start_row = sb("start_row", [P, NT], U32)
        r_in = sb("r_in", [P, NT])
        rs_in = sb("rs_in", [P, NT])
        rs_out = sb("rs_out", [P, NT])
        eps5 = sb("eps5", [P, 1])
        one_eps = sb("one_eps", [P, 1])
        c1 = sb("c1", [P, 4])
        rowmask = sb("rowmask", [P, NT])

        def flat_rows(table, n, width=BW):
            return table[bass.ds(n * width, width), :].rearrange("(t p) f -> p t f", p=P)

        def prepare():
            with ExitStack() as st:
                loaded, made, done, stored = sem("prep_loaded"), sem("prep_made"), sem("prep_done"), sem("prep_stored")
                sums_ready = sem("prep_sums")
                zero = st.enter_context(nc.sbuf_tensor("prep_zero", [P, RW], F32))
                xb = st.enter_context(nc.sbuf_tensor("prep_xb", [P, NT, D], F32))
                ht = st.enter_context(nc.sbuf_tensor("prep_ht", [TP, TK, 5], I32))
                same = st.enter_context(nc.sbuf_tensor("prep_same", [TP, TK], F32))
                key = st.enter_context(nc.sbuf_tensor("prep_key", [TP, TK], F32))
                base = st.enter_context(nc.sbuf_tensor("prep_base", [P, NT], F32))
                g_in = st.enter_context(nc.sbuf_tensor("prep_g", [P, 6], F32))
                ps = st.enter_context(nc.psum_tensor("prep_ps", [P, 512], F32))
                with nc.Block() as block:
                    @block.sync
                    def _(sp):
                        sp.dma_start(x_now[:, :, :], xp.rearrange("(j p) f -> p j f", p=P)).then_inc(loaded, 16)
                        sp.dma_start(wm[:, :, :], wmat).then_inc(loaded, 16)
                        sp.dma_start(wr[:, :, :], wrow).then_inc(loaded, 16)
                        sp.dma_start(bc[:, :, :], wbc.partition_broadcast(P)).then_inc(loaded, 16)
                        sp.dma_start(src_i[:, :], srccol).then_inc(loaded, 16)
                        sp.dma_start(dst_i[:, :], dstcol).then_inc(loaded, 16)
                        sp.dma_start(w_col[:, :], wcol).then_inc(loaded, 16)
                        sp.dma_start(ht[:, :, :], headtail).then_inc(loaded, 16)
                        sp.dma_start(g_in[:, :], gvec).then_inc(loaded, 16)
                        sp.wait_ge(done, 2)
                        sp.dma_start(tab[0].rearrange("(j p) f -> p j f", p=P), xb[:, :, :]).then_inc(stored, 16)
                        for t in sums:
                            sp.dma_start(t[EP:EP + P, :], zero[:, 0:D]).then_inc(stored, 16)
                        sp.dma_start(sums_att[EP:EP + P, :], zero[:, :]).then_inc(stored, 16)
                        sp.wait_ge(stored, 16 * 6)

                    @block.gpsimd
                    def _(pool):
                        pool.memset(ones[:, :], 1.0).then_inc(made, 1)
                        pool.memset(eps5[:, :], 1e-5).then_inc(made, 1)
                        pool.iota(iota[:, :], [[1, P]], base=0, channel_multiplier=0,
                                  allow_small_or_imprecise_dtypes=True).then_inc(made, 1)
                        pool.iota(iota_hi[:, :], [[1, NT]], base=0, channel_multiplier=0,
                                  allow_small_or_imprecise_dtypes=True).then_inc(made, 1)
                        pool.iota(base[:, :], [[P, NT]], base=0, channel_multiplier=0,
                                  allow_small_or_imprecise_dtypes=True).then_inc(made, 1)
                        pool.wait_ge(made, 5)
                        pool.affine_select(out=ident[:, :], in_=ones[:, :], compare_op=ALU.is_equal, fill=0.0,
                                           base=0, pattern=[[-1, P]], channel_multiplier=1).then_inc(made, 1)
                        pool.affine_select(out=tri[:, :], in_=ones[:, :], compare_op=ALU.is_ge, fill=0.0,
                                           base=0, pattern=[[1, P]], channel_multiplier=-1).then_inc(made, 1)
                        pool.affine_select(out=rowmask[:, :], in_=ones[:, 0:NT], compare_op=ALU.is_ge, fill=0.0,
                                           base=N - 1, pattern=[[-P, NT]], channel_multiplier=-1).then_inc(made, 1)

                    @block.vector
                    def _(dve):
                        dve.memset(zero[:, :], 0.0).then_inc(done, 1)
                        dve.memset(deg_in[:, :], 0.0)
                        dve.memset(deg_out[:, :], 0.0)
                        dve.wait_ge(loaded, 16 * 9)
                        dve.tensor_tensor(xb[:, :, :], x_now[:, :, :],
                                          bc[:, B_EB:B_EB + 1, :].broadcast_to([P, NT, D]), ALU.add).then_inc(done, 1)
                        dve.wait_ge(made, 8)
                        dve.tensor_tensor(same[:, :], ht[:, :, 0], ht[:, :, 1], ALU.is_equal).then_inc(made, 1)
                        dve.wait_ge(made, 9)
                        dve.scalar_tensor_tensor(key[:, :], ht[:, :, 0], 1.0, same[:, :], ALU.add, ALU.mult).then_inc(made, 1)
                        dve.wait_ge(made, 10)
                        dve.scalar_tensor_tensor(key_rel[:, :, :],
                                                 key[:, :].unsqueeze(1).broadcast_to([TP, NT, TK]), -1.0,
                                                 base[0:TP, :].unsqueeze(2).broadcast_to([TP, NT, TK]),
                                                 ALU.add, ALU.subtract).then_inc(made, 1)
                        dve.tensor_scalar(one_eps[:, :], g_in[:, 1:2], 1.0, None, ALU.add)
                        dve.wait_ge(sums_ready, 1)
                        dve.tensor_tensor(c1[:, :], ps[:, 0:4], g_in[:, 2:6], ALU.add)

                    @block.tensor
                    def _(pe):
                        pe.wait_ge(loaded, 16 * 9)
                        for c in range(4):
                            last = nc.tensor.matmul(ps[:, c:c + 1], wm[:, W_1G + c, :], g_in[:, 0:1], start=True, stop=True)
                        last.then_inc(sums_ready, 1)

        def mask_tile(dve, mask, dstrow, n):
            return dve.tensor_tensor(mask[:, :, :], dstrow[:, :, :],
                                     dst_i[:, bass.ds(n * TB, TB)].unsqueeze(2).broadcast_to([P, TB, P]), ALU.is_equal)

        def edges_layer0():
            with ExitStack() as st:
                def ring(name, shape, dt=F32, slots=ES):
                    return [st.enter_context(nc.sbuf_tensor(f"e0_{name}{s}", shape, dt)) for s in range(slots)]

                c = Products(sem, "e0", ES, "pre mask idx x clamp expd w ln sig t m p evac lo cnt acc")
                landed = [sem(f"e0_landed{s}") for s in range(ES)]
                stored = [sem(f"e0_stored{s}") for s in range(ES)]
                eT, drow = ring("eT", [P, TB, P]), ring("drow", [P, TB, P], I32)
                g, x, u, w = (ring(k, [P, TB, D]) for k in "gxuw")
                mask, row, idx = ring("mask", [P, TB, P]), ring("row", [P, TB, D]), ring("idx", [P, TB], U32)
                lo, hi = ring("lo", [P, TB, P], BF16, 1)[0], ring("hi", [P, TB, NT], BF16, 1)[0]
                bins = ring("bins", [P, 2, ET], I32, 1)[0]
                two = ring("two", [P, 1], F32, 1)[0]
                binned = sem("e0_binned")
                ps_pre = [st.enter_context(nc.psum_tensor(f"e0_pre{s}", [P, 1024], F32)) for s in range(2)]
                ps_sum = st.enter_context(nc.psum_tensor("e0_sum", [P, 1024], F32))
                ps_cnt = st.enter_context(nc.psum_tensor("e0_cnt", [P, 512], F32))

                def as_tiles(ps):
                    return ps[:, 0:BW].rearrange("p (t f) -> p t f", f=P)

                with nc.Block() as block:
                    @block.sync
                    def _(sp):
                        c.credit(sp)

                        def load(n, s, r):
                            c.free(sp, "pre", n)
                            c.hold(sp)
                            sp.dma_start(eT[s][:, :, :], edgesT[:, bass.ds(n * BW, BW)].rearrange("p (t e) -> p t e", e=P)).then_inc(landed[s], 16)
                            c.free(sp, "mask", n)
                            c.hold(sp)
                            sp.dma_start(drow[s][:, :, :].rearrange("p t e -> p (t e)"),
                                         dstflat[bass.ds(n * BW + 1, BW)].partition_broadcast(P)).then_inc(landed[s], 16)

                        pipelined(sp, NB, ES, [(0, load)])
                        for s in range(ES):
                            sp.wait_ge(stored[s], NB // ES * 16)

                    @block.gpsimd
                    def _(pool):
                        def gather(n, s, r):
                            c.ready(pool, "idx", n)
                            c.free(pool, "x", n)
                            c.hold(pool)
                            for t in range(TB):
                                pool.indirect_dma_start(g[s][:, t, :], None, tab[0][:, :],
                                                        bass.IndirectOffsetOnAxis(ap=idx[s][:, t:t + 1], axis=0)).then_inc(gathered[s], 16)

                        pipelined(pool, NB, ES, [(0, gather)])

                    @block.tensor
                    def _(pe):
                        def pre(n, s, r):
                            pe.wait_ge(landed[s], (r + 1) * 32)
                            c.free(pe, "x", n, 2)
                            for t in range(TB):
                                last = nc.tensor.matmul(as_tiles(ps_pre[s % 2])[:, t, :], eT[s][:, t, :], wm[:, W_E, :], start=True, stop=True)
                            last.then_inc(c["pre"], 1)

                        def count(n, s, r):
                            c.ready(pe, "lo", n)
                            c.free(pe, "acc", n, 1)
                            for t in range(TB):
                                last = nc.tensor.matmul(ps_cnt[:, 0:NT], lo[:, t, :], hi[:, t, :], start=(t == 0), stop=(t == TB - 1))
                            last.then_inc(c["cnt"], 1)

                        def total(n, s, r):
                            c.ready(pe, "m", n)
                            c.free(pe, "evac", n, 1)
                            for t in range(TB):
                                last = nc.tensor.matmul(as_tiles(ps_sum)[:, t, :], mask[s][:, t, :], x[s][:, t, :], start=True, stop=True)
                            last.then_inc(c["p"], 1)

                        pipelined(pe, NB, ES, [(0, pre), (3, count), (4, total)])

                    @block.scalar
                    def _(act):
                        def exp(n, s, r):
                            c.ready(act, "clamp", n)
                            nc.scalar.activation(u[s][:, :, :], u[s][:, :, :], ACT.Exp).then_inc(c["expd"], 1)

                        def sig(n, s, r):
                            c.ready(act, "w", n)
                            nc.scalar.activation(u[s][:, :, :], w[s][:, :, :], ACT.Ln, bias=two[:, :]).then_inc(c["ln"], 1)
                            c.ready(act, "ln", n)
                            nc.scalar.activation(u[s][:, :, :], u[s][:, :, :], ACT.Exp, scale=-1.0).then_inc(c["sig"], 1)

                        def evac(n, s, r):
                            c.ready(act, "p", n)
                            if not (isinstance(r, int) and r == 0):
                                c.hold(act)
                                act.wait_ge(stored[s], r * 16)
                            nc.scalar.activation(row[s][:, :, :], as_tiles(ps_sum), ACT.Copy).then_inc(c["evac"], 1)

                        def store(n, s, r):
                            c.ready(act, "evac", n)
                            act.dma_start(flat_rows(sums[0], n), row[s][:, :, :]).then_inc(stored[s], 16)

                        act.wait_ge(binned, 5)
                        act.preload_act_table_set("natural_log_exp_and_others")
                        pipelined(act, NB, ES, [(3, evac), (1, sig), (0, exp), (3, store)], head=2)

                    @block.vector
                    def _(dve):
                        dve.tensor_scalar(bins[:, 0, :], dst_i[:, :], 127, None, ALU.bitwise_and).then_inc(binned, 1)
                        dve.tensor_scalar(bins[:, 1, :], dst_i[:, :], 7, None, ALU.logical_shift_right).then_inc(binned, 1)
                        dve.memset(two[:, :], 2.0).then_inc(binned, 3)

                        def index(n, s, r):
                            nc.vector.tensor_copy(idx[s][:, :], src_i[:, bass.ds(n * TB, TB)].bitcast(U32)).then_inc(c["idx"], 1)

                        def pre(n, s, r):
                            dve.wait_ge(landed[s], (r + 1) * 32)
                            c.free(dve, "p", n)
                            mask_tile(dve, mask[s], drow[s], n).then_inc(c["mask"], 1)
                            c.ready(dve, "pre", n)
                            wait_rows(dve, s, r, TB)
                            dve.tensor_tensor(x[s][:, :, :], as_tiles(ps_pre[s % 2]), g[s][:, :, :], ALU.add).then_inc(c["x"], 1)
                            c.ready(dve, "x", n)
                            c.free(dve, "t", n)
                            dve.tensor_scalar(u[s][:, :, :], x[s][:, :, :], 20.0, None, ALU.min).then_inc(c["clamp"], 1)

                        def square(n, s, r):
                            c.ready(dve, "expd", n)
                            c.free(dve, "m", n)
                            dve.scalar_tensor_tensor(w[s][:, :, :], u[s][:, :, :], 2.0, u[s][:, :, :], ALU.add, ALU.mult).then_inc(c["w"], 1)
                            dve.wait_ge(binned, 5)
                            c.free(dve, "cnt", n, 1)
                            dve.tensor_tensor(lo[:, :, :], iota[:, :].unsqueeze(1).broadcast_to([P, TB, P]),
                                              bins[:, 0, bass.ds(n * TB, TB)].unsqueeze(2).broadcast_to([P, TB, P]), ALU.is_equal)
                            dve.tensor_tensor(hi[:, :, :], iota_hi[:, :].unsqueeze(1).broadcast_to([P, TB, NT]),
                                              bins[:, 1, bass.ds(n * TB, TB)].unsqueeze(2).broadcast_to([P, TB, NT]), ALU.is_equal).then_inc(c["lo"], 1)

                        def message(n, s, r):
                            c.ready(dve, "sig", n)
                            dve.tensor_tensor(w[s][:, :, :], w[s][:, :, :], u[s][:, :, :], ALU.mult).then_inc(c["t"], 1)
                            c.ready(dve, "t", n)
                            dve.tensor_tensor(x[s][:, :, :], w[s][:, :, :], x[s][:, :, :], ALU.mult).then_inc(c["m"], 1)

                        def tally(n, s, r):
                            c.ready(dve, "cnt", n)
                            c.free(dve, "acc", n, 1)
                            dve.tensor_tensor(deg_in[:, :], deg_in[:, :], ps_cnt[:, 0:NT], ALU.add).then_inc(c["acc"], 1)

                        pipelined(dve, NB, ES, [(0, index), (3, square), (2, pre), (4, message), (4, tally)])
            count_rows(ES, NB, TB)

        def edges_sum(stage, table, target, count_src=False, clear=None):
            with ExitStack() as st:
                def ring(name, shape, dt=F32, slots=ES):
                    return [st.enter_context(nc.sbuf_tensor(f"{stage}_{name}{s}", shape, dt)) for s in range(slots)]

                c = Products(sem, stage, ES, "mask idx p evac lo cnt acc")
                landed = [sem(f"{stage}_landed{s}") for s in range(ES)]
                stored = [sem(f"{stage}_stored{s}") for s in range(ES)]
                binned, cleared = sem(f"{stage}_binned"), sem(f"{stage}_cleared")
                drow, g = ring("drow", [P, TB, P], I32), ring("g", [P, TB, D])
                mask, row, idx = ring("mask", [P, TB, P]), ring("row", [P, TB, D]), ring("idx", [P, TB], U32)
                lo, hi = ring("lo", [P, TB, P], BF16, 1)[0], ring("hi", [P, TB, NT], BF16, 1)[0]
                bins = ring("bins", [P, 2, ET], I32, 1)[0]
                zero = ring("zero", [P, TB * QW], F32, 1)[0]
                ps_sum = [st.enter_context(nc.psum_tensor(f"{stage}_sum{s}", [P, 1024], F32)) for s in range(2)]
                ps_cnt = st.enter_context(nc.psum_tensor(f"{stage}_cnt", [P, 512], F32))

                def as_tiles(ps):
                    return ps[:, 0:BW].rearrange("p (t f) -> p t f", f=P)

                with nc.Block() as block:
                    @block.sync
                    def _(sp):
                        c.credit(sp)
                        if clear is not None:
                            sp.wait_ge(binned, 1)

                        def load(n, s, r):
                            c.free(sp, "mask", n)
                            c.hold(sp)
                            sp.dma_start(drow[s][:, :, :].rearrange("p t e -> p (t e)"),
                                         dstflat[bass.ds(n * BW + 1, BW)].partition_broadcast(P)).then_inc(landed[s], 16)

                        def wipe(n, s, r):
                            sp.dma_start(clear[bass.ds(n * BW, BW), :].rearrange("(p t) f -> p (t f)", p=P), zero[:, :]).then_inc(cleared, 16)

                        pipelined(sp, NB, ES, [(0, load)] + ([(0, wipe)] if clear is not None else []))
                        for s in range(ES):
                            sp.wait_ge(stored[s], NB // ES * 16)
                        if clear is not None:
                            sp.wait_ge(cleared, NB * 16)

                    @block.gpsimd
                    def _(pool):
                        def gather(n, s, r):
                            c.ready(pool, "idx", n)
                            c.free(pool, "p", n)
                            c.hold(pool)
                            for t in range(TB):
                                pool.indirect_dma_start(g[s][:, t, :], None, table[:, :],
                                                        bass.IndirectOffsetOnAxis(ap=idx[s][:, t:t + 1], axis=0)).then_inc(gathered[s], 16)

                        pipelined(pool, NB, ES, [(0, gather)])

                    @block.tensor
                    def _(pe):
                        def total(n, s, r):
                            c.ready(pe, "mask", n)
                            c.free(pe, "evac", n, 2)
                            wait_rows(pe, s, r, TB)
                            for t in range(TB):
                                last = nc.tensor.matmul(as_tiles(ps_sum[s % 2])[:, t, :], mask[s][:, t, :], g[s][:, t, :], start=True, stop=True)
                            last.then_inc(c["p"], 1)

                        def count(n, s, r):
                            c.ready(pe, "lo", n)
                            c.free(pe, "acc", n, 1)
                            for t in range(TB):
                                last = nc.tensor.matmul(ps_cnt[:, 0:NT], lo[:, t, :], hi[:, t, :], start=(t == 0), stop=(t == TB - 1))
                            last.then_inc(c["cnt"], 1)

                        pipelined(pe, NB, ES, [(0, count)] * count_src + [(0, total)])

                    @block.scalar
                    def _(act):
                        def evac(n, s, r):
                            c.ready(act, "p", n)
                            if not (isinstance(r, int) and r == 0):
                                c.hold(act)
                                act.wait_ge(stored[s], r * 16)
                            nc.scalar.activation(row[s][:, :, :], as_tiles(ps_sum[s % 2]), ACT.Copy).then_inc(c["evac"], 1)
                            c.ready(act, "evac", n)
                            act.dma_start(flat_rows(target, n), row[s][:, :, :]).then_inc(stored[s], 16)

                        pipelined(act, NB, ES, [(0, evac)], head=2)

                    @block.vector
                    def _(dve):
                        if clear is not None:
                            dve.memset(zero[:, :], 0.0).then_inc(binned, 1)
                        if count_src:
                            dve.tensor_scalar(bins[:, 0, :], src_i[:, :], 127, None, ALU.bitwise_and).then_inc(binned, 1)
                            dve.tensor_scalar(bins[:, 1, :], src_i[:, :], 7, None, ALU.logical_shift_right).then_inc(binned, 1)
                            dve.wait_ge(binned, 2 + (clear is not None))

                        def index(n, s, r):
                            if isinstance(r, int) and r == 0:
                                pass
                            else:
                                wait_rows(dve, s, r - 1, TB)
                            nc.vector.tensor_copy(idx[s][:, :], src_i[:, bass.ds(n * TB, TB)].bitcast(U32)).then_inc(c["idx"], 1)

                        def masks(n, s, r):
                            dve.wait_ge(landed[s], (r + 1) * 16)
                            c.free(dve, "p", n)
                            mask_tile(dve, mask[s], drow[s], n).then_inc(c["mask"], 1)

                        def bin_src(n, s, r):
                            c.free(dve, "cnt", n, 1)
                            dve.tensor_tensor(lo[:, :, :], iota[:, :].unsqueeze(1).broadcast_to([P, TB, P]),
                                              bins[:, 0, bass.ds(n * TB, TB)].unsqueeze(2).broadcast_to([P, TB, P]), ALU.is_equal)
                            dve.tensor_tensor(hi[:, :, :], iota_hi[:, :].unsqueeze(1).broadcast_to([P, TB, NT]),
                                              bins[:, 1, bass.ds(n * TB, TB)].unsqueeze(2).broadcast_to([P, TB, NT]), ALU.is_equal).then_inc(c["lo"], 1)

                        def tally(n, s, r):
                            c.ready(dve, "cnt", n)
                            c.free(dve, "acc", n, 1)
                            dve.tensor_tensor(deg_out[:, :], deg_out[:, :], ps_cnt[:, 0:NT], ALU.add).then_inc(c["acc"], 1)

                        pipelined(dve, NB, ES, [(0, index), (1, masks)] + [(2, tally), (1, bin_src)] * count_src)
            count_rows(ES, NB, TB)

        def degrees(stage, deg, with_rows):
            with ExitStack() as st:
                def tmp(name, dt=F32):
                    return st.enter_context(nc.sbuf_tensor(f"{stage}_{name}", [P, NT], dt))

                step, summed, clipped, rooted = sem(f"{stage}_step"), sem(f"{stage}_summed"), sem(f"{stage}_clipped"), sem(f"{stage}_rooted")
                numbered = sem(f"{stage}_numbered")
                tot, incl, has, cum, row, nid, clip, rec = (tmp(k) for k in "tot incl has cum row nid clip rec".split())
                ps = st.enter_context(nc.psum_tensor(f"{stage}_ps", [P, 512], F32))
                with nc.Block() as block:
                    @block.tensor
                    def _(pe):
                        if with_rows:
                            nc.tensor.matmul(ps[:, 0:NT], tri[:, :], deg[:, :], start=True, stop=True)
                            nc.tensor.matmul(ps[:, 64:64 + NT], ones[:, :], deg[:, :], start=True, stop=True).then_inc(summed, 1)

                    @block.gpsimd
                    def _(pool):
                        pool.iota(nid[:, :], [[P, NT]], base=EP, channel_multiplier=1,
                                  allow_small_or_imprecise_dtypes=True).then_inc(numbered, 1)

                    @block.scalar
                    def _(act):
                        act.wait_ge(clipped, 1)
                        nc.scalar.activation((rs_in if with_rows else rs_out)[:, :], (r_in if with_rows else rec)[:, :], ACT.Sqrt).then_inc(rooted, 1)

                    @block.vector
                    def _(dve):
                        n = [0]

                        def after(ins):
                            n[0] += 1
                            ins.then_inc(step, 1)
                            dve.wait_ge(step, n[0])

                        after(dve.tensor_scalar(clip[:, :], deg[:, :], 1.0, None, ALU.max))
                        dve.reciprocal((r_in if with_rows else rec)[:, :], clip[:, :]).then_inc(clipped, 1)
                        if with_rows:
                            dve.wait_ge(summed, 1)
                            after(dve.tensor_copy(tot[:, :], ps[:, 64:64 + NT]))
                            after(dve.tensor_tensor_scan(incl[:, :], ones[:, 0:NT], tot[:, :], 0.0, ALU.mult, ALU.add))
                            after(dve.tensor_tensor(incl[:, :], incl[:, :], tot[:, :], ALU.subtract))
                            after(dve.tensor_tensor(cum[:, :], incl[:, :], ps[:, 0:NT], ALU.add))
                            after(dve.tensor_scalar(has[:, :], deg[:, :], 0.0, None, ALU.is_gt))
                            after(dve.scalar_tensor_tensor(row[:, :], cum[:, :], -1.0 - EP, has[:, :], ALU.add, ALU.mult))
                            dve.tensor_scalar(end_row[:, :], row[:, :], float(EP), None, ALU.add)
                            dve.wait_ge(numbered, 1)
                            after(dve.tensor_tensor(cum[:, :], cum[:, :], deg[:, :], ALU.subtract))
                            after(dve.tensor_tensor(cum[:, :], cum[:, :], nid[:, :], ALU.subtract))
                            after(dve.tensor_tensor(cum[:, :], cum[:, :], has[:, :], ALU.mult))
                            dve.tensor_tensor(start_row[:, :], cum[:, :], nid[:, :], ALU.add)

        def tails(table, width):
            return table[0:EP, :].rearrange("(k p e) f -> p k e f", e=P, p=TP)[:, :, P - 1, 0:width]

        def pick(dve, z, n):
            return dve.tensor_tensor(z[:, :, :], iota[0:TP, :].unsqueeze(1).broadcast_to([TP, TK, P]),
                                     key_rel[:, bass.ds(n, 1), :].rearrange("p j k -> p (j k)").unsqueeze(2).broadcast_to([TP, TK, P]),
                                     ALU.is_equal)

        def col(buf, n):
            return buf[:, bass.ds(n, 1)]

        def tile_of(buf, n):
            return buf[:, bass.ds(n, 1), :].rearrange("p j f -> p (j f)")

        def nodes_layer0():
            with ExitStack() as st:
                def ring(name, shape, dt=F32, slots=NS):
                    return [st.enter_context(nc.sbuf_tensor(f"n0_{name}{s}", shape, dt)) for s in range(slots)]

                c = Products(sem, "n0", NS, "idx z h agg ht mm1 hid mm2 res stat var std rstd norm")
                tails_in, stored = sem("n0_tails"), sem("n0_stored")
                tail = ring("tail", [TP, TK, D], slots=1)[0]
                idx, g, z = ring("idx", [P, 1], U32), ring("g", [P, D]), ring("z", [TP, TK, P])
                hT, hid, res = ring("hT", [P, P]), ring("hid", [P, 4, P]), ring("res", [P, D])
                stat, mv, std = ring("stat", [P, 6]), ring("mv", [P, 2]), ring("std", [P, 2])
                ps = [st.enter_context(nc.psum_tensor(f"n0_ps{s}", [P, 512], F32)) for s in range(3)]
                with nc.Block() as block:
                    @block.sync
                    def _(sp):
                        c.credit(sp)
                        sp.dma_start(tail[:, :, :], tails(sums[0], D)).then_inc(tails_in, 16)

                        def store(n, s, r):
                            c.ready(sp, "norm", n)
                            c.hold(sp)
                            sp.dma_start(tab[1][bass.ds(n * P, P), :], tile_of(x_now, n)).then_inc(stored, 16)

                        pipelined(sp, NT, NS, [(0, store)])
                        sp.wait_ge(stored, 16 * NT)

                    @block.gpsimd
                    def _(pool):
                        def gather(n, s, r):
                            c.ready(pool, "idx", n)
                            c.free(pool, "agg", n)
                            c.hold(pool)
                            pool.indirect_dma_start(g[s][:, :], None, sums[0][:, :],
                                                    bass.IndirectOffsetOnAxis(ap=idx[s][:, :], axis=0)).then_inc(gathered[s], 16)

                        pipelined(pool, NT, NS, [(0, gather)])

                    @block.tensor
                    def _(pe):
                        pe.wait_ge(tails_in, 16)

                        def agg(n, s, r):
                            c.ready(pe, "z", n)
                            c.ready(pe, "h", n)
                            c.free(pe, "ht", n, 1)
                            nc.tensor.matmul(ps[0][:, 0:P], g[s][:, :], ident[:, :], start=True, stop=False)
                            for k in range(TK):
                                last = nc.tensor.matmul(ps[0][:, 0:P], tail[:, k, :], z[s][:, k, :], start=False, stop=(k == TK - 1))
                            last.then_inc(c["agg"], 1)

                        def up(n, s, r):
                            c.ready(pe, "ht", n)
                            c.free(pe, "hid", n, 1)
                            for k in range(4):
                                last = nc.tensor.matmul(ps[1][:, k * P:(k + 1) * P], wm[:, W_1 + k, :], hT[s][:, :], start=True, stop=True)
                            last.then_inc(c["mm1"], 1)

                        def down(n, s, r):
                            c.ready(pe, "hid", n)
                            c.free(pe, "res", n, 1)
                            nc.tensor.matmul(ps[2][:, 0:D], ones[0:1, :], wr[:, R_B2, :], start=True, stop=False)
                            for k in range(4):
                                last = nc.tensor.matmul(ps[2][:, 0:D], hid[s][:, k, :], wm[:, W_2 + k, :], start=False, stop=(k == 3))
                            last.then_inc(c["mm2"], 1)

                        pipelined(pe, NT, NS, [(0, agg), (1, up), (2, down)])

                    @block.scalar
                    def _(act):
                        def move(n, s, r):
                            c.ready(act, "agg", n)
                            c.free(act, "mm1", n)
                            nc.scalar.activation(hT[s][:, :], ps[0][:, 0:P], ACT.Copy).then_inc(c["ht"], 1)

                        def root(n, s, r):
                            c.ready(act, "var", n)
                            c.free(act, "rstd", n)
                            nc.scalar.activation(std[s][:, 0:1], mv[s][:, 1:2], ACT.Sqrt, bias=eps5[:, :]).then_inc(c["std"], 1)

                        pipelined(act, NT, NS, [(0, move), (3, root)])

                    @block.vector
                    def _(dve):
                        def index(n, s, r):
                            c.free(dve, "h", n)
                            nc.vector.tensor_copy(idx[s][:, :], col(end_row, n)).then_inc(c["idx"], 1)
                            c.free(dve, "agg", n)
                            pick(dve, z[s], n).then_inc(c["z"], 1)

                        def own(n, s, r):
                            wait_rows(dve, s, r)
                            dve.scalar_tensor_tensor(g[s][:, :], tile_of(x_now, n), one_eps[:, :], g[s][:, :], ALU.mult, ALU.add).then_inc(c["h"], 1)

                        def relu(n, s, r):
                            c.ready(dve, "mm1", n)
                            c.free(dve, "mm2", n)
                            for k in range(4):
                                last = dve.tensor_scalar(hid[s][:, k, :], ps[1][:, k * P:(k + 1) * P], c1[:, k:k + 1], 0.0, ALU.add, ALU.max)
                            last.then_inc(c["hid"], 1)

                        def residual(n, s, r):
                            c.ready(dve, "mm2", n)
                            c.free(dve, "norm", n)
                            dve.tensor_tensor(res[s][:, :], ps[2][:, 0:D], tile_of(x_now, n), ALU.add).then_inc(c["res"], 1)
                            c.ready(dve, "res", n)
                            dve.bn_stats(stat[s][:, :], res[s][:, :]).then_inc(c["stat"], 1)
                            c.ready(dve, "stat", n)
                            c.hold(dve)
                            dve.bn_aggr(mv[s][:, :], stat[s][:, :]).then_inc(c["var"], 1)

                        def norm(n, s, r):
                            c.ready(dve, "std", n)
                            dve.reciprocal(std[s][:, 1:2], std[s][:, 0:1]).then_inc(c["rstd"], 1)
                            c.ready(dve, "rstd", n)
                            dve.tensor_scalar(tile_of(x_now, n), res[s][:, :], mv[s][:, 0:1], std[s][:, 1:2], ALU.subtract, ALU.mult).then_inc(c["norm"], 1)

                        pipelined(dve, NT, NS, [(0, index), (1, own), (5, norm), (3, relu), (4, residual)])
            count_rows(NS, NT)

        def nodes_sage(stage, table, target, x_in, w_self, w_neigh, bias, final):
            with ExitStack() as st:
                def ring(name, shape, dt=F32, slots=NS):
                    return [st.enter_context(nc.sbuf_tensor(f"{stage}_{name}{s}", shape, dt)) for s in range(slots)]

                c = Products(sem, stage, NS, "idx z xs dg zt a tr at mm h sq root inv res stat var std rstd norm scaled scl_free")
                tails_in, stored = sem(f"{stage}_tails"), [sem(f"{stage}_stored{s}") for s in range(NS)]
                tail = ring("tail", [TP, TK, D], slots=1)[0]
                idx, g, z = ring("idx", [P, 1], U32), ring("g", [P, D]), ring("z", [TP, TK, P])
                xs, dg, aT = ring("xs", [P, D]), ring("dg", [P, P]), ring("aT", [P, 2, P])
                h, res, sq = ring("h", [P, D]), ring("res", [P, D]), ring("sq", [P, D])
                stat, mv, std, nrm = ring("stat", [P, 6]), ring("mv", [P, 2]), ring("std", [P, 2]), ring("nrm", [P, 3])
                scl = ring("scl", [P, D])
                ps = [st.enter_context(nc.psum_tensor(f"{stage}_ps{s}", [P, 512], F32)) for s in range(3)]
                with nc.Block() as block:
                    @block.sync
                    def _(sp):
                        c.credit(sp)
                        sp.dma_start(tail[:, :, :], tails(table, D)).then_inc(tails_in, 16)

                        def store(n, s, r):
                            c.ready(sp, "scaled" if final else "h", n)
                            c.hold(sp)
                            sp.dma_start(target[bass.ds(n * P, P), :], scl[s][:, :] if final else tile_of(h_now, n)).then_inc(stored[s], 16)

                        def retire(n, s, r):
                            sp.wait_ge(stored[s], (r + 1) * 16)
                            sp.sem_inc(c["scl_free"], 1)

                        pipelined(sp, NT, NS, [(0, store), (1, retire)])

                    @block.gpsimd
                    def _(pool):
                        def gather(n, s, r):
                            c.ready(pool, "idx", n)
                            c.free(pool, "tr", n)
                            c.hold(pool)
                            pool.indirect_dma_start(g[s][:, :], None, table[:, :],
                                                    bass.IndirectOffsetOnAxis(ap=idx[s][:, :], axis=0)).then_inc(gathered[s], 16)

                        pipelined(pool, NT, NS, [(0, gather)])

                    @block.tensor
                    def _(pe):
                        pe.wait_ge(tails_in, 16)

                        def earlier(n, s, r):
                            c.ready(pe, "z", n)
                            c.free(pe, "a", n, 1)
                            for k in range(TK):
                                last = nc.tensor.matmul(ps[0][:, 0:D], z[s][:, k, :], tail[:, k, :], start=(k == 0), stop=(k == TK - 1))
                            last.then_inc(c["zt"], 1)

                        def turn(n, s, r):
                            c.ready(pe, "a", n)
                            c.ready(pe, "dg", n)
                            c.ready(pe, "xs", n)
                            c.free(pe, "at", n, 1)
                            nc.tensor.matmul(ps[1][:, 0:P], g[s][:, :], dg[s][:, :], start=True, stop=True)
                            nc.tensor.matmul(ps[1][:, P:2 * P], xs[s][:, :], ident[:, :], start=True, stop=True).then_inc(c["tr"], 1)

                        def product(n, s, r):
                            c.ready(pe, "at", n)
                            c.free(pe, "h", n, 1)
                            nc.tensor.matmul(ps[2][:, 0:D], ones[0:1, :], wr[:, bias, :], start=True, stop=False)
                            nc.tensor.matmul(ps[2][:, 0:D], aT[s][:, 0, :], wm[:, w_neigh, :], start=False, stop=False)
                            nc.tensor.matmul(ps[2][:, 0:D], aT[s][:, 1, :], wm[:, w_self, :], start=False, stop=True).then_inc(c["mm"], 1)

                        pipelined(pe, NT, NS, [(0, earlier), (1, turn), (2, product)])

                    @block.scalar
                    def _(act):
                        def own(n, s, r):
                            c.free(act, "tr", n)
                            nc.scalar.activation(xs[s][:, :], tile_of(x_in, n), ACT.Copy).then_inc(c["xs"], 1)

                        def move(n, s, r):
                            c.ready(act, "tr", n)
                            c.free(act, "mm", n)
                            nc.scalar.activation(aT[s][:, :, :], ps[1][:, 0:2 * P].rearrange("p (a m) -> p a m", a=2), ACT.Copy).then_inc(c["at"], 1)

                        def relu(n, s, r):
                            c.ready(act, "mm", n)
                            if final:
                                c.free(act, "res", n)
                            nc.scalar.activation(h[s][:, :] if final else tile_of(h_now, n), ps[2][:, 0:D], ACT.Relu).then_inc(c["h"], 1)

                        def square(n, s, r):
                            c.ready(act, "h", n)
                            c.free(act, "root", n)
                            nc.scalar.activation(sq[s][:, :], h[s][:, :], ACT.Square, accum_out=nrm[s][:, 0:1]).then_inc(c["sq"], 1)

                        def length(n, s, r):
                            c.ready(act, "sq", n)
                            c.free(act, "inv", n)
                            nc.scalar.activation(nrm[s][:, 1:2], nrm[s][:, 0:1], ACT.Sqrt).then_inc(c["root"], 1)

                        def root(n, s, r):
                            c.ready(act, "var", n)
                            c.free(act, "rstd", n)
                            nc.scalar.activation(std[s][:, 0:1], mv[s][:, 1:2], ACT.Sqrt, bias=eps5[:, :]).then_inc(c["std"], 1)

                        tail_end = [(2, square), (3, length), (4, root)] if final else []
                        pipelined(act, NT, NS, [(0, own), (0, move), (1, relu)] + tail_end)

                    @block.vector
                    def _(dve):
                        def index(n, s, r):
                            c.free(dve, "a", n)
                            nc.vector.tensor_copy(idx[s][:, :], col(end_row, n)).then_inc(c["idx"], 1)
                            c.free(dve, "zt", n)
                            pick(dve, z[s], n).then_inc(c["z"], 1)
                            c.free(dve, "tr", n)
                            dve.tensor_scalar(dg[s][:, :], ident[:, :], col(r_in, n), None, ALU.mult).then_inc(c["dg"], 1)

                        def whole(n, s, r):
                            c.ready(dve, "zt", n)
                            wait_rows(dve, s, r)
                            dve.tensor_tensor(g[s][:, :], ps[0][:, 0:D], g[s][:, :], ALU.add).then_inc(c["a"], 1)

                        def residual(n, s, r):
                            c.ready(dve, "root", n)
                            dve.tensor_scalar(nrm[s][:, 2:3], nrm[s][:, 1:2], 1e-12, None, ALU.max).then_inc(c["stat"], 1)
                            dve.wait_ge(c["stat"], n * 2 + (1 + NS))
                            dve.reciprocal(nrm[s][:, 1:2], nrm[s][:, 2:3]).then_inc(c["inv"], 1)
                            c.ready(dve, "inv", n)
                            c.free(dve, "norm", n)
                            dve.scalar_tensor_tensor(res[s][:, :], h[s][:, :], nrm[s][:, 1:2], tile_of(x_now, n), ALU.mult, ALU.add).then_inc(c["res"], 1)
                            c.ready(dve, "res", n)
                            dve.bn_stats(stat[s][:, :], res[s][:, :]).then_inc(c["stat"], 1)
                            dve.wait_ge(c["stat"], n * 2 + (2 + NS))
                            c.hold(dve)
                            dve.bn_aggr(mv[s][:, :], stat[s][:, :]).then_inc(c["var"], 1)

                        def norm(n, s, r):
                            c.ready(dve, "std", n)
                            dve.reciprocal(std[s][:, 1:2], std[s][:, 0:1]).then_inc(c["rstd"], 1)
                            c.ready(dve, "rstd", n)
                            dve.tensor_scalar(tile_of(x_now, n), res[s][:, :], mv[s][:, 0:1], std[s][:, 1:2], ALU.subtract, ALU.mult).then_inc(c["norm"], 1)
                            c.ready(dve, "norm", n)
                            c.free(dve, "scl_free", n)
                            dve.tensor_scalar(scl[s][:, :], tile_of(x_now, n), col(rs_out, n), None, ALU.mult).then_inc(c["scaled"], 1)

                        pipelined(dve, NT, NS, [(0, index), (1, whole)] + ([(5, norm), (4, residual)] if final else []))
            count_rows(NS, NT)

        def nodes_gcn():
            with ExitStack() as st:
                def ring(name, shape, dt=F32, slots=NS):
                    return [st.enter_context(nc.sbuf_tensor(f"n2_{name}{s}", shape, dt)) for s in range(slots)]

                c = Products(sem, "n2", NS, "idx z zt a tr at mm h")
                tails_in = sem("n2_tails")
                tail = ring("tail", [TP, TK, D], slots=1)[0]
                idx, g, z, aT = ring("idx", [P, 1], U32), ring("g", [P, D]), ring("z", [TP, TK, P]), ring("aT", [P, P])
                ps = [st.enter_context(nc.psum_tensor(f"n2_ps{s}", [P, 512], F32)) for s in range(3)]
                with nc.Block() as block:
                    @block.sync
                    def _(sp):
                        c.credit(sp)
                        sp.dma_start(tail[:, :, :], tails(sums[3], D)).then_inc(tails_in, 16)

                    @block.gpsimd
                    def _(pool):
                        def gather(n, s, r):
                            c.ready(pool, "idx", n)
                            c.free(pool, "tr", n)
                            c.hold(pool)
                            pool.indirect_dma_start(g[s][:, :], None, sums[3][:, :],
                                                    bass.IndirectOffsetOnAxis(ap=idx[s][:, :], axis=0)).then_inc(gathered[s], 16)

                        pipelined(pool, NT, NS, [(0, gather)])

                    @block.tensor
                    def _(pe):
                        pe.wait_ge(tails_in, 16)

                        def earlier(n, s, r):
                            c.ready(pe, "z", n)
                            c.free(pe, "a", n, 1)
                            for k in range(TK):
                                last = nc.tensor.matmul(ps[0][:, 0:D], z[s][:, k, :], tail[:, k, :], start=(k == 0), stop=(k == TK - 1))
                            last.then_inc(c["zt"], 1)

                        def turn(n, s, r):
                            c.ready(pe, "a", n)
                            c.free(pe, "at", n, 1)
                            nc.tensor.matmul(ps[1][:, 0:P], g[s][:, :], ident[:, :], start=True, stop=True).then_inc(c["tr"], 1)

                        def product(n, s, r):
                            c.ready(pe, "at", n)
                            c.free(pe, "h", n, 1)
                            nc.tensor.matmul(ps[2][:, 0:D], aT[s][:, :], wm[:, W_L2, :], start=True, stop=True).then_inc(c["mm"], 1)

                        pipelined(pe, NT, NS, [(0, earlier), (1, turn), (2, product)])

                    @block.scalar
                    def _(act):
                        def move(n, s, r):
                            c.ready(act, "tr", n)
                            c.free(act, "mm", n)
                            nc.scalar.activation(aT[s][:, :], ps[1][:, 0:P], ACT.Copy).then_inc(c["at"], 1)

                        pipelined(act, NT, NS, [(0, move)])

                    @block.vector
                    def _(dve):
                        def index(n, s, r):
                            c.free(dve, "a", n)
                            nc.vector.tensor_copy(idx[s][:, :], col(end_row, n)).then_inc(c["idx"], 1)
                            c.free(dve, "zt", n)
                            pick(dve, z[s], n).then_inc(c["z"], 1)

                        def whole(n, s, r):
                            c.ready(dve, "zt", n)
                            wait_rows(dve, s, r)
                            dve.tensor_tensor(g[s][:, :], ps[0][:, 0:D], g[s][:, :], ALU.add).then_inc(c["a"], 1)

                        def scale(n, s, r):
                            c.ready(dve, "mm", n)
                            dve.tensor_scalar(tile_of(h_now, n), ps[2][:, 0:D], col(rs_in, n), None, ALU.mult).then_inc(c["h"], 1)

                        pipelined(dve, NT, NS, [(0, index), (1, whole), (3, scale)])
            count_rows(NS, NT)

        def rows(a):
            return a[:, :].unsqueeze(2).broadcast_to([P, NT, D])

        def cols(a):
            return a.broadcast_to([P, NT, D])

        class Steps:

            def __init__(self, stage):
                self.sem = {e: sem(f"{stage}_{e}_done") for e in ("dve", "act", "pe", "pool", "dma")}
                self.count = {e: 0 for e in self.sem}

            def did(self, engine, ins, by=1):
                self.count[engine] += by
                ins.then_inc(self.sem[engine], by)
                return self.count[engine]

        def norm_rows(dve, k, a, sq, small, first, squares):
            dve.tensor_reduce(small[:, 0, :], a[:, :, :], AX.X, ALU.add).then_inc(k.sem["dve"], 1)
            dve.wait_ge(k.sem["dve"], first + 1)
            dve.tensor_scalar(small[:, 0, :], small[:, 0, :], 1.0 / D, None, ALU.mult).then_inc(k.sem["dve"], 1)
            dve.wait_ge(k.sem["dve"], first + 2)
            dve.tensor_tensor(a[:, :, :], a[:, :, :], rows(small[:, 0, :]), ALU.subtract).then_inc(k.sem["dve"], 1)
            dve.wait_ge(k.sem["act"], squares)
            dve.tensor_reduce(small[:, 1, :], sq[:, :, :], AX.X, ALU.add).then_inc(k.sem["dve"], 1)
            dve.wait_ge(k.sem["act"], squares + 1)
            dve.reciprocal(small[:, 0, :], small[:, 2, :]).then_inc(k.sem["dve"], 1)
            dve.wait_ge(k.sem["dve"], first + 5)
            dve.tensor_tensor(a[:, :, :], a[:, :, :], rows(small[:, 0, :]), ALU.mult).then_inc(k.sem["dve"], 1)
            dve.wait_ge(k.sem["dve"], first + 6)

        def norm_squares(act, k, a, sq, small, first):
            act.wait_ge(k.sem["dve"], first + 3)
            nc.scalar.activation(sq[:, :, :], a[:, :, :], ACT.Square).then_inc(k.sem["act"], 1)
            act.wait_ge(k.sem["dve"], first + 4)
            nc.scalar.activation(small[:, 2, :], small[:, 1, :], ACT.Sqrt, bias=eps5[:, :], scale=1.0 / D).then_inc(k.sem["act"], 1)

        def batch_norm():
            with ExitStack() as st:
                k = Steps("bn")
                sq = st.enter_context(nc.sbuf_tensor("bn_sq", [P, NT, D], F32))
                small = st.enter_context(nc.sbuf_tensor("bn_small", [P, 3, NT], F32))
                f = st.enter_context(nc.sbuf_tensor("bn_f", [P, 5, D], F32))
                ps = st.enter_context(nc.psum_tensor("bn_ps", [P, 512], F32))
                dv, ac, pe_s = k.sem["dve"], k.sem["act"], k.sem["pe"]
                with nc.Block() as block:
                    @block.tensor
                    def _(pe):
                        pe.wait_ge(dv, 1)
                        nc.tensor.matmul(ps[:, 0:D], ones[:, :], f[:, 0, :], start=True, stop=True).then_inc(pe_s, 1)
                        pe.wait_ge(dv, 5)
                        nc.tensor.matmul(ps[:, 0:D], ones[:, :], f[:, 0, :], start=True, stop=True).then_inc(pe_s, 1)

                    @block.scalar
                    def _(act):
                        act.wait_ge(dv, 3)
                        nc.scalar.activation(sq[:, :, :], h_now[:, :, :], ACT.Square).then_inc(ac, 1)
                        act.wait_ge(pe_s, 2)
                        nc.scalar.activation(f[:, 2, :], ps[:, 0:D], ACT.Sqrt, bias=eps5[:, :], scale=1.0 / N).then_inc(ac, 1)
                        act.wait_ge(dv, 9)
                        nc.scalar.activation(h_now[:, :, :], h_now[:, :, :], ACT.Relu).then_inc(ac, 1)
                        act.wait_ge(ac, 3)
                        nc.scalar.activation(sq[:, :, :], h_now[:, :, :], ACT.Square).then_inc(ac, 1)
                        act.wait_ge(dv, 10)
                        nc.scalar.activation(small[:, 1, :], small[:, 0, :], ACT.Sqrt).then_inc(ac, 1)
                        norm_squares(act, k, x_now, sq, small, 14)

                    @block.vector
                    def _(dve):
                        dve.tensor_reduce(f[:, 0, :], h_now[:, :, :].rearrange("p j f -> p f j"), AX.X, ALU.add).then_inc(dv, 1)
                        dve.wait_ge(pe_s, 1)
                        dve.tensor_scalar(f[:, 1, :], ps[:, 0:D], 1.0 / N, None, ALU.mult).then_inc(dv, 1)
                        dve.wait_ge(dv, 2)
                        dve.tensor_tensor(h_now[:, :, :], h_now[:, :, :], cols(f[:, 1:2, :]), ALU.subtract).then_inc(dv, 1)
                        dve.wait_ge(ac, 1)
                        dve.tensor_scalar(sq[:, NT - 1, :], sq[:, NT - 1, :], rowmask[:, NT - 1:NT], None, ALU.mult).then_inc(dv, 1)
                        dve.wait_ge(dv, 4)
                        dve.tensor_reduce(f[:, 0, :], sq[:, :, :].rearrange("p j f -> p f j"), AX.X, ALU.add).then_inc(dv, 1)
                        dve.wait_ge(ac, 2)
                        dve.reciprocal(f[:, 3, :], f[:, 2, :]).then_inc(dv, 1)
                        dve.wait_ge(dv, 6)
                        dve.tensor_tensor(f[:, 4, :], f[:, 3, :], bc[:, B_G2, :], ALU.mult).then_inc(dv, 1)
                        dve.wait_ge(dv, 7)
                        dve.tensor_tensor(h_now[:, :, :], h_now[:, :, :], cols(f[:, 4:5, :]), ALU.mult).then_inc(dv, 1)
                        dve.wait_ge(dv, 8)
                        dve.tensor_tensor(h_now[:, :, :], h_now[:, :, :], cols(bc[:, B_B2:B_B2 + 1, :]), ALU.add).then_inc(dv, 1)
                        dve.wait_ge(ac, 4)
                        dve.tensor_reduce(small[:, 0, :], sq[:, :, :], AX.X, ALU.add).then_inc(dv, 1)
                        dve.wait_ge(ac, 5)
                        dve.tensor_scalar(small[:, 2, :], small[:, 1, :], 1e-12, None, ALU.max).then_inc(dv, 1)
                        dve.wait_ge(dv, 11)
                        dve.reciprocal(small[:, 0, :], small[:, 2, :]).then_inc(dv, 1)
                        dve.wait_ge(dv, 12)
                        dve.tensor_tensor(h_now[:, :, :], h_now[:, :, :], rows(small[:, 0, :]), ALU.mult).then_inc(dv, 1)
                        dve.wait_ge(dv, 13)
                        dve.tensor_tensor(x_now[:, :, :], h_now[:, :, :], x_now[:, :, :], ALU.add).then_inc(dv, 1)
                        dve.wait_ge(dv, 14)
                        norm_rows(dve, k, x_now, sq, small, 14, 6)

        def project():
            with ExitStack() as st:
                def ring(name, shape, dt=F32, slots=NS):
                    return [st.enter_context(nc.sbuf_tensor(f"n3_{name}{s}", shape, dt)) for s in range(slots)]

                c = Products(sem, "n3", NS, "idx xs tr at mm q kv skip qe qw rows_free")
                stored = [sem(f"n3_stored{s}") for s in range(NS)]
                first_in, first_u, first_out = sem("n3_first_in"), sem("n3_first_u"), sem("n3_first_out")
                idx, xs, xT = ring("idx", [P, 1], U32), ring("xs", [P, D]), ring("xT", [P, P])
                q, kv, prod = ring("q", [P, QW]), ring("kv", [P, 2 * D]), ring("prod", [P, D])
                firsts = ring("first", [TP, TK], I32, 1)[0]
                firstu = ring("firstu", [TP, TK], U32, 1)[0]
                qfirst = ring("qfirst", [TP, TK, QW], F32, 1)[0]
                ps = [st.enter_context(nc.psum_tensor(f"n3_ps{s}", [P, 512], F32)) for s in range(2)]
                with nc.Block() as block:
                    @block.sync
                    def _(sp):
                        c.credit(sp)
                        with nc.allow_non_contiguous_dma(reason="five numbers per edge tile"):
                            sp.dma_start(firsts[:, :], headtail[:, :, 4]).then_inc(first_in, 16)

                        def store(n, s, r):
                            c.ready(sp, "kv", n)
                            c.hold(sp)
                            sp.dma_start(kv_table[bass.ds(n * P, P), :], kv[s][:, :]).then_inc(stored[s], 16)
                            c.ready(sp, "qw", n)
                            c.hold(sp)
                            sp.dma_start(q_table[bass.ds(n * P, P), :], q[s][:, :]).then_inc(stored[s], 16)

                        def retire(n, s, r):
                            sp.wait_ge(stored[s], (r + 1) * 32)
                            c.hold(sp)
                            wait_rows(sp, s, r)
                            sp.sem_inc(c["rows_free"], 1)

                        pipelined(sp, NT, NS, [(0, store), (1, retire)])
                        sp.wait_ge(picked, 16 * TK)
                        sp.dma_start(q_starts[0:EP, :].rearrange("(k p e) f -> p k e f", e=P, p=TP)[:, :, 0, :],
                                     qfirst[:, :, :]).then_inc(first_out, 16)
                        sp.wait_ge(first_out, 16)

                    @block.gpsimd
                    def _(pool):
                        def scatter(n, s, r):
                            c.ready(pool, "idx", n)
                            c.ready(pool, "qw", n)
                            c.hold(pool)
                            pool.indirect_dma_start(q_starts[:, :], bass.IndirectOffsetOnAxis(ap=idx[s][:, :], axis=0),
                                                    q[s][:, :], None).then_inc(gathered[s], 16)

                        pipelined(pool, NT, NS, [(0, scatter)])
                        pool.wait_ge(c["rows_free"], NT + NS)
                        pool.wait_ge(first_u, 1)
                        for k in range(TK):
                            pool.indirect_dma_start(qfirst[:, k, :], None, q_table[:, :],
                                                    bass.IndirectOffsetOnAxis(ap=firstu[:, k:k + 1], axis=0)).then_inc(picked, 16)

                    @block.tensor
                    def _(pe):
                        def turn(n, s, r):
                            c.ready(pe, "xs", n)
                            c.free(pe, "at", n, 1)
                            nc.tensor.matmul(ps[0][:, 0:P], xs[s][:, :], ident[:, :], start=True, stop=True).then_inc(c["tr"], 1)

                        def product(n, s, r):
                            c.ready(pe, "at", n)
                            c.free(pe, "skip", n, 1)
                            nc.tensor.matmul(ps[1][:, :], ones[0:1, :], wr[:, R_Q:R_Q + 4, :].rearrange("p a f -> p (a f)"), start=True, stop=False)
                            nc.tensor.matmul(ps[1][:, :], xT[s][:, :], wm[:, W_Q:W_Q + 4, :].rearrange("p a f -> p (a f)"), start=False, stop=True).then_inc(c["mm"], 1)

                        pipelined(pe, NT, NS, [(0, turn), (1, product)])

                    @block.scalar
                    def _(act):
                        def own(n, s, r):
                            c.free(act, "tr", n)
                            nc.scalar.activation(xs[s][:, :], tile_of(x_now, n), ACT.Copy).then_inc(c["xs"], 1)

                        def move(n, s, r):
                            c.ready(act, "tr", n)
                            c.free(act, "mm", n)
                            nc.scalar.activation(xT[s][:, :], ps[0][:, 0:P], ACT.Copy).then_inc(c["at"], 1)

                        def split(n, s, r):
                            c.ready(act, "mm", n)
                            c.free(act, "rows_free", n)
                            c.free(act, "qw", n)
                            nc.scalar.activation(q[s][:, 0:D], ps[1][:, 0:D], ACT.Copy, scale=0.25).then_inc(c["q"], 1)
                            nc.scalar.activation(kv[s][:, :], ps[1][:, D:3 * D], ACT.Copy).then_inc(c["kv"], 1)
                            nc.scalar.activation(tile_of(h_now, n), ps[1][:, 3 * D:4 * D], ACT.Copy).then_inc(c["skip"], 1)

                        pipelined(act, NT, NS, [(0, own), (0, move), (1, split)])

                    @block.vector
                    def _(dve):
                        dve.wait_ge(first_in, 16)
                        dve.tensor_scalar(firstu[:, :], firsts[:, :], float(NP - 1), None, ALU.min).then_inc(first_u, 1)

                        def with_edges(n, s, r):
                            c.ready(dve, "q", n)
                            c.free(dve, "qw", n)
                            dve.tensor_tensor(prod[s][:, :], q[s][:, 0:D], bc[:, B_WE, :], ALU.mult).then_inc(c["qe"], 1)
                            c.ready(dve, "qe", n)
                            dve.tensor_reduce(q[s][:, D:QW], prod[s][:, :].rearrange("p (h d) -> p h d", d=HD), AX.X, ALU.add).then_inc(c["qw"], 1)

                        def index(n, s, r):
                            c.free(dve, "rows_free", n)
                            nc.vector.tensor_copy(idx[s][:, :], col(start_row, n)).then_inc(c["idx"], 1)

                        pipelined(dve, NT, NS, [(0, index), (1, with_edges)])
            count_rows(NS, NT)

        def edges_attention():
            with ExitStack() as st:
                def ring(name, shape, dt=F32, slots=ES):
                    bufs = [st.enter_context(nc.sbuf_tensor(f"e4_{name}{s}", shape, dt)) for s in range(slots)]
                    return bufs * (KS // slots)

                c = Products(sem, "e4", KS, "mask idx brk brk2 fq prod red wq al at fs bs mt dif m ex exw exv p evp")
                landed = [sem(f"e4_landed{s}") for s in range(KS)]
                stored = [sem(f"e4_stored{s}") for s in range(KS)]
                HR = TB * H
                drow, qs, kv = ring("drow", [P, TB, P], I32, 2), ring("qs", [P, TB, QW], slots=RS), ring("kv", [P, TB, 2 * D], slots=KS)
                dh, brk = ring("dh", [HR, P + 2], I32), ring("brk", [HR, P + 1])
                mask, row, idx = ring("mask", [P, TB, P], slots=KS), ring("row", [P, TB, RW], slots=RS), ring("idx", [P, TB], U32, KS)
                prod = ring("prod", [P, TB, D], slots=1)[0]
                red, wq, al = ring("red", [P, HR]), ring("wq", [P, HR]), ring("al", [P, HR])
                fs, bs, dif = ring("fs", [HR, P]), ring("bs", [HR, P]), ring("dif", [P, HR])
                msg = ring("msg", [P, TB, MW], slots=RS)
                ps_q, ps_p = (st.enter_context(nc.psum_tensor(f"e4_{k}", [P, 3 * BANK], F32)) for k in "qp")
                ps_a, ps_m = (st.enter_context(nc.psum_tensor(f"e4_{k}", [P, BANK], F32)) for k in "am")

                def in_bank(ps, t, width):
                    at = t // PT * BANK + t % PT * width
                    return ps[:, at:at + width]

                def many(ps, width, lo, hi):
                    return ps[:, 0:TM // PT * BANK].rearrange("p (b c) -> p b c", c=BANK)[:, :, 0:PT * width] \
                        .rearrange("p b (t f) -> p b t f", f=width)[:, :, :, lo:hi]

                def one(ps, width, lo, hi):
                    return in_bank(ps, TM, width)[:, lo:hi]

                def by_bank(a):
                    return a[:, 0:TM, :].rearrange("p (b t) f -> p b t f", t=PT)

                def row_free(eng, s, r):
                    if s >= RS:
                        c.hold(eng)
                        eng.wait_ge(stored[s - RS], (r + 1) * 16)
                    elif not (isinstance(r, int) and r == 0):
                        c.hold(eng)
                        eng.wait_ge(stored[s + KS - RS], r * 16)

                def weights(n):
                    return w_col[:, bass.ds(n * TB, TB)].unsqueeze(2).broadcast_to([P, TB, H])

                def heads(a):
                    return a.rearrange("p (t h) -> p t h", h=H)

                with nc.Block() as block:
                    @block.sync
                    def _(sp):
                        c.credit(sp)

                        def load(n, s, r):
                            c.free(sp, "mask", n, 2)
                            c.hold(sp)
                            sp.dma_start(drow[s][:, :, :].rearrange("p t e -> p (t e)"),
                                         dstflat[bass.ds(n * BW + 1, BW)].partition_broadcast(P)).then_inc(landed[s], 16)
                            c.free(sp, "fq", n, RS)
                            c.hold(sp)
                            sp.dma_start(qs[s][:, :, :], flat_rows(q_starts, n)).then_inc(landed[s], 16)
                            c.free(sp, "brk", n, ES)
                            c.hold(sp)
                            sp.dma_start(dh[s][:, :], dsthead[bass.ds(n * HR, HR), :]).then_inc(landed[s], 16)

                        pipelined(sp, NB, KS, [(0, load)])
                        for s in range(KS):
                            sp.wait_ge(stored[s], NB // KS * 16)

                    @block.gpsimd
                    def _(pool):
                        def gather(n, s, r):
                            c.ready(pool, "idx", n)
                            c.free(pool, "exv", n)
                            c.hold(pool)
                            for t in range(TB):
                                pool.indirect_dma_start(kv[s][:, t, :], None, kv_table[:, :],
                                                        bass.IndirectOffsetOnAxis(ap=idx[s][:, t:t + 1], axis=0)).then_inc(gathered[s], 16)

                        pipelined(pool, NB, KS, [(0, gather)])

                    @block.tensor
                    def _(pe):
                        def fill(n, s, r):
                            c.ready(pe, "mask", n)
                            pe.wait_ge(landed[s], (r + 1) * 48)
                            c.free(pe, "prod", n, 1)
                            c.free(pe, "wq", n, 1)
                            for t in range(TB):
                                last = nc.tensor.matmul(in_bank(ps_q, t, QW), mask[s][:, t, :], qs[s][:, t, :], start=True, stop=True)
                            last.then_inc(c["fq"], 1)

                        def turn(n, s, r):
                            c.ready(pe, "al", n)
                            c.free(pe, "fs", n, 1)
                            c.hold(pe)
                            nc.tensor.transpose(ps_a[0:HR, 0:P], al[s][:, :], ident[:, :]).then_inc(c["at"], 1)

                        def back(n, s, r):
                            c.ready(pe, "bs", n)
                            c.free(pe, "dif", n, 1)
                            c.free(pe, "m", n, 1)
                            c.hold(pe)
                            nc.tensor.transpose(ps_m[:, 0:HR], bs[s][:, :], ident[0:HR, 0:HR]).then_inc(c["mt"], 1)

                        def total(n, s, r):
                            c.ready(pe, "exv", n)
                            c.ready(pe, "exw", n)
                            c.free(pe, "evp", n, 1)
                            for t in range(TB):
                                last = nc.tensor.matmul(in_bank(ps_p, t, MW), mask[s][:, t, :], msg[s][:, t, :], start=True, stop=True)
                            last.then_inc(c["p"], 1)

                        pipelined(pe, NB, KS, [(4, total), (2, back), (0, fill), (1, turn)])

                    @block.scalar
                    def _(act):
                        def exp(n, s, r):
                            c.ready(act, "dif", n)
                            c.free(act, "p", n, RS)
                            nc.scalar.activation(msg[s][:, :, D:D + H], heads(dif[s][:, :]), ACT.Exp).then_inc(c["ex"], 1)

                        def evac(n, s, r):
                            row_free(act, s, r)
                            c.ready(act, "p", n)
                            nc.scalar.activation(by_bank(row[s])[:, :, :, 0:MW], many(ps_p, MW, 0, MW), ACT.Copy)
                            nc.scalar.activation(row[s][:, TM, 0:MW], one(ps_p, MW, 0, MW), ACT.Copy).then_inc(c["evp"], 1)

                        def store(n, s, r):
                            c.ready(act, "evp", n)
                            c.hold(act)
                            c.ready(act, "m", n)
                            act.dma_start(flat_rows(sums_att, n), row[s][:, :, :]).then_inc(stored[s], 16)

                        pipelined(act, NB, KS, [(0, exp), (1, evac), (1, store)], head=2)

                    @block.vector
                    def _(dve):
                        def message(n, s, r):
                            c.ready(dve, "ex", n)
                            dve.tensor_tensor(msg[s][:, :, D + H:MW], msg[s][:, :, D:D + H], weights(n), ALU.mult).then_inc(c["exw"], 1)
                            c.free(dve, "p", n, RS)
                            dve.tensor_tensor(msg[s][:, :, 0:D].rearrange("p t (h d) -> p t h d", d=HD),
                                              kv[s][:, :, D:2 * D].rearrange("p t (h d) -> p t h d", d=HD),
                                              msg[s][:, :, D:D + H].unsqueeze(3).broadcast_to([P, TB, H, HD]), ALU.mult).then_inc(c["exv"], 1)

                        def differ(n, s, r):
                            c.ready(dve, "mt", n)
                            c.free(dve, "ex", n, ES)
                            dve.tensor_tensor(dif[s][:, :], al[s][:, :], ps_m[:, 0:HR], ALU.subtract).then_inc(c["dif"], 1)
                            row_free(dve, s, r)
                            dve.tensor_copy(row[s][:, :, MW:RW], heads(ps_m[:, 0:HR])).then_inc(c["m"], 1)

                        def maxima(n, s, r):
                            c.ready(dve, "at", n)
                            c.ready(dve, "brk2", n)
                            dve.tensor_tensor_scan(fs[s][:, :], brk[s][:, 0:P], ps_a[0:HR, 0:P], -BIG, ALU.add, ALU.max).then_inc(c["fs"], 1)
                            c.ready(dve, "fs", n)
                            c.free(dve, "mt", n, ES)
                            dve.tensor_tensor_scan(bs[s][:, ::-1], brk[s][:, P:0:-1], fs[s][:, ::-1], -BIG, ALU.add, ALU.max).then_inc(c["bs"], 1)

                        def index(n, s, r):
                            nc.vector.tensor_copy(idx[s][:, :], src_i[:, bass.ds(n * TB, TB)].bitcast(U32)).then_inc(c["idx"], 1)

                        def masks(n, s, r):
                            dve.wait_ge(landed[s], (r + 1) * 48)
                            c.free(dve, "p", n)
                            mask_tile(dve, mask[s], drow[s], n).then_inc(c["mask"], 1)
                            c.free(dve, "bs", n, ES)
                            dve.tensor_tensor(brk[s][:, :], dh[s][:, 0:P + 1], dh[s][:, 1:P + 2], ALU.not_equal).then_inc(c["brk"], 1)
                            c.ready(dve, "brk", n)
                            dve.tensor_scalar(brk[s][:, :], brk[s][:, :], -BIG, None, ALU.mult).then_inc(c["brk2"], 1)

                        def scores(n, s, r):
                            c.ready(dve, "fq", n)
                            wait_rows(dve, s, r, TB)
                            c.free(dve, "red", n, 1)
                            dve.tensor_tensor(by_bank(prod), many(ps_q, QW, 0, D), by_bank(kv[s])[:, :, :, 0:D], ALU.mult)
                            dve.tensor_tensor(prod[:, TM, :], one(ps_q, QW, 0, D), kv[s][:, TM, 0:D], ALU.mult).then_inc(c["prod"], 1)
                            dve.tensor_tensor(by_bank(heads(wq[s][:, :])), many(ps_q, QW, D, QW), by_bank(weights(n)), ALU.mult)
                            dve.tensor_tensor(heads(wq[s][:, :])[:, TM, :], one(ps_q, QW, D, QW), weights(n)[:, TM, :], ALU.mult).then_inc(c["wq"], 1)
                            c.ready(dve, "prod", n)
                            dve.tensor_reduce(red[s][:, :], prod[:, :, :].rearrange("p t (h d) -> p (t h) d", d=HD), AX.X, ALU.add).then_inc(c["red"], 1)
                            c.ready(dve, "red", n)
                            c.free(dve, "dif", n, ES)
                            dve.tensor_tensor(al[s][:, :], red[s][:, :], wq[s][:, :], ALU.add).then_inc(c["al"], 1)

                        pipelined(dve, NB, KS, [(7, message), (6, differ), (5, maxima), (0, index), (3, masks), (4, scores)], head=2)
            count_rows(KS, NB, TB)

        def join_tails(scaled):
            with ExitStack() as st:
                def tmp(name, shape, dt=F32):
                    return st.enter_context(nc.sbuf_tensor(f"j_{name}", shape, dt))

                loaded, dv, pe_s, ac, masked = sem("j_loaded"), sem("j_dve"), sem("j_pe"), sem("j_act"), sem("j_masked")
                tail, head = tmp("tail", [TP, TK, RW]), tmp("head", [TP, TK, H])
                ht, lastrow = tmp("ht", [TP, TK, 5], I32), tmp("lastrow", [H, ET + 2], I32)
                same, twice, both, lastf = (tmp(k, [TP, TK]) for k in "same twice both lastf".split())
                mm, dif, sc = tmp("mm", [TP, TK, H]), tmp("dif", [TP, 2, TK, H]), tmp("sc", [TP, 2, TK, H])
                brk, fs, bs = tmp("brk", [H, ET + 1]), tmp("fs", [H, ET]), tmp("bs", [H, ET])
                ps = [st.enter_context(nc.psum_tensor(f"j_ps{s}", [P, 512], F32)) for s in range(2)]
                with nc.Block() as block:
                    @block.sync
                    def _(sp):
                        sp.dma_start(tail[:, :, :], tails(sums_att, RW)).then_inc(loaded, 16)
                        with nc.allow_non_contiguous_dma(reason="one maximum per head and edge tile"):
                            sp.dma_start(head[:, :, :], sums_att[P:EP + P, :].rearrange("(k p e) f -> p k e f", e=P, p=TP)[:, :, 0, MW:RW]).then_inc(loaded, 16)
                        sp.dma_start(ht[:, :, :], headtail).then_inc(loaded, 16)
                        sp.dma_start(lastrow[:, :], lasthead).then_inc(loaded, 16)

                    @block.tensor
                    def _(pe):
                        pe.wait_ge(dv, 7)
                        for k in range(TK):
                            last = nc.tensor.transpose(ps[0][0:H, k * TP:(k + 1) * TP], mm[:, k, :], ident[0:TP, 0:TP])
                        last.then_inc(pe_s, 1)
                        pe.wait_ge(dv, 11)
                        for k in range(TK):
                            last = nc.tensor.transpose(ps[1][0:TP, k * H:(k + 1) * H], bs[:, k * TP:(k + 1) * TP], ident[0:H, 0:H])
                        last.then_inc(pe_s, 1)

                    @block.scalar
                    def _(act):
                        act.wait_ge(dv, 13)
                        nc.scalar.activation(sc[:, :, :, :], dif[:, :, :, :], ACT.Exp).then_inc(ac, 1)

                    @block.vector
                    def _(dve):
                        n = [0]

                        def after(ins):
                            n[0] += 1
                            ins.then_inc(dv, 1)
                            dve.wait_ge(dv, n[0])

                        dve.wait_ge(loaded, 64)
                        after(dve.tensor_tensor(same[:, :], ht[:, :, 0], ht[:, :, 1], ALU.is_equal))
                        after(dve.tensor_tensor(twice[:, :], ht[:, :, 2], ht[:, :, 3], ALU.is_equal))
                        after(dve.tensor_tensor(both[:, :], ht[:, :, 0], ht[:, :, 2], ALU.is_equal))
                        after(dve.tensor_tensor(both[:, :], both[:, :], twice[:, :], ALU.mult))
                        after(dve.tensor_scalar(lastf[:, :], both[:, :], -1.0, 1.0, ALU.mult, ALU.add))
                        after(dve.tensor_scalar(twice[:, :], same[:, :], 1.0, BIG, ALU.subtract, ALU.mult))
                        dve.tensor_tensor(head[:, :, :], head[:, :, :], twice[:, :].unsqueeze(2).broadcast_to([TP, TK, H]), ALU.add).then_inc(masked, 1)
                        dve.wait_ge(masked, 1)
                        after(dve.tensor_tensor(mm[:, :, :], tail[:, :, MW:RW], head[:, :, :], ALU.max))
                        after(dve.tensor_tensor(brk[:, :], lastrow[:, 0:ET + 1], lastrow[:, 1:ET + 2], ALU.not_equal))
                        after(dve.tensor_scalar(brk[:, :], brk[:, :], -BIG, None, ALU.mult))
                        dve.wait_ge(pe_s, 1)
                        after(dve.tensor_tensor_scan(fs[:, :], brk[:, 0:ET], ps[0][0:H, 0:ET], -BIG, ALU.add, ALU.max))
                        after(dve.tensor_tensor_scan(bs[:, ::-1], brk[:, ET:0:-1], fs[:, ::-1], -BIG, ALU.add, ALU.max))
                        dve.wait_ge(pe_s, 2)
                        m_all = ps[1][0:TP, 0:TK * H].rearrange("p (k h) -> p k h", h=H)
                        after(dve.tensor_tensor(dif[:, 0, :, :], tail[:, :, MW:RW], m_all, ALU.subtract))
                        after(dve.tensor_tensor(dif[:, 1, :, :], head[:, :, :], m_all, ALU.subtract))
                        dve.wait_ge(ac, 1)
                        for k in range(TK):
                            dve.tensor_tensor(scaled[:, k, 0:D].rearrange("p (h d) -> p h d", d=HD),
                                              tail[:, k, 0:D].rearrange("p (h d) -> p h d", d=HD),
                                              sc[:, 0, k, :].unsqueeze(2).broadcast_to([TP, H, HD]), ALU.mult)
                            dve.tensor_tensor(scaled[:, k, D:MW].rearrange("p (a h) -> p a h", h=H),
                                              tail[:, k, D:MW].rearrange("p (a h) -> p a h", h=H),
                                              sc[:, 0, k, :].unsqueeze(1).broadcast_to([TP, 2, H]), ALU.mult)
                        dve.tensor_tensor(scaled[:, :, MW:RW], sc[:, 1, :, :], lastf[:, :].unsqueeze(2).broadcast_to([TP, TK, H]), ALU.mult)
                        dve.tensor_copy(scaled[:, :, RW:SW], lastf[:, :].unsqueeze(2))

        def nodes_attention(scaled, att):
            with ExitStack() as st:
                def ring(name, shape, dt=F32, slots=NS):
                    return [st.enter_context(nc.sbuf_tensor(f"n4_{name}{s}", shape, dt)) for s in range(slots)]

                c = Products(sem, "n4", NS, "idx z zt nl en t1 t2 sum")
                idx, g, z = ring("idx", [P, 1], U32), ring("g", [P, RW]), ring("z", [TP, TK, P])
                nl, en = ring("nl", [P, 1]), ring("en", [P, H])
                ps = st.enter_context(nc.psum_tensor("n4_ps", [P, 512], F32))
                with nc.Block() as block:
                    @block.sync
                    def _(sp):
                        c.credit(sp)

                    @block.gpsimd
                    def _(pool):
                        def gather(n, s, r):
                            c.ready(pool, "idx", n)
                            c.free(pool, "sum", n)
                            c.hold(pool)
                            pool.indirect_dma_start(g[s][:, :], None, sums_att[:, :],
                                                    bass.IndirectOffsetOnAxis(ap=idx[s][:, :], axis=0)).then_inc(gathered[s], 16)

                        pipelined(pool, NT, NS, [(0, gather)])

                    @block.tensor
                    def _(pe):
                        def earlier(n, s, r):
                            c.ready(pe, "z", n)
                            c.free(pe, "sum", n, 1)
                            for k in range(TK):
                                last = nc.tensor.matmul(ps[:, 0:SW], z[s][:, k, :], scaled[:, k, :], start=(k == 0), stop=(k == TK - 1))
                            last.then_inc(c["zt"], 1)

                        pipelined(pe, NT, NS, [(0, earlier)])

                    @block.vector
                    def _(dve):
                        def index(n, s, r):
                            c.free(dve, "sum", n)
                            nc.vector.tensor_copy(idx[s][:, :], col(end_row, n)).then_inc(c["idx"], 1)
                            c.free(dve, "zt", n)
                            pick(dve, z[s], n).then_inc(c["z"], 1)

                        def whole(n, s, r):
                            c.ready(dve, "zt", n)
                            dve.tensor_scalar(nl[s][:, :], ps[:, RW:SW], -1.0, 1.0, ALU.mult, ALU.add).then_inc(c["nl"], 1)
                            c.ready(dve, "nl", n)
                            dve.tensor_scalar(en[s][:, :], ps[:, MW:RW], nl[s][:, 0:1], None, ALU.add).then_inc(c["en"], 1)
                            c.ready(dve, "en", n)
                            wait_rows(dve, s, r)
                            dve.tensor_tensor(g[s][:, 0:D].rearrange("p (h d) -> p h d", d=HD), g[s][:, 0:D].rearrange("p (h d) -> p h d", d=HD),
                                              en[s][:, :].unsqueeze(2).broadcast_to([P, H, HD]), ALU.mult).then_inc(c["t1"], 1)
                            dve.tensor_tensor(g[s][:, D:MW].rearrange("p (a h) -> p a h", h=H), g[s][:, D:MW].rearrange("p (a h) -> p a h", h=H),
                                              en[s][:, :].unsqueeze(1).broadcast_to([P, 2, H]), ALU.mult).then_inc(c["t2"], 1)
                            c.ready(dve, "t1", n)
                            c.ready(dve, "t2", n)
                            dve.tensor_tensor(tile_of(att, n), g[s][:, 0:MW], ps[:, 0:MW], ALU.add).then_inc(c["sum"], 1)

                        pipelined(dve, NT, NS, [(0, index), (1, whole)])
            count_rows(NS, NT)

        def layer3_nodes():
            with ExitStack() as st:
                scaled = st.enter_context(nc.sbuf_tensor("scaled", [TP, TK, SW], F32))
                att = st.enter_context(nc.sbuf_tensor("att", [P, NT, MW], F32))
                join_tails(scaled)
                nodes_attention(scaled, att)
                finish(att)

        def finish(att):
            with ExitStack() as st:
                k = Steps("fin")
                c = Products(sem, "fo", NS, "xs tr at mm res")
                sq = st.enter_context(nc.sbuf_tensor("fin_sq", [P, NT, D], F32))
                small = st.enter_context(nc.sbuf_tensor("fin_small", [P, 3, NT], F32))
                den = st.enter_context(nc.sbuf_tensor("fin_den", [P, NT, H], F32))
                xs = [st.enter_context(nc.sbuf_tensor(f"fin_xs{s}", [P, D], F32)) for s in range(NS)]
                xT = [st.enter_context(nc.sbuf_tensor(f"fin_xT{s}", [P, P], F32)) for s in range(NS)]
                ps = [st.enter_context(nc.psum_tensor(f"fin_ps{s}", [P, 512], F32)) for s in range(2)]
                dv, ac, stored = k.sem["dve"], k.sem["act"], k.sem["dma"]
                with nc.Block() as block:
                    @block.sync
                    def _(sp):
                        c.credit(sp)
                        sp.wait_ge(dv, 21)
                        full = N // P
                        sp.dma_start(out[0:full * P, :].rearrange("(j p) f -> p j f", p=P), x_now[:, 0:full, :]).then_inc(stored, 16)
                        sp.dma_start(out[full * P:N, :], x_now[0:N - full * P, full, :]).then_inc(stored, 16)
                        sp.wait_ge(stored, 32)

                    @block.tensor
                    def _(pe):
                        def turn(n, s, r):
                            c.ready(pe, "xs", n)
                            c.free(pe, "at", n, 1)
                            nc.tensor.matmul(ps[0][:, 0:P], xs[s][:, :], ident[:, :], start=True, stop=True).then_inc(c["tr"], 1)

                        def product(n, s, r):
                            c.ready(pe, "at", n)
                            c.free(pe, "res", n, 1)
                            nc.tensor.matmul(ps[1][:, 0:D], ones[0:1, :], wr[:, R_O, :], start=True, stop=False)
                            nc.tensor.matmul(ps[1][:, 0:D], xT[s][:, :], wm[:, W_O, :], start=False, stop=True).then_inc(c["mm"], 1)

                        pipelined(pe, NT, NS, [(0, turn), (1, product)])

                    @block.scalar
                    def _(act):
                        act.wait_ge(dv, 6)

                        def own(n, s, r):
                            c.free(act, "tr", n)
                            nc.scalar.activation(xs[s][:, :], tile_of(h_now, n), ACT.Copy).then_inc(c["xs"], 1)

                        def move(n, s, r):
                            c.ready(act, "tr", n)
                            c.free(act, "mm", n)
                            nc.scalar.activation(xT[s][:, :], ps[0][:, 0:P], ACT.Copy).then_inc(c["at"], 1)

                        pipelined(act, NT, NS, [(0, own), (0, move)])
                        norm_squares(act, k, h_now, sq, small, 6)
                        norm_squares(act, k, x_now, sq, small, 15)

                    @block.vector
                    def _(dve):
                        dve.tensor_scalar(den[:, :, :], att[:, :, D:D + H], 1e-16, None, ALU.max).then_inc(dv, 1)
                        dve.tensor_tensor(sq[:, :, :].rearrange("p j (h d) -> p j h d", d=HD),
                                          bc[:, B_WE, :].rearrange("p (h d) -> p h d", d=HD).unsqueeze(1).broadcast_to([P, NT, H, HD]),
                                          att[:, :, D + H:MW].unsqueeze(3).broadcast_to([P, NT, H, HD]), ALU.mult).then_inc(dv, 1)
                        dve.wait_ge(dv, 1)
                        dve.reciprocal(den[:, :, :], den[:, :, :]).then_inc(dv, 1)
                        dve.wait_ge(dv, 2)
                        dve.tensor_tensor(sq[:, :, :], sq[:, :, :], att[:, :, 0:D], ALU.add).then_inc(dv, 1)
                        dve.wait_ge(dv, 4)
                        dve.tensor_tensor(sq[:, :, :].rearrange("p j (h d) -> p (j h) d", d=HD), sq[:, :, :].rearrange("p j (h d) -> p (j h) d", d=HD),
                                          den[:, :, :].rearrange("p j h -> p (j h)").unsqueeze(2).broadcast_to([P, NT * H, HD]), ALU.mult).then_inc(dv, 1)
                        dve.wait_ge(dv, 5)
                        dve.tensor_tensor(h_now[:, :, :], sq[:, :, :], h_now[:, :, :], ALU.add).then_inc(dv, 1)

                        def residual(n, s, r):
                            c.ready(dve, "mm", n)
                            dve.tensor_tensor(tile_of(h_now, n), ps[1][:, 0:D], tile_of(x_now, n), ALU.add).then_inc(c["res"], 1)

                        pipelined(dve, NT, NS, [(0, residual)])
                        dve.wait_ge(c["res"], NT + NS)
                        norm_rows(dve, k, h_now, sq, small, 6, 1)
                        dve.tensor_tensor(h_now[:, :, :], h_now[:, :, :], cols(bc[:, B_G3:B_G3 + 1, :]), ALU.mult).then_inc(dv, 1)
                        dve.wait_ge(dv, 13)
                        dve.tensor_tensor(h_now[:, :, :], h_now[:, :, :], cols(bc[:, B_B3:B_B3 + 1, :]), ALU.add).then_inc(dv, 1)
                        dve.wait_ge(dv, 14)
                        dve.tensor_tensor(x_now[:, :, :], h_now[:, :, :], x_now[:, :, :], ALU.add).then_inc(dv, 1)
                        dve.wait_ge(dv, 15)
                        norm_rows(dve, k, x_now, sq, small, 15, 3)

        stages = [
            prepare,
            edges_layer0,
            lambda: degrees("d0", deg_in, True),
            nodes_layer0,
            lambda: edges_sum("e1", tab[1], sums[1], count_src=True),
            lambda: degrees("d1", deg_out, False),
            lambda: nodes_sage("n1a", sums[1], tab[2], x_now, W_S0, W_N0, R_S0, False),
            lambda: edges_sum("e2", tab[2], sums[2], clear=q_starts),
            lambda: nodes_sage("n1b", sums[2], tab[3], h_now, W_S1, W_N1, R_S1, True),
            lambda: edges_sum("e3", tab[3], sums[3]),
            nodes_gcn,
            batch_norm,
            project,
            edges_attention,
            layer3_nodes,
        ]
        for stage in stages:
            stage()
            end_stage()


def kernel(**inputs):
    import numpy as np
    import concourse.bacc as bacc
    from concourse.bass_utils import run_bass_kernel_spmd as run

    a = {k: np.ascontiguousarray(v) for k, v in inputs.items()}
    f4 = np.float32

    def heads_last(w):
        return w.transpose(1, 0, 2).reshape(D, H * HD)

    def cut(w):
        return [w[i:i + P, j:j + P] for i in range(0, w.shape[0], P) for j in range(0, w.shape[1], P)]

    x = np.zeros((NP, D), f4)
    x[:N] = a["x"]
    src = np.full((EP,), N, np.int32)
    src[:E] = a["src"]
    dst = np.full((EP,), NP, np.int32)
    dst[:E] = a["dst"]
    flat = np.full((EP + 2,), -1, np.int32)
    flat[1:EP + 1] = dst
    wts = np.zeros((EP,), f4)
    wts[:E] = a["edge_weight"]
    edges = np.zeros((D, EP), f4)
    edges[:, :E] = a["edge_attr_128"].T
    first, last = dst[0::P], dst[P - 1::P]
    after = [np.append(v[1:], np.int32(-1)) for v in (first, last)]
    after2 = np.append(after[0][1:], np.int32(-1))
    headtail = np.stack([last, after[0], after[1], after2, first], -1).reshape(TK, TP, 5).transpose(1, 0, 2)
    window = np.lib.stride_tricks.sliding_window_view(flat, P + 2)[::P]
    dsthead = np.repeat(window.reshape(ET, 1, P + 2), H, 1).reshape(ET * H, P + 2)
    lastrow = np.full((ET + 2,), -1, np.int32)
    lastrow[1:ET + 1] = last
    mats = cut(a["L0_gnn_W_e_k"]) + cut(a["L0_gnn_W1"]) + cut(a["L0_gnn_W2"])
    for k in ("L1_gnn_W_self0", "L1_gnn_W_neigh0", "L1_gnn_W_self1", "L1_gnn_W_neigh1", "L2_gnn_W"):
        mats += cut(a[k])
    mats += [heads_last(a[f"L3_gnn_W{k}"]) for k in ("q", "k", "v", "skip")] + [a["L3_gnn_Wo"]]
    rows = [a["L0_gnn_b2"], a["L1_gnn_b0"], a["L1_gnn_b1"]] + [a[f"L3_gnn_b{k}"].reshape(-1) for k in ("q", "k", "v", "skip", "o")]
    wide = [a["L0_gnn_W_e_b"], a["L2_gnn_gamma"], a["L2_gnn_beta"], a["L3_gnn_We"].reshape(-1), a["L3_gnn_gamma"], a["L3_gnn_beta"], a["L3_gnn_beta"]]
    gvec = np.concatenate([a["L0_gnn_globals_g"].reshape(P, 1), np.broadcast_to(a["L0_gnn_eps"], (P, 1)), a["L0_gnn_b1"].reshape(4, P).T], 1)

    def per_partition(v):
        return v.reshape(ET, P).T

    given = {
        "xp": x, "srccol": per_partition(src), "dstcol": per_partition(dst), "dstflat": flat, "dsthead": dsthead,
        "lasthead": np.broadcast_to(lastrow, (H, ET + 2)), "headtail": headtail, "wcol": per_partition(wts),
        "edgesT": edges, "wmat": np.stack(mats, 1), "wrow": np.stack(rows)[None], "wbc": np.stack(wide), "gvec": gvec,
    }
    nc = bacc.Bacc("TRN2", target_bir_lowering=False, num_devices=1)
    arrays, args = {}, {}
    for name, v in given.items():
        v = np.ascontiguousarray(v)
        arrays[f"in_{name}"] = v
        args[name] = nc.dram_tensor(f"in_{name}", v.shape, mybir.dt.from_np(v.dtype), kind="ExternalInput").ap()
    args["out"] = nc.dram_tensor("out", (N, D), F32, kind="ExternalOutput").ap()
    gnn_kernel(nc, **args)
    return run(nc, [arrays], core_ids=[0]).results[0]["out"]
```

```python
import concourse.bass as bass
from concourse import mybir
from contextlib import ExitStack

F32 = mybir.dt.float32
I32 = mybir.dt.int32
U32 = mybir.dt.uint32
BF16 = mybir.dt.bfloat16
ALU = mybir.AluOpType
ACT = mybir.ActivationFunctionType
AX = mybir.AxisListType

P = 128
D = 128
N, E = 3125, 50000
NT = -(-N // P)
NP = NT * P
TB = 7
NB = 56
ET = TB * NB
EP = ET * P
BW = TB * P
TK = 4
TP = ET // TK
H, HD = 8, 16
QW = D + H
MW = D + 2 * H
RW = MW + H
SW = MW + H + 1
ES = 4
KS = 8
RS = 2
BANK = 512
PT = BANK // MW
TM = TB // PT * PT
NS = 5
BIG = 1.0e30
assert TM == TB - 1 and NB % KS == 0 and KS % ES == 0 and NT % NS == 0 and EP >= E and ET == TK * TP


def pipelined(eng, count, slots, sections, head=1):
    deepest = max(lag for lag, _ in sections)
    assert deepest <= slots and count % slots == 0
    for step in range(head * slots):
        for lag, do in sections:
            if step >= lag:
                do(step - lag, (step - lag) % slots, (step - lag) // slots)
    with eng.Fori(head, count // slots) as i:
        for k in range(slots):
            for lag, do in sections:
                do(i * slots + (k - lag), (k - lag) % slots, i + (k - lag) // slots)
    for step in range(count, count + deepest):
        for lag, do in sections:
            if step - lag < count:
                do(step - lag, (step - lag) % slots, (step - lag) // slots)


class Products:

    def __init__(self, sem, stage, slots, names):
        self.slots = slots
        self.of = {name: sem(f"{stage}_{name}") for name in (names + " held").split()}

    def credit(self, eng):
        for s in self.of.values():
            eng.sem_inc(s, self.slots)

    def __getitem__(self, name):
        return self.of[name]

    def ready(self, eng, name, n):
        eng.wait_ge(self.of[name], n + (1 + self.slots))

    def hold(self, eng):
        eng.sem_inc(self.of["held"], 1)

    def free(self, eng, name, n, slots=None):
        eng.wait_ge(self.of[name], n + (1 + self.slots - (slots or self.slots)))


def gnn_kernel(nc, xp, srccol, dstcol, dstflat, dsthead, lasthead, headtail, wcol, edgesT, wmat, wrow, wbc, gvec, out):
    ctx = ExitStack()
    with ctx:
        def sb(name, shape, dt=F32):
            return ctx.enter_context(nc.sbuf_tensor(name, shape, dt))

        stage_sems = []
        gathered = [nc.alloc_semaphore(f"gathered{s}") for s in range(KS)]
        before = [0] * KS

        def wait_rows(eng, s, r, copies=1):
            eng.wait_ge(gathered[s], (r + 1) * (16 * copies) + before[s])

        def count_rows(slots, items, copies=1):
            for s in range(slots):
                before[s] += items // slots * copies * 16
        picked = nc.alloc_semaphore("picked")
        late_loaded = nc.alloc_semaphore("late_loaded")

        def sem(name):
            stage_sems.append(nc.alloc_semaphore(name))
            return stage_sems[-1]

        def end_stage():
            with nc.Block() as block:
                @block.sync
                def _(sp):
                    for s in stage_sems:
                        sp.sem_clear(s)
            for s in stage_sems:
                nc.release_semaphore(s)
            stage_sems.clear()

        def dram(name, shape, dt=F32):
            return nc.dram_tensor(name, shape, dt, kind="Internal").ap()

        tab = [dram(f"table{i}", [NP, D]) for i in range(4)]
        sums = [dram(f"sums{i}", [EP + P, D]) for i in range(4)]
        kv_table = dram("kv_table", [NP, 2 * D])
        q_table = dram("q_table", [NP, QW])
        q_starts = dram("q_starts", [EP + NP, QW])
        sums_att = dram("sums_att", [EP + P, RW])

        x_now = sb("x_now", [P, NT, D])
        h_now = sb("h_now", [P, NT, D])
        wm = sb("wm", [P, 23, D])
        wr = sb("wr", [1, 4, D])
        bc = sb("bc", [P, 10, D])
        W_E, W_1, W_1G, W_2, W_S0, W_N0, W_S1, W_N1, W_L2, W_Q, W_O = 0, 1, 5, 9, 13, 14, 15, 16, 17, 18, 22
        R_B2, R_S0, R_S1, R_O = range(4)
        B_EB, B_G2, B_B2, B_WE, B_G3, B_B3, B_Q = range(7)
        ident = sb("ident", [P, P])
        ones = sb("ones", [P, P])
        iota = sb("iota", [P, P])
        tri = sb("tri", [P, P])
        iota_hi = sb("iota_hi", [P, NT])
        src_i = sb("src_i", [P, ET], I32)
        dst_i = sb("dst_i", [P, ET], I32)
        w_col = sb("w_col", [P, ET])
        key_rel = sb("key_rel", [TP, NT, TK])
        deg_in = sb("deg_in", [P, NT])
        deg_out = sb("deg_out", [P, NT])
        end_row = sb("end_row", [P, NT], U32)
        start_row = sb("start_row", [P, NT], U32)
        r_in = sb("r_in", [P, NT])
        rs_in = sb("rs_in", [P, NT])
        rs_out = sb("rs_out", [P, NT])
        eps5 = sb("eps5", [P, 1])
        one_eps = sb("one_eps", [P, 1])
        c1 = sb("c1", [P, 4])
        g_in = sb("g_in", [P, 6])
        rowmask = sb("rowmask", [P, NT])

        def flat_rows(table, n, width=BW):
            return table[bass.ds(n * width, width), :].rearrange("(t p) f -> p t f", p=P)

        def prepare():
            with ExitStack() as st:
                x_in = [sem(f"prep_x_in{h}") for h in range(2)]
                summed = [sem(f"prep_summed{h}") for h in range(2)]
                bias_in = sem("prep_bias_in")
                parts = [slice(0, NT // 2), slice(NT // 2, NT)]
                loaded, made, done, stored = sem("prep_loaded"), sem("prep_made"), sem("prep_done"), sem("prep_stored")
                zero = st.enter_context(nc.sbuf_tensor("prep_zero", [P, RW], F32))
                xb = st.enter_context(nc.sbuf_tensor("prep_xb", [P, NT, D], F32))
                ht = st.enter_context(nc.sbuf_tensor("prep_ht", [TP, TK, 5], I32))
                same = st.enter_context(nc.sbuf_tensor("prep_same", [TP, TK], F32))
                key = st.enter_context(nc.sbuf_tensor("prep_key", [TP, TK], F32))
                base = st.enter_context(nc.sbuf_tensor("prep_base", [P, NT], F32))
                with nc.Block() as block:
                    @block.sync
                    def _(sp):
                        for part, x_ready in zip(parts, x_in):
                            sp.dma_start(x_now[:, part, :], xp.rearrange("(j p) f -> p j f", p=P)[:, part, :]).then_inc(x_ready, 16)
                        sp.dma_start(src_i[:, :], srccol).then_inc(loaded, 16)
                        sp.dma_start(dst_i[:, :], dstcol).then_inc(loaded, 16)
                        sp.dma_start(wm[:, W_E, :], wmat[:, W_E, :]).then_inc(loaded, 16)
                        for part, sum_ready in zip(parts, summed):
                            sp.wait_ge(sum_ready, 1)
                            sp.dma_start(tab[0].rearrange("(j p) f -> p j f", p=P)[:, part, :], xb[:, part, :]).then_inc(stored, 16)
                        sp.dma_start(wm[:, W_1:, :], wmat[:, W_1:, :]).then_inc(late_loaded, 16)
                        sp.dma_start(wr[:, :, :], wrow).then_inc(late_loaded, 16)
                        sp.dma_start(w_col[:, :], wcol).then_inc(late_loaded, 16)
                        sp.wait_ge(stored, 16 * (2 + len(sums) + 1))
                        sp.wait_ge(loaded, 16 * 5)

                    @block.scalar
                    def _(act):
                        act.dma_start(bc[:, :, :], wbc.partition_broadcast(P)).then_inc(bias_in, 16)
                        act.dma_start(ht[:, :, :], headtail).then_inc(loaded, 16)
                        act.dma_start(g_in[:, :], gvec).then_inc(loaded, 16)
                        act.wait_ge(done, 1)
                        for t in sums:
                            act.dma_start(t[EP:EP + P, :], zero[:, 0:D]).then_inc(stored, 16)
                        act.dma_start(sums_att[EP:EP + P, :], zero[:, :]).then_inc(stored, 16)

                    @block.gpsimd
                    def _(pool):
                        pool.memset(ones[:, :], 1.0).then_inc(made, 1)
                        pool.memset(eps5[:, :], 1e-5).then_inc(made, 1)
                        pool.iota(iota[:, :], [[1, P]], base=0, channel_multiplier=0,
                                  allow_small_or_imprecise_dtypes=True).then_inc(made, 1)
                        pool.iota(iota_hi[:, :], [[1, NT]], base=0, channel_multiplier=0,
                                  allow_small_or_imprecise_dtypes=True).then_inc(made, 1)
                        pool.iota(base[:, :], [[P, NT]], base=0, channel_multiplier=0,
                                  allow_small_or_imprecise_dtypes=True).then_inc(made, 1)
                        pool.wait_ge(made, 5)
                        pool.affine_select(out=ident[:, :], in_=ones[:, :], compare_op=ALU.is_equal, fill=0.0,
                                           base=0, pattern=[[-1, P]], channel_multiplier=1).then_inc(made, 1)
                        pool.affine_select(out=tri[:, :], in_=ones[:, :], compare_op=ALU.is_ge, fill=0.0,
                                           base=0, pattern=[[1, P]], channel_multiplier=-1).then_inc(made, 1)
                        pool.affine_select(out=rowmask[:, :], in_=ones[:, 0:NT], compare_op=ALU.is_ge, fill=0.0,
                                           base=N - 1, pattern=[[-P, NT]], channel_multiplier=-1).then_inc(made, 1)

                    @block.vector
                    def _(dve):
                        dve.memset(zero[:, :], 0.0).then_inc(done, 1)
                        dve.memset(deg_in[:, :], 0.0)
                        dve.memset(deg_out[:, :], 0.0)
                        dve.wait_ge(bias_in, 16)
                        for part, x_ready, sum_ready in zip(parts, x_in, summed):
                            dve.wait_ge(x_ready, 16)
                            dve.tensor_tensor(xb[:, part, :], x_now[:, part, :],
                                              bc[:, B_EB:B_EB + 1, :].broadcast_to([P, part.stop - part.start, D]), ALU.add).then_inc(sum_ready, 1)
                        dve.wait_ge(loaded, 16 * 5)
                        dve.wait_ge(made, 8)
                        dve.tensor_tensor(same[:, :], ht[:, :, 0], ht[:, :, 1], ALU.is_equal).then_inc(made, 1)
                        dve.wait_ge(made, 9)
                        dve.scalar_tensor_tensor(key[:, :], ht[:, :, 0], 1.0, same[:, :], ALU.add, ALU.mult).then_inc(made, 1)
                        dve.wait_ge(made, 10)
                        dve.scalar_tensor_tensor(key_rel[:, :, :],
                                                 key[:, :].unsqueeze(1).broadcast_to([TP, NT, TK]), -1.0,
                                                 base[0:TP, :].unsqueeze(2).broadcast_to([TP, NT, TK]),
                                                 ALU.add, ALU.subtract).then_inc(made, 1)
                        dve.tensor_scalar(one_eps[:, :], g_in[:, 1:2], 1.0, None, ALU.add)

        def hidden_bias():
            with ExitStack() as st:
                sums_ready = sem("hb_sums")
                ps = st.enter_context(nc.psum_tensor("hb_ps", [P, 512], F32))
                with nc.Block() as block:
                    @block.tensor
                    def _(pe):
                        pe.wait_ge(late_loaded, 16 * 3)
                        for c in range(4):
                            last = nc.tensor.matmul(ps[:, c:c + 1], wm[:, W_1G + c, :], g_in[:, 0:1], start=True, stop=True)
                        last.then_inc(sums_ready, 1)

                    @block.vector
                    def _(dve):
                        dve.wait_ge(sums_ready, 1)
                        dve.tensor_tensor(c1[:, :], ps[:, 0:4], g_in[:, 2:6], ALU.add)

        def mask_tile(dve, mask, dstrow, n):
            return dve.tensor_tensor(mask[:, :, :], dstrow[:, :, :],
                                     dst_i[:, bass.ds(n * TB, TB)].unsqueeze(2).broadcast_to([P, TB, P]), ALU.is_equal)

        def edges_layer0():
            with ExitStack() as st:
                def ring(name, shape, dt=F32, slots=ES):
                    return [st.enter_context(nc.sbuf_tensor(f"e0_{name}{s}", shape, dt)) for s in range(slots)]

                c = Products(sem, "e0", ES, "pre mask idx x clamp expd w ln sig t m p evac lo cnt acc")
                landed = [sem(f"e0_landed{s}") for s in range(ES)]
                stored = [sem(f"e0_stored{s}") for s in range(ES)]
                eT, drow = ring("eT", [P, TB, P]), ring("drow", [P, TB, P], I32)
                g, x, u, w = (ring(k, [P, TB, D]) for k in "gxuw")
                mask, row, idx = ring("mask", [P, TB, P]), ring("row", [P, TB, D]), ring("idx", [P, TB], U32)
                lo, hi = ring("lo", [P, TB, P], BF16, 1)[0], ring("hi", [P, TB, NT], BF16, 1)[0]
                bins = ring("bins", [P, 2, ET], I32, 1)[0]
                two = ring("two", [P, 1], F32, 1)[0]
                binned = sem("e0_binned")
                ps_pre = [st.enter_context(nc.psum_tensor(f"e0_pre{s}", [P, 1024], F32)) for s in range(2)]
                ps_sum = st.enter_context(nc.psum_tensor("e0_sum", [P, 1024], F32))
                ps_cnt = st.enter_context(nc.psum_tensor("e0_cnt", [P, 512], F32))

                def as_tiles(ps):
                    return ps[:, 0:BW].rearrange("p (t f) -> p t f", f=P)

                with nc.Block() as block:
                    @block.sync
                    def _(sp):
                        c.credit(sp)

                        def load(n, s, r):
                            c.free(sp, "pre", n)
                            c.hold(sp)
                            sp.dma_start(eT[s][:, :, :], edgesT[:, bass.ds(n * BW, BW)].rearrange("p (t e) -> p t e", e=P)).then_inc(landed[s], 16)
                            c.free(sp, "mask", n)
                            c.hold(sp)
                            sp.dma_start(drow[s][:, :, :].rearrange("p t e -> p (t e)"),
                                         dstflat[bass.ds(n * BW + 1, BW)].partition_broadcast(P)).then_inc(landed[s], 16)

                        pipelined(sp, NB, ES, [(0, load)])
                        for s in range(ES):
                            sp.wait_ge(stored[s], NB // ES * 16)

                    @block.gpsimd
                    def _(pool):
                        def gather(n, s, r):
                            c.ready(pool, "idx", n)
                            c.free(pool, "x", n)
                            c.hold(pool)
                            for t in range(TB):
                                pool.indirect_dma_start(g[s][:, t, :], None, tab[0][:, :],
                                                        bass.IndirectOffsetOnAxis(ap=idx[s][:, t:t + 1], axis=0)).then_inc(gathered[s], 16)

                        pipelined(pool, NB, ES, [(0, gather)])

                    @block.tensor
                    def _(pe):
                        def pre(n, s, r):
                            pe.wait_ge(landed[s], (r + 1) * 32)
                            c.free(pe, "x", n, 2)
                            for t in range(TB):
                                last = nc.tensor.matmul(as_tiles(ps_pre[s % 2])[:, t, :], eT[s][:, t, :], wm[:, W_E, :], start=True, stop=True)
                            last.then_inc(c["pre"], 1)

                        def count(n, s, r):
                            c.ready(pe, "lo", n)
                            c.free(pe, "acc", n, 1)
                            for t in range(TB):
                                last = nc.tensor.matmul(ps_cnt[:, 0:NT], lo[:, t, :], hi[:, t, :], start=(t == 0), stop=(t == TB - 1))
                            last.then_inc(c["cnt"], 1)

                        def total(n, s, r):
                            c.ready(pe, "m", n)
                            c.free(pe, "evac", n, 1)
                            for t in range(TB):
                                last = nc.tensor.matmul(as_tiles(ps_sum)[:, t, :], mask[s][:, t, :], x[s][:, t, :], start=True, stop=True)
                            last.then_inc(c["p"], 1)

                        pipelined(pe, NB, ES, [(0, pre), (3, count), (4, total)])

                    @block.scalar
                    def _(act):
                        def exp(n, s, r):
                            c.ready(act, "clamp", n)
                            nc.scalar.activation(u[s][:, :, :], u[s][:, :, :], ACT.Exp).then_inc(c["expd"], 1)

                        def sig(n, s, r):
                            c.ready(act, "w", n)
                            nc.scalar.activation(u[s][:, :, :], w[s][:, :, :], ACT.Ln, bias=two[:, :]).then_inc(c["ln"], 1)
                            c.ready(act, "ln", n)
                            nc.scalar.activation(u[s][:, :, :], u[s][:, :, :], ACT.Exp, scale=-1.0).then_inc(c["sig"], 1)

                        def evac(n, s, r):
                            c.ready(act, "p", n)
                            if not (isinstance(r, int) and r == 0):
                                c.hold(act)
                                act.wait_ge(stored[s], r * 16)
                            nc.scalar.activation(row[s][:, :, :], as_tiles(ps_sum), ACT.Copy).then_inc(c["evac"], 1)

                        def store(n, s, r):
                            c.ready(act, "evac", n)
                            act.dma_start(flat_rows(sums[0], n), row[s][:, :, :]).then_inc(stored[s], 16)

                        act.wait_ge(binned, 5)
                        act.preload_act_table_set("natural_log_exp_and_others")
                        pipelined(act, NB, ES, [(3, evac), (1, sig), (0, exp), (3, store)], head=2)

                    @block.vector
                    def _(dve):
                        dve.tensor_scalar(bins[:, 0, :], dst_i[:, :], 127, None, ALU.bitwise_and).then_inc(binned, 1)
                        dve.tensor_scalar(bins[:, 1, :], dst_i[:, :], 7, None, ALU.logical_shift_right).then_inc(binned, 1)
                        dve.memset(two[:, :], 2.0).then_inc(binned, 3)

                        def index(n, s, r):
                            nc.vector.tensor_copy(idx[s][:, :], src_i[:, bass.ds(n * TB, TB)].bitcast(U32)).then_inc(c["idx"], 1)

                        def pre(n, s, r):
                            dve.wait_ge(landed[s], (r + 1) * 32)
                            c.free(dve, "p", n)
                            mask_tile(dve, mask[s], drow[s], n).then_inc(c["mask"], 1)
                            c.ready(dve, "pre", n)
                            wait_rows(dve, s, r, TB)
                            dve.tensor_tensor(x[s][:, :, :], as_tiles(ps_pre[s % 2]), g[s][:, :, :], ALU.add).then_inc(c["x"], 1)
                            c.ready(dve, "x", n)
                            c.free(dve, "t", n)
                            dve.tensor_scalar(u[s][:, :, :], x[s][:, :, :], 20.0, None, ALU.min).then_inc(c["clamp"], 1)

                        def square(n, s, r):
                            c.ready(dve, "expd", n)
                            c.free(dve, "m", n)
                            dve.scalar_tensor_tensor(w[s][:, :, :], u[s][:, :, :], 2.0, u[s][:, :, :], ALU.add, ALU.mult).then_inc(c["w"], 1)
                            dve.wait_ge(binned, 5)
                            c.free(dve, "cnt", n, 1)
                            dve.tensor_tensor(lo[:, :, :], iota[:, :].unsqueeze(1).broadcast_to([P, TB, P]),
                                              bins[:, 0, bass.ds(n * TB, TB)].unsqueeze(2).broadcast_to([P, TB, P]), ALU.is_equal)
                            dve.tensor_tensor(hi[:, :, :], iota_hi[:, :].unsqueeze(1).broadcast_to([P, TB, NT]),
                                              bins[:, 1, bass.ds(n * TB, TB)].unsqueeze(2).broadcast_to([P, TB, NT]), ALU.is_equal).then_inc(c["lo"], 1)

                        def message(n, s, r):
                            c.ready(dve, "sig", n)
                            dve.tensor_tensor(w[s][:, :, :], w[s][:, :, :], u[s][:, :, :], ALU.mult).then_inc(c["t"], 1)
                            c.ready(dve, "t", n)
                            dve.tensor_tensor(x[s][:, :, :], w[s][:, :, :], x[s][:, :, :], ALU.mult).then_inc(c["m"], 1)

                        def tally(n, s, r):
                            c.ready(dve, "cnt", n)
                            c.free(dve, "acc", n, 1)
                            dve.tensor_tensor(deg_in[:, :], deg_in[:, :], ps_cnt[:, 0:NT], ALU.add).then_inc(c["acc"], 1)

                        pipelined(dve, NB, ES, [(0, index), (3, square), (2, pre), (4, message), (4, tally)])
            count_rows(ES, NB, TB)

        def edges_sum(stage, table, target, count_src=False, clear=None):
            with ExitStack() as st:
                def ring(name, shape, dt=F32, slots=ES):
                    return [st.enter_context(nc.sbuf_tensor(f"{stage}_{name}{s}", shape, dt)) for s in range(slots)]

                c = Products(sem, stage, ES, "mask idx p evac lo cnt acc")
                landed = [sem(f"{stage}_landed{s}") for s in range(ES)]
                stored = [sem(f"{stage}_stored{s}") for s in range(ES)]
                binned, cleared = sem(f"{stage}_binned"), sem(f"{stage}_cleared")
                drow, g = ring("drow", [P, TB, P], I32), ring("g", [P, TB, D])
                mask, row, idx = ring("mask", [P, TB, P]), ring("row", [P, TB, D]), ring("idx", [P, TB], U32)
                lo, hi = ring("lo", [P, TB, P], BF16, 1)[0], ring("hi", [P, TB, NT], BF16, 1)[0]
                bins = ring("bins", [P, 2, ET], I32, 1)[0]
                zero = ring("zero", [P, TB * QW], F32, 1)[0]
                ps_sum = [st.enter_context(nc.psum_tensor(f"{stage}_sum{s}", [P, 1024], F32)) for s in range(2)]
                ps_cnt = st.enter_context(nc.psum_tensor(f"{stage}_cnt", [P, 512], F32))

                def as_tiles(ps):
                    return ps[:, 0:BW].rearrange("p (t f) -> p t f", f=P)

                with nc.Block() as block:
                    @block.sync
                    def _(sp):
                        c.credit(sp)
                        if clear is not None:
                            sp.wait_ge(binned, 1)

                        def load(n, s, r):
                            c.free(sp, "mask", n)
                            c.hold(sp)
                            sp.dma_start(drow[s][:, :, :].rearrange("p t e -> p (t e)"),
                                         dstflat[bass.ds(n * BW + 1, BW)].partition_broadcast(P)).then_inc(landed[s], 16)

                        def wipe(n, s, r):
                            sp.dma_start(clear[bass.ds(n * BW, BW), :].rearrange("(p t) f -> p (t f)", p=P), zero[:, :]).then_inc(cleared, 16)

                        pipelined(sp, NB, ES, [(0, load)] + ([(0, wipe)] if clear is not None else []))
                        for s in range(ES):
                            sp.wait_ge(stored[s], NB // ES * 16)
                        if clear is not None:
                            sp.wait_ge(cleared, NB * 16)

                    @block.gpsimd
                    def _(pool):
                        def gather(n, s, r):
                            c.ready(pool, "idx", n)
                            c.free(pool, "p", n)
                            c.hold(pool)
                            for t in range(TB):
                                pool.indirect_dma_start(g[s][:, t, :], None, table[:, :],
                                                        bass.IndirectOffsetOnAxis(ap=idx[s][:, t:t + 1], axis=0)).then_inc(gathered[s], 16)

                        pipelined(pool, NB, ES, [(0, gather)])

                    @block.tensor
                    def _(pe):
                        def total(n, s, r):
                            c.ready(pe, "mask", n)
                            c.free(pe, "evac", n, 2)
                            wait_rows(pe, s, r, TB)
                            for t in range(TB):
                                last = nc.tensor.matmul(as_tiles(ps_sum[s % 2])[:, t, :], mask[s][:, t, :], g[s][:, t, :], start=True, stop=True)
                            last.then_inc(c["p"], 1)

                        def count(n, s, r):
                            c.ready(pe, "lo", n)
                            c.free(pe, "acc", n, 1)
                            for t in range(TB):
                                last = nc.tensor.matmul(ps_cnt[:, 0:NT], lo[:, t, :], hi[:, t, :], start=(t == 0), stop=(t == TB - 1))
                            last.then_inc(c["cnt"], 1)

                        pipelined(pe, NB, ES, [(0, count)] * count_src + [(0, total)])

                    @block.scalar
                    def _(act):
                        def evac(n, s, r):
                            c.ready(act, "p", n)
                            if not (isinstance(r, int) and r == 0):
                                c.hold(act)
                                act.wait_ge(stored[s], r * 16)
                            nc.scalar.activation(row[s][:, :, :], as_tiles(ps_sum[s % 2]), ACT.Copy).then_inc(c["evac"], 1)
                            c.ready(act, "evac", n)
                            act.dma_start(flat_rows(target, n), row[s][:, :, :]).then_inc(stored[s], 16)

                        pipelined(act, NB, ES, [(0, evac)], head=2)

                    @block.vector
                    def _(dve):
                        if clear is not None:
                            dve.memset(zero[:, :], 0.0).then_inc(binned, 1)
                        if count_src:
                            dve.tensor_scalar(bins[:, 0, :], src_i[:, :], 127, None, ALU.bitwise_and).then_inc(binned, 1)
                            dve.tensor_scalar(bins[:, 1, :], src_i[:, :], 7, None, ALU.logical_shift_right).then_inc(binned, 1)
                            dve.wait_ge(binned, 2 + (clear is not None))

                        def index(n, s, r):
                            if isinstance(r, int) and r == 0:
                                pass
                            else:
                                wait_rows(dve, s, r - 1, TB)
                            nc.vector.tensor_copy(idx[s][:, :], src_i[:, bass.ds(n * TB, TB)].bitcast(U32)).then_inc(c["idx"], 1)

                        def masks(n, s, r):
                            dve.wait_ge(landed[s], (r + 1) * 16)
                            c.free(dve, "p", n)
                            mask_tile(dve, mask[s], drow[s], n).then_inc(c["mask"], 1)

                        def bin_src(n, s, r):
                            c.free(dve, "cnt", n, 1)
                            dve.tensor_tensor(lo[:, :, :], iota[:, :].unsqueeze(1).broadcast_to([P, TB, P]),
                                              bins[:, 0, bass.ds(n * TB, TB)].unsqueeze(2).broadcast_to([P, TB, P]), ALU.is_equal)
                            dve.tensor_tensor(hi[:, :, :], iota_hi[:, :].unsqueeze(1).broadcast_to([P, TB, NT]),
                                              bins[:, 1, bass.ds(n * TB, TB)].unsqueeze(2).broadcast_to([P, TB, NT]), ALU.is_equal).then_inc(c["lo"], 1)

                        def tally(n, s, r):
                            c.ready(dve, "cnt", n)
                            c.free(dve, "acc", n, 1)
                            dve.tensor_tensor(deg_out[:, :], deg_out[:, :], ps_cnt[:, 0:NT], ALU.add).then_inc(c["acc"], 1)

                        pipelined(dve, NB, ES, [(0, index), (1, masks)] + [(2, tally), (1, bin_src)] * count_src)
            count_rows(ES, NB, TB)

        def degrees(stage, deg, with_rows):
            with ExitStack() as st:
                def tmp(name, dt=F32):
                    return st.enter_context(nc.sbuf_tensor(f"{stage}_{name}", [P, NT], dt))

                step, summed, clipped, rooted = sem(f"{stage}_step"), sem(f"{stage}_summed"), sem(f"{stage}_clipped"), sem(f"{stage}_rooted")
                numbered = sem(f"{stage}_numbered")
                tot, incl, has, cum, row, nid, clip, rec = (tmp(k) for k in "tot incl has cum row nid clip rec".split())
                ps = st.enter_context(nc.psum_tensor(f"{stage}_ps", [P, 512], F32))
                with nc.Block() as block:
                    @block.tensor
                    def _(pe):
                        if with_rows:
                            nc.tensor.matmul(ps[:, 0:NT], tri[:, :], deg[:, :], start=True, stop=True)
                            nc.tensor.matmul(ps[:, 64:64 + NT], ones[:, :], deg[:, :], start=True, stop=True).then_inc(summed, 1)

                    @block.gpsimd
                    def _(pool):
                        pool.iota(nid[:, :], [[P, NT]], base=EP, channel_multiplier=1,
                                  allow_small_or_imprecise_dtypes=True).then_inc(numbered, 1)

                    @block.scalar
                    def _(act):
                        act.wait_ge(clipped, 1)
                        nc.scalar.activation((rs_in if with_rows else rs_out)[:, :], (r_in if with_rows else rec)[:, :], ACT.Sqrt).then_inc(rooted, 1)

                    @block.vector
                    def _(dve):
                        n = [0]

                        def after(ins):
                            n[0] += 1
                            ins.then_inc(step, 1)
                            dve.wait_ge(step, n[0])

                        after(dve.tensor_scalar(clip[:, :], deg[:, :], 1.0, None, ALU.max))
                        dve.reciprocal((r_in if with_rows else rec)[:, :], clip[:, :]).then_inc(clipped, 1)
                        if with_rows:
                            dve.wait_ge(summed, 1)
                            after(dve.tensor_copy(tot[:, :], ps[:, 64:64 + NT]))
                            after(dve.tensor_tensor_scan(incl[:, :], ones[:, 0:NT], tot[:, :], 0.0, ALU.mult, ALU.add))
                            after(dve.tensor_tensor(incl[:, :], incl[:, :], tot[:, :], ALU.subtract))
                            after(dve.tensor_tensor(cum[:, :], incl[:, :], ps[:, 0:NT], ALU.add))
                            after(dve.tensor_scalar(has[:, :], deg[:, :], 0.0, None, ALU.is_gt))
                            after(dve.scalar_tensor_tensor(row[:, :], cum[:, :], -1.0 - EP, has[:, :], ALU.add, ALU.mult))
                            dve.tensor_scalar(end_row[:, :], row[:, :], float(EP), None, ALU.add)
                            dve.wait_ge(numbered, 1)
                            after(dve.tensor_tensor(cum[:, :], cum[:, :], deg[:, :], ALU.subtract))
                            after(dve.tensor_tensor(cum[:, :], cum[:, :], nid[:, :], ALU.subtract))
                            after(dve.tensor_tensor(cum[:, :], cum[:, :], has[:, :], ALU.mult))
                            dve.tensor_tensor(start_row[:, :], cum[:, :], nid[:, :], ALU.add)

        def tails(table, width):
            return table[0:EP, :].rearrange("(k p e) f -> p k e f", e=P, p=TP)[:, :, P - 1, 0:width]

        def pick(dve, z, n):
            return dve.tensor_tensor(z[:, :, :], iota[0:TP, :].unsqueeze(1).broadcast_to([TP, TK, P]),
                                     key_rel[:, bass.ds(n, 1), :].rearrange("p j k -> p (j k)").unsqueeze(2).broadcast_to([TP, TK, P]),
                                     ALU.is_equal)

        def col(buf, n):
            return buf[:, bass.ds(n, 1)]

        def tile_of(buf, n):
            return buf[:, bass.ds(n, 1), :].rearrange("p j f -> p (j f)")

        def nodes_layer0():
            with ExitStack() as st:
                def ring(name, shape, dt=F32, slots=NS):
                    return [st.enter_context(nc.sbuf_tensor(f"n0_{name}{s}", shape, dt)) for s in range(slots)]

                c = Products(sem, "n0", NS, "idx z h agg ht mm1 hid mm2 res stat var std rstd norm")
                tails_in, stored = sem("n0_tails"), sem("n0_stored")
                tail = ring("tail", [TP, TK, D], slots=1)[0]
                idx, g, z = ring("idx", [P, 1], U32), ring("g", [P, D]), ring("z", [TP, TK, P])
                hT, hid, res = ring("hT", [P, P]), ring("hid", [P, 4, P]), ring("res", [P, D])
                stat, mv, std = ring("stat", [P, 6]), ring("mv", [P, 2]), ring("std", [P, 2])
                ps = [st.enter_context(nc.psum_tensor(f"n0_ps{s}", [P, 512], F32)) for s in range(3)]
                with nc.Block() as block:
                    @block.sync
                    def _(sp):
                        c.credit(sp)
                        sp.dma_start(tail[:, :, :], tails(sums[0], D)).then_inc(tails_in, 16)

                        def store(n, s, r):
                            c.ready(sp, "norm", n)
                            c.hold(sp)
                            sp.dma_start(tab[1][bass.ds(n * P, P), :], tile_of(x_now, n)).then_inc(stored, 16)

                        pipelined(sp, NT, NS, [(0, store)])
                        sp.wait_ge(stored, 16 * NT)

                    @block.gpsimd
                    def _(pool):
                        def gather(n, s, r):
                            c.ready(pool, "idx", n)
                            c.free(pool, "agg", n)
                            c.hold(pool)
                            pool.indirect_dma_start(g[s][:, :], None, sums[0][:, :],
                                                    bass.IndirectOffsetOnAxis(ap=idx[s][:, :], axis=0)).then_inc(gathered[s], 16)

                        pipelined(pool, NT, NS, [(0, gather)])

                    @block.tensor
                    def _(pe):
                        pe.wait_ge(tails_in, 16)

                        def agg(n, s, r):
                            c.ready(pe, "z", n)
                            c.ready(pe, "h", n)
                            c.free(pe, "ht", n, 1)
                            nc.tensor.matmul(ps[0][:, 0:P], g[s][:, :], ident[:, :], start=True, stop=False)
                            for k in range(TK):
                                last = nc.tensor.matmul(ps[0][:, 0:P], tail[:, k, :], z[s][:, k, :], start=False, stop=(k == TK - 1))
                            last.then_inc(c["agg"], 1)

                        def up(n, s, r):
                            c.ready(pe, "ht", n)
                            c.free(pe, "hid", n, 1)
                            for k in range(4):
                                last = nc.tensor.matmul(ps[1][:, k * P:(k + 1) * P], wm[:, W_1 + k, :], hT[s][:, :], start=True, stop=True)
                            last.then_inc(c["mm1"], 1)

                        def down(n, s, r):
                            c.ready(pe, "hid", n)
                            c.free(pe, "res", n, 1)
                            nc.tensor.matmul(ps[2][:, 0:D], ones[0:1, :], wr[:, R_B2, :], start=True, stop=False)
                            for k in range(4):
                                last = nc.tensor.matmul(ps[2][:, 0:D], hid[s][:, k, :], wm[:, W_2 + k, :], start=False, stop=(k == 3))
                            last.then_inc(c["mm2"], 1)

                        pipelined(pe, NT, NS, [(0, agg), (1, up), (2, down)])

                    @block.scalar
                    def _(act):
                        def move(n, s, r):
                            c.ready(act, "agg", n)
                            c.free(act, "mm1", n)
                            nc.scalar.activation(hT[s][:, :], ps[0][:, 0:P], ACT.Copy).then_inc(c["ht"], 1)

                        def root(n, s, r):
                            c.ready(act, "var", n)
                            c.free(act, "rstd", n)
                            nc.scalar.activation(std[s][:, 0:1], mv[s][:, 1:2], ACT.Sqrt, bias=eps5[:, :]).then_inc(c["std"], 1)

                        def relu(n, s, r):
                            c.ready(act, "mm1", n)
                            c.free(act, "mm2", n)
                            for k in range(4):
                                last = nc.scalar.activation(hid[s][:, k, :], ps[1][:, k * P:(k + 1) * P], ACT.Relu, bias=c1[:, k:k + 1])
                            last.then_inc(c["hid"], 1)

                        pipelined(act, NT, NS, [(4, root), (0, move), (1, relu)])

                    @block.vector
                    def _(dve):
                        def index(n, s, r):
                            c.free(dve, "h", n)
                            nc.vector.tensor_copy(idx[s][:, :], col(end_row, n)).then_inc(c["idx"], 1)
                            c.free(dve, "agg", n)
                            pick(dve, z[s], n).then_inc(c["z"], 1)

                        def own(n, s, r):
                            wait_rows(dve, s, r)
                            dve.scalar_tensor_tensor(g[s][:, :], tile_of(x_now, n), one_eps[:, :], g[s][:, :], ALU.mult, ALU.add).then_inc(c["h"], 1)

                        def residual(n, s, r):
                            c.ready(dve, "mm2", n)
                            c.free(dve, "norm", n)
                            dve.tensor_tensor(res[s][:, :], ps[2][:, 0:D], tile_of(x_now, n), ALU.add).then_inc(c["res"], 1)
                            c.ready(dve, "res", n)
                            dve.bn_stats(stat[s][:, :], res[s][:, :]).then_inc(c["stat"], 1)
                            c.ready(dve, "stat", n)
                            c.hold(dve)
                            dve.bn_aggr(mv[s][:, :], stat[s][:, :]).then_inc(c["var"], 1)

                        def norm(n, s, r):
                            c.ready(dve, "std", n)
                            dve.reciprocal(std[s][:, 1:2], std[s][:, 0:1]).then_inc(c["rstd"], 1)
                            c.ready(dve, "rstd", n)
                            dve.tensor_scalar(tile_of(x_now, n), res[s][:, :], mv[s][:, 0:1], std[s][:, 1:2], ALU.subtract, ALU.mult).then_inc(c["norm"], 1)

                        pipelined(dve, NT, NS, [(0, index), (1, own), (5, norm), (4, residual)])
            count_rows(NS, NT)

        def nodes_sage(stage, table, target, x_in, w_self, w_neigh, bias, final):
            with ExitStack() as st:
                def ring(name, shape, dt=F32, slots=NS):
                    return [st.enter_context(nc.sbuf_tensor(f"{stage}_{name}{s}", shape, dt)) for s in range(slots)]

                c = Products(sem, stage, NS, "idx z xs dg zt a tr at mm h sq root inv res stat var std rstd norm scaled scl_free")
                late = 1 if final else 2
                tails_in, stored = sem(f"{stage}_tails"), [sem(f"{stage}_stored{s}") for s in range(NS)]
                tail = ring("tail", [TP, TK, D], slots=1)[0]
                idx, g, z = ring("idx", [P, 1], U32), ring("g", [P, D]), ring("z", [TP, TK, P])
                xs, dg, aT = ring("xs", [P, D]), ring("dg", [P, P]), ring("aT", [P, 2, P])
                h, res, sq = ring("h", [P, D]), ring("res", [P, D]), ring("sq", [P, D])
                stat, mv, std, nrm = ring("stat", [P, 6]), ring("mv", [P, 2]), ring("std", [P, 2]), ring("nrm", [P, 3])
                scl = ring("scl", [P, D])
                ps_z = [st.enter_context(nc.psum_tensor(f"{stage}_psz{s}", [P, 512], F32)) for s in range(NS)]
                ps_t, ps_h = (st.enter_context(nc.psum_tensor(f"{stage}_ps{k}", [P, 512], F32)) for k in "th")
                with nc.Block() as block:
                    @block.sync
                    def _(sp):
                        c.credit(sp)
                        sp.dma_start(tail[:, :, :], tails(table, D)).then_inc(tails_in, 16)

                        def store(n, s, r):
                            c.ready(sp, "scaled" if final else "h", n)
                            c.hold(sp)
                            sp.dma_start(target[bass.ds(n * P, P), :], scl[s][:, :] if final else tile_of(h_now, n)).then_inc(stored[s], 16)

                        def retire(n, s, r):
                            sp.wait_ge(stored[s], (r + 1) * 16)
                            sp.sem_inc(c["scl_free"], 1)

                        pipelined(sp, NT, NS, [(0, store), (1, retire)])

                    @block.gpsimd
                    def _(pool):
                        def gather(n, s, r):
                            c.ready(pool, "idx", n)
                            c.free(pool, "tr", n)
                            c.hold(pool)
                            pool.indirect_dma_start(g[s][:, :], None, table[:, :],
                                                    bass.IndirectOffsetOnAxis(ap=idx[s][:, :], axis=0)).then_inc(gathered[s], 16)

                        pipelined(pool, NT, NS, [(0, gather)])

                    @block.tensor
                    def _(pe):
                        pe.wait_ge(tails_in, 16)

                        def earlier(n, s, r):
                            c.ready(pe, "z", n)
                            c.free(pe, "a", n)
                            for k in range(TK):
                                last = nc.tensor.matmul(ps_z[s][:, 0:D], z[s][:, k, :], tail[:, k, :], start=(k == 0), stop=(k == TK - 1))
                            last.then_inc(c["zt"], 1)

                        def turn(n, s, r):
                            c.ready(pe, "a", n)
                            c.ready(pe, "dg", n)
                            c.ready(pe, "xs", n)
                            c.free(pe, "at", n, 1)
                            nc.tensor.matmul(ps_t[:, 0:P], g[s][:, :], dg[s][:, :], start=True, stop=True)
                            c.hold(pe)
                            nc.tensor.transpose(ps_t[:, P:2 * P], xs[s][:, :], ident[:, :]).then_inc(c["tr"], 1)

                        def product(n, s, r):
                            c.ready(pe, "at", n)
                            c.free(pe, "h", n, 1)
                            nc.tensor.matmul(ps_h[:, 0:D], ones[0:1, :], wr[:, bias, :], start=True, stop=False)
                            nc.tensor.matmul(ps_h[:, 0:D], aT[s][:, 0, :], wm[:, w_neigh, :], start=False, stop=False)
                            nc.tensor.matmul(ps_h[:, 0:D], aT[s][:, 1, :], wm[:, w_self, :], start=False, stop=True).then_inc(c["mm"], 1)

                        pipelined(pe, NT, NS, [(0, earlier), (late, turn), (1 + late, product)])

                    @block.scalar
                    def _(act):
                        def own(n, s, r):
                            c.free(act, "tr", n)
                            nc.scalar.activation(xs[s][:, :], tile_of(x_in, n), ACT.Copy).then_inc(c["xs"], 1)
                            nc.scalar.activation(dg[s][:, :], ident[:, :], ACT.Copy, scale=col(r_in, n)).then_inc(c["dg"], 1)

                        def move(n, s, r):
                            c.ready(act, "tr", n)
                            c.free(act, "mm", n)
                            nc.scalar.activation(aT[s][:, :, :], ps_t[:, 0:2 * P].rearrange("p (a m) -> p a m", a=2), ACT.Copy).then_inc(c["at"], 1)

                        def relu(n, s, r):
                            c.ready(act, "mm", n)
                            if final:
                                c.free(act, "res", n)
                            nc.scalar.activation(h[s][:, :] if final else tile_of(h_now, n), ps_h[:, 0:D], ACT.Relu).then_inc(c["h"], 1)

                        def square(n, s, r):
                            c.ready(act, "h", n)
                            c.free(act, "root", n)
                            nc.scalar.activation(sq[s][:, :], h[s][:, :], ACT.Square, accum_out=nrm[s][:, 0:1]).then_inc(c["sq"], 1)

                        def length(n, s, r):
                            c.ready(act, "sq", n)
                            c.free(act, "inv", n)
                            nc.scalar.activation(nrm[s][:, 1:2], nrm[s][:, 0:1], ACT.Sqrt).then_inc(c["root"], 1)

                        def root(n, s, r):
                            c.ready(act, "var", n)
                            c.free(act, "rstd", n)
                            nc.scalar.activation(std[s][:, 0:1], mv[s][:, 1:2], ACT.Sqrt, bias=eps5[:, :]).then_inc(c["std"], 1)

                        def scale(n, s, r):
                            c.ready(act, "norm", n)
                            c.free(act, "scl_free", n)
                            nc.scalar.activation(scl[s][:, :], tile_of(x_now, n), ACT.Copy, scale=col(rs_out, n)).then_inc(c["scaled"], 1)

                        tail_end = [(5, root), (4, length), (3, square)] if final else []
                        pipelined(act, NT, NS, tail_end + [(0, own), (1, move), (2, relu)] + [(5, scale)] * final)

                    @block.vector
                    def _(dve):
                        def index(n, s, r):
                            c.free(dve, "a", n)
                            nc.vector.tensor_copy(idx[s][:, :], col(end_row, n)).then_inc(c["idx"], 1)
                            c.free(dve, "zt", n)
                            pick(dve, z[s], n).then_inc(c["z"], 1)

                        def whole(n, s, r):
                            c.ready(dve, "zt", n)
                            wait_rows(dve, s, r)
                            dve.tensor_tensor(g[s][:, :], ps_z[s][:, 0:D], g[s][:, :], ALU.add).then_inc(c["a"], 1)

                        def residual(n, s, r):
                            c.ready(dve, "root", n)
                            dve.tensor_scalar(nrm[s][:, 2:3], nrm[s][:, 1:2], 1e-12, None, ALU.max).then_inc(c["stat"], 1)
                            dve.wait_ge(c["stat"], n * 2 + (1 + NS))
                            dve.reciprocal(nrm[s][:, 1:2], nrm[s][:, 2:3]).then_inc(c["inv"], 1)
                            c.ready(dve, "inv", n)
                            c.free(dve, "norm", n)
                            dve.scalar_tensor_tensor(res[s][:, :], h[s][:, :], nrm[s][:, 1:2], tile_of(x_now, n), ALU.mult, ALU.add).then_inc(c["res"], 1)
                            c.ready(dve, "res", n)
                            dve.bn_stats(stat[s][:, :], res[s][:, :]).then_inc(c["stat"], 1)
                            dve.wait_ge(c["stat"], n * 2 + (2 + NS))
                            c.hold(dve)
                            dve.bn_aggr(mv[s][:, :], stat[s][:, :]).then_inc(c["var"], 1)

                        def norm(n, s, r):
                            c.ready(dve, "std", n)
                            dve.reciprocal(std[s][:, 1:2], std[s][:, 0:1]).then_inc(c["rstd"], 1)
                            c.ready(dve, "rstd", n)
                            dve.tensor_scalar(tile_of(x_now, n), res[s][:, :], mv[s][:, 0:1], std[s][:, 1:2], ALU.subtract, ALU.mult).then_inc(c["norm"], 1)

                        pipelined(dve, NT, NS, [(0, index), (late, whole)] + ([(5, norm), (4, residual)] if final else []))
            count_rows(NS, NT)

        def nodes_gcn():
            with ExitStack() as st:
                def ring(name, shape, dt=F32, slots=NS):
                    return [st.enter_context(nc.sbuf_tensor(f"n2_{name}{s}", shape, dt)) for s in range(slots)]

                c = Products(sem, "n2", NS, "idx z zt a tr at mm h")
                tails_in = sem("n2_tails")
                tail = ring("tail", [TP, TK, D], slots=1)[0]
                idx, g, z, aT = ring("idx", [P, 1], U32), ring("g", [P, D]), ring("z", [TP, TK, P]), ring("aT", [P, P])
                ps_z = [st.enter_context(nc.psum_tensor(f"n2_psz{s}", [P, 512], F32)) for s in range(NS)]
                ps_t, ps_h = (st.enter_context(nc.psum_tensor(f"n2_ps{k}", [P, 512], F32)) for k in "th")
                with nc.Block() as block:
                    @block.sync
                    def _(sp):
                        c.credit(sp)
                        sp.dma_start(tail[:, :, :], tails(sums[3], D)).then_inc(tails_in, 16)

                    @block.gpsimd
                    def _(pool):
                        def gather(n, s, r):
                            c.ready(pool, "idx", n)
                            c.free(pool, "tr", n)
                            c.hold(pool)
                            pool.indirect_dma_start(g[s][:, :], None, sums[3][:, :],
                                                    bass.IndirectOffsetOnAxis(ap=idx[s][:, :], axis=0)).then_inc(gathered[s], 16)

                        pipelined(pool, NT, NS, [(0, gather)])

                    @block.tensor
                    def _(pe):
                        pe.wait_ge(tails_in, 16)

                        def earlier(n, s, r):
                            c.ready(pe, "z", n)
                            c.free(pe, "a", n)
                            for k in range(TK):
                                last = nc.tensor.matmul(ps_z[s][:, 0:D], z[s][:, k, :], tail[:, k, :], start=(k == 0), stop=(k == TK - 1))
                            last.then_inc(c["zt"], 1)

                        def turn(n, s, r):
                            c.ready(pe, "a", n)
                            c.free(pe, "at", n, 1)
                            c.hold(pe)
                            nc.tensor.transpose(ps_t[:, 0:P], g[s][:, :], ident[:, :]).then_inc(c["tr"], 1)

                        def product(n, s, r):
                            c.ready(pe, "at", n)
                            c.free(pe, "h", n, 1)
                            nc.tensor.matmul(ps_h[:, 0:D], aT[s][:, :], wm[:, W_L2, :], start=True, stop=True).then_inc(c["mm"], 1)

                        pipelined(pe, NT, NS, [(0, earlier), (2, turn), (3, product)])

                    @block.scalar
                    def _(act):
                        def move(n, s, r):
                            c.ready(act, "tr", n)
                            c.free(act, "mm", n)
                            nc.scalar.activation(aT[s][:, :], ps_t[:, 0:P], ACT.Copy).then_inc(c["at"], 1)

                        pipelined(act, NT, NS, [(0, move)])

                    @block.vector
                    def _(dve):
                        def index(n, s, r):
                            c.free(dve, "a", n)
                            nc.vector.tensor_copy(idx[s][:, :], col(end_row, n)).then_inc(c["idx"], 1)
                            c.free(dve, "zt", n)
                            pick(dve, z[s], n).then_inc(c["z"], 1)

                        def whole(n, s, r):
                            c.ready(dve, "zt", n)
                            wait_rows(dve, s, r)
                            dve.tensor_tensor(g[s][:, :], ps_z[s][:, 0:D], g[s][:, :], ALU.add).then_inc(c["a"], 1)

                        def scale(n, s, r):
                            c.ready(dve, "mm", n)
                            dve.tensor_scalar(tile_of(h_now, n), ps_h[:, 0:D], col(rs_in, n), None, ALU.mult).then_inc(c["h"], 1)

                        pipelined(dve, NT, NS, [(0, index), (2, whole), (4, scale)])
            count_rows(NS, NT)

        def cols(a):
            return a.broadcast_to([P, NT, D])

        class Steps:

            def __init__(self, stage):
                self.sem = {e: sem(f"{stage}_{e}_done") for e in ("dve", "act", "pe", "pool", "dma")}

        MINE = NT * 3 // 4

        class RowNorm:

            HALF = NT // 2

            def __init__(self, st, stage, a):
                self.a = a
                self.stat = st.enter_context(nc.sbuf_tensor(f"{stage}_stat", [P, NT, 6], F32))
                self.mv = st.enter_context(nc.sbuf_tensor(f"{stage}_mv", [P, NT, 2], F32))
                self.small = st.enter_context(nc.sbuf_tensor(f"{stage}_small", [P, 3, NT], F32))
                self.counted, self.varied, self.rooted, self.inverted, self.shifted, self.first_done, self.others_done = (
                    sem(f"{stage}_{k}") for k in "counted varied rooted inverted shifted first others".split())

            def stats(self, dve):
                for j in range(NT):
                    last = dve.bn_stats(self.stat[:, j, :], self.a[:, j, :])
                last.then_inc(self.counted, 1)
                dve.wait_ge(self.counted, 1)
                self.aggregate(dve)

            def aggregate(self, dve):
                for j in range(NT):
                    last = dve.bn_aggr(self.mv[:, j, :], self.stat[:, j, :])
                last.then_inc(self.varied, 1)

            def root(self, act, turn):
                act.wait_ge(self.varied, turn)
                nc.scalar.activation(self.small[:, 2, :], self.mv[:, :, 1], ACT.Sqrt, bias=eps5[:, :]).then_inc(self.rooted, 1)
                act.wait_ge(self.shifted, turn)
                for j in range(self.HALF, NT):
                    last = nc.scalar.activation(self.a[:, j, :], self.a[:, j, :], ACT.Identity,
                                                bias=self.small[:, 1, j:j + 1], scale=self.small[:, 0, j:j + 1])
                last.then_inc(self.others_done, 1)

            def apply(self, dve, turn):
                dve.wait_ge(self.rooted, turn)
                dve.reciprocal(self.small[:, 0, :], self.small[:, 2, :]).then_inc(self.inverted, 1)
                dve.wait_ge(self.inverted, turn)
                dve.scalar_tensor_tensor(self.small[:, 1, :], self.mv[:, :, 0], -1.0, self.small[:, 0, :], ALU.mult, ALU.mult).then_inc(self.shifted, 1)
                for j in range(self.HALF):
                    last = dve.tensor_scalar(self.a[:, j, :], self.a[:, j, :], self.mv[:, j, 0:1], self.small[:, 0, j:j + 1], ALU.subtract, ALU.mult)
                last.then_inc(self.first_done, 1)

        def batch_norm():
            with ExitStack() as st:
                k = Steps("bn")
                norm = RowNorm(st, "bn_rows", x_now)
                sq = st.enter_context(nc.sbuf_tensor("bn_sq", [P, NT, D], F32))
                small = st.enter_context(nc.sbuf_tensor("bn_small", [P, 3, NT], F32))
                f = st.enter_context(nc.sbuf_tensor("bn_f", [P, 5, D], F32))
                ps = st.enter_context(nc.psum_tensor("bn_ps", [P, 512], F32))
                dv, ac, pe_s, po = k.sem["dve"], k.sem["act"], k.sem["pe"], k.sem["pool"]

                def part(a, lo, hi):
                    return a[:, lo:hi, :]

                def some(a, lo, hi):
                    return a.broadcast_to([P, hi - lo, D])

                def rows_of(a, lo, hi):
                    return a[:, lo:hi].unsqueeze(2).broadcast_to([P, hi - lo, D])

                with nc.Block() as block:
                    @block.tensor
                    def _(pe):
                        pe.wait_ge(dv, 1)
                        nc.tensor.matmul(ps[:, 0:D], ones[:, :], f[:, 0, :], start=True, stop=True).then_inc(pe_s, 1)
                        pe.wait_ge(dv, 5)
                        nc.tensor.matmul(ps[:, 0:D], ones[:, :], f[:, 0, :], start=True, stop=True).then_inc(pe_s, 1)

                    @block.gpsimd
                    def _(pool):
                        lo, hi = MINE, NT
                        pool.wait_ge(dv, 2)
                        pool.tensor_tensor(part(h_now, lo, hi), part(h_now, lo, hi), some(f[:, 1:2, :], lo, hi), ALU.subtract).then_inc(po, 1)
                        pool.wait_ge(ac, 1)
                        pool.wait_ge(dv, 7)
                        pool.tensor_tensor(part(h_now, lo, hi), part(h_now, lo, hi), some(f[:, 4:5, :], lo, hi), ALU.mult).then_inc(po, 1)
                        pool.wait_ge(po, 2)
                        pool.tensor_tensor(part(h_now, lo, hi), part(h_now, lo, hi), some(bc[:, B_B2:B_B2 + 1, :], lo, hi), ALU.add).then_inc(po, 1)
                        pool.wait_ge(dv, 12)
                        pool.tensor_tensor(part(h_now, lo, hi), part(h_now, lo, hi), rows_of(small[:, 0, :], lo, hi), ALU.mult).then_inc(po, 1)
                        pool.wait_ge(po, 4)
                        pool.tensor_tensor(part(x_now, lo, hi), part(h_now, lo, hi), part(x_now, lo, hi), ALU.add).then_inc(po, 1)

                    @block.scalar
                    def _(act):
                        act.wait_ge(dv, 3)
                        act.wait_ge(po, 1)
                        nc.scalar.activation(sq[:, :, :], h_now[:, :, :], ACT.Square).then_inc(ac, 1)
                        act.wait_ge(pe_s, 2)
                        nc.scalar.activation(f[:, 2, :], ps[:, 0:D], ACT.Sqrt, bias=eps5[:, :], scale=1.0 / N).then_inc(ac, 1)
                        act.wait_ge(dv, 9)
                        act.wait_ge(po, 3)
                        nc.scalar.activation(h_now[:, :, :], h_now[:, :, :], ACT.Relu).then_inc(ac, 1)
                        act.wait_ge(ac, 3)
                        nc.scalar.activation(sq[:, :, :], h_now[:, :, :], ACT.Square).then_inc(ac, 1)
                        act.wait_ge(dv, 10)
                        nc.scalar.activation(small[:, 1, :], small[:, 0, :], ACT.Sqrt).then_inc(ac, 1)
                        norm.root(act, 1)

                    @block.vector
                    def _(dve):
                        dve.tensor_reduce(f[:, 0, :], h_now[:, :, :].rearrange("p j f -> p f j"), AX.X, ALU.add).then_inc(dv, 1)
                        dve.wait_ge(pe_s, 1)
                        dve.tensor_scalar(f[:, 1, :], ps[:, 0:D], 1.0 / N, None, ALU.mult).then_inc(dv, 1)
                        dve.wait_ge(dv, 2)
                        dve.tensor_tensor(part(h_now, 0, MINE), part(h_now, 0, MINE), some(f[:, 1:2, :], 0, MINE), ALU.subtract).then_inc(dv, 1)
                        dve.wait_ge(ac, 1)
                        dve.tensor_scalar(sq[:, NT - 1, :], sq[:, NT - 1, :], rowmask[:, NT - 1:NT], None, ALU.mult).then_inc(dv, 1)
                        dve.wait_ge(dv, 4)
                        dve.tensor_reduce(f[:, 0, :], sq[:, :, :].rearrange("p j f -> p f j"), AX.X, ALU.add).then_inc(dv, 1)
                        dve.wait_ge(ac, 2)
                        dve.reciprocal(f[:, 3, :], f[:, 2, :]).then_inc(dv, 1)
                        dve.wait_ge(dv, 6)
                        dve.tensor_tensor(f[:, 4, :], f[:, 3, :], bc[:, B_G2, :], ALU.mult).then_inc(dv, 1)
                        dve.wait_ge(dv, 7)
                        dve.tensor_tensor(part(h_now, 0, MINE), part(h_now, 0, MINE), some(f[:, 4:5, :], 0, MINE), ALU.mult).then_inc(dv, 1)
                        dve.wait_ge(dv, 8)
                        dve.tensor_tensor(part(h_now, 0, MINE), part(h_now, 0, MINE), some(bc[:, B_B2:B_B2 + 1, :], 0, MINE), ALU.add).then_inc(dv, 1)
                        dve.wait_ge(ac, 4)
                        dve.tensor_reduce(small[:, 0, :], sq[:, :, :], AX.X, ALU.add).then_inc(dv, 1)
                        dve.wait_ge(ac, 5)
                        dve.tensor_scalar(small[:, 2, :], small[:, 1, :], 1e-12, None, ALU.max).then_inc(dv, 1)
                        dve.wait_ge(dv, 11)
                        dve.reciprocal(small[:, 0, :], small[:, 2, :]).then_inc(dv, 1)
                        dve.wait_ge(dv, 12)
                        dve.tensor_tensor(part(h_now, 0, MINE), part(h_now, 0, MINE), rows_of(small[:, 0, :], 0, MINE), ALU.mult).then_inc(dv, 1)
                        dve.wait_ge(dv, 13)
                        dve.tensor_tensor(part(x_now, 0, MINE), part(h_now, 0, MINE), part(x_now, 0, MINE), ALU.add).then_inc(dv, 1)
                        dve.wait_ge(dv, 14)
                        dve.wait_ge(po, 5)
                        norm.stats(dve)
                        norm.apply(dve, 1)

        def project():
            with ExitStack() as st:
                def ring(name, shape, dt=F32, slots=NS):
                    return [st.enter_context(nc.sbuf_tensor(f"n3_{name}{s}", shape, dt)) for s in range(slots)]

                c = Products(sem, "n3", NS, "idx xs tr at mm q kv skip qe qw rows_free")
                stored = [sem(f"n3_stored{s}") for s in range(NS)]
                first_in, first_u, first_out = sem("n3_first_in"), sem("n3_first_u"), sem("n3_first_out")
                idx, xs, xT = ring("idx", [P, 1], U32), ring("xs", [P, D]), ring("xT", [P, P])
                q, kv, prod = ring("q", [P, QW]), ring("kv", [P, 2 * D]), ring("prod", [P, D])
                firsts = ring("first", [TP, TK], I32, 1)[0]
                firstu = ring("firstu", [TP, TK], U32, 1)[0]
                qfirst = ring("qfirst", [TP, TK, QW], F32, 1)[0]
                bq = ring("bq", [P, D], F32, 1)[0]
                biased = sem("n3_biased")
                ps_t = st.enter_context(nc.psum_tensor("n3_pst", [P, 512], F32))
                ps = [st.enter_context(nc.psum_tensor(f"n3_ps{s}", [P, 512], F32)) for s in range(NS)]
                with nc.Block() as block:
                    @block.sync
                    def _(sp):
                        c.credit(sp)
                        with nc.allow_non_contiguous_dma(reason="five numbers per edge tile"):
                            sp.dma_start(firsts[:, :], headtail[:, :, 4]).then_inc(first_in, 16)

                        def store(n, s, r):
                            c.ready(sp, "kv", n)
                            c.hold(sp)
                            sp.dma_start(kv_table[bass.ds(n * P, P), :], kv[s][:, :]).then_inc(stored[s], 16)
                            c.ready(sp, "qw", n)
                            c.hold(sp)
                            sp.dma_start(q_table[bass.ds(n * P, P), :], q[s][:, :]).then_inc(stored[s], 16)

                        def retire(n, s, r):
                            sp.wait_ge(stored[s], (r + 1) * 32)
                            c.hold(sp)
                            wait_rows(sp, s, r)
                            sp.sem_inc(c["rows_free"], 1)

                        pipelined(sp, NT, NS, [(0, store), (3, retire)])
                        sp.wait_ge(picked, 16 * TK)
                        sp.dma_start(q_starts[0:EP, :].rearrange("(k p e) f -> p k e f", e=P, p=TP)[:, :, 0, :],
                                     qfirst[:, :, :]).then_inc(first_out, 16)
                        sp.wait_ge(first_out, 16)

                    @block.gpsimd
                    def _(pool):
                        def scatter(n, s, r):
                            c.ready(pool, "idx", n)
                            c.ready(pool, "qw", n)
                            c.hold(pool)
                            pool.indirect_dma_start(q_starts[:, :], bass.IndirectOffsetOnAxis(ap=idx[s][:, :], axis=0),
                                                    q[s][:, :], None).then_inc(gathered[s], 16)

                        pipelined(pool, NT, NS, [(0, scatter)])
                        pool.wait_ge(c["rows_free"], NT + NS)
                        pool.wait_ge(first_u, 1)
                        for k in range(TK):
                            pool.indirect_dma_start(qfirst[:, k, :], None, q_table[:, :],
                                                    bass.IndirectOffsetOnAxis(ap=firstu[:, k:k + 1], axis=0)).then_inc(picked, 16)

                    @block.tensor
                    def _(pe):
                        def turn(n, s, r):
                            c.ready(pe, "xs", n)
                            c.free(pe, "at", n, 1)
                            c.hold(pe)
                            nc.tensor.transpose(ps_t[:, 0:P], xs[s][:, :], ident[:, :]).then_inc(c["tr"], 1)

                        def product(n, s, r):
                            c.ready(pe, "at", n)
                            c.free(pe, "skip", n)
                            nc.tensor.matmul(ps[s][:, :], xT[s][:, :], wm[:, W_Q:W_Q + 4, :].rearrange("p a f -> p (a f)"), start=True, stop=True).then_inc(c["mm"], 1)

                        pipelined(pe, NT, NS, [(0, turn), (1, product)])

                    @block.scalar
                    def _(act):
                        def own(n, s, r):
                            c.free(act, "tr", n)
                            nc.scalar.activation(xs[s][:, :], tile_of(x_now, n), ACT.Copy).then_inc(c["xs"], 1)

                        def move(n, s, r):
                            c.ready(act, "tr", n)
                            c.free(act, "mm", n)
                            nc.scalar.activation(xT[s][:, :], ps_t[:, 0:P], ACT.Copy).then_inc(c["at"], 1)

                        pipelined(act, NT, NS, [(0, own), (1, move)])

                    @block.vector
                    def _(dve):
                        dve.wait_ge(first_in, 16)
                        dve.tensor_scalar(firstu[:, :], firsts[:, :], float(NP - 1), None, ALU.min).then_inc(first_u, 1)

                        dve.tensor_scalar(bq[:, :], bc[:, B_Q, :], 0.25, None, ALU.mult).then_inc(biased, 1)
                        dve.wait_ge(biased, 1)

                        def split(n, s, r):
                            c.ready(dve, "mm", n)
                            c.free(dve, "rows_free", n)
                            dve.scalar_tensor_tensor(q[s][:, 0:D], ps[s][:, 0:D], 0.25, bq[:, :], ALU.mult, ALU.add).then_inc(c["q"], 1)
                            dve.tensor_tensor(kv[s][:, :], ps[s][:, D:3 * D], bc[:, B_Q + 1:B_Q + 3, :].rearrange("p a f -> p (a f)"), ALU.add).then_inc(c["kv"], 1)
                            dve.tensor_tensor(tile_of(h_now, n), ps[s][:, 3 * D:4 * D], bc[:, B_Q + 3, :], ALU.add).then_inc(c["skip"], 1)

                        def with_edges(n, s, r):
                            c.ready(dve, "q", n)
                            dve.tensor_tensor(prod[s][:, :], q[s][:, 0:D], bc[:, B_WE, :], ALU.mult).then_inc(c["qe"], 1)
                            c.ready(dve, "qe", n)
                            dve.tensor_reduce(q[s][:, D:QW], prod[s][:, :].rearrange("p (h d) -> p h d", d=HD), AX.X, ALU.add).then_inc(c["qw"], 1)

                        def index(n, s, r):
                            if not (isinstance(r, int) and r == 0):
                                wait_rows(dve, s, r - 1)
                            nc.vector.tensor_copy(idx[s][:, :], col(start_row, n)).then_inc(c["idx"], 1)

                        pipelined(dve, NT, NS, [(0, index), (2, split), (2, with_edges)])
            count_rows(NS, NT)

        def edges_attention():
            with ExitStack() as st:
                def ring(name, shape, dt=F32, slots=ES):
                    bufs = [st.enter_context(nc.sbuf_tensor(f"e4_{name}{s}", shape, dt)) for s in range(slots)]
                    return bufs * (KS // slots)

                c = Products(sem, "e4", KS, "mask idx brk brk2 fq prod red wq al at fs bs mt dif m ex exw exv p evp")
                landed = [sem(f"e4_landed{s}") for s in range(KS)]
                stored = [sem(f"e4_stored{s}") for s in range(KS)]
                HR = TB * H
                drow, qs, kv = ring("drow", [P, TB, P], I32, 2), ring("qs", [P, TB, QW], slots=RS), ring("kv", [P, TB, 2 * D], slots=KS)
                dh, brk = ring("dh", [HR, P + 2], I32), ring("brk", [HR, P + 1])
                mask, row, idx = ring("mask", [P, TB, P], slots=KS), ring("row", [P, TB, RW], slots=RS), ring("idx", [P, TB], U32, KS)
                prod = ring("prod", [P, TB, D], slots=1)[0]
                red, wq, al = ring("red", [P, HR]), ring("wq", [P, HR]), ring("al", [P, HR])
                fs, bs, dif = ring("fs", [HR, P]), ring("bs", [HR, P]), ring("dif", [P, HR])
                msg = ring("msg", [P, TB, MW], slots=RS)
                ps_q, ps_p = (st.enter_context(nc.psum_tensor(f"e4_{k}", [P, 3 * BANK], F32)) for k in "qp")
                ps_a, ps_m = (st.enter_context(nc.psum_tensor(f"e4_{k}", [P, BANK], F32)) for k in "am")

                def in_bank(ps, t, width):
                    at = t // PT * BANK + t % PT * width
                    return ps[:, at:at + width]

                def many(ps, width, lo, hi):
                    return ps[:, 0:TM // PT * BANK].rearrange("p (b c) -> p b c", c=BANK)[:, :, 0:PT * width] \
                        .rearrange("p b (t f) -> p b t f", f=width)[:, :, :, lo:hi]

                def one(ps, width, lo, hi):
                    return in_bank(ps, TM, width)[:, lo:hi]

                def by_bank(a):
                    return a[:, 0:TM, :].rearrange("p (b t) f -> p b t f", t=PT)

                def row_free(eng, s, r):
                    if s >= RS:
                        c.hold(eng)
                        eng.wait_ge(stored[s - RS], (r + 1) * 16)
                    elif not (isinstance(r, int) and r == 0):
                        c.hold(eng)
                        eng.wait_ge(stored[s + KS - RS], r * 16)

                def weights(n):
                    return w_col[:, bass.ds(n * TB, TB)].unsqueeze(2).broadcast_to([P, TB, H])

                def heads(a):
                    return a.rearrange("p (t h) -> p t h", h=H)

                with nc.Block() as block:
                    @block.sync
                    def _(sp):
                        c.credit(sp)

                        def load(n, s, r):
                            c.free(sp, "mask", n, 2)
                            c.hold(sp)
                            sp.dma_start(drow[s][:, :, :].rearrange("p t e -> p (t e)"),
                                         dstflat[bass.ds(n * BW + 1, BW)].partition_broadcast(P)).then_inc(landed[s], 16)
                            c.free(sp, "fq", n, RS)
                            c.hold(sp)
                            sp.dma_start(qs[s][:, :, :], flat_rows(q_starts, n)).then_inc(landed[s], 16)
                            c.free(sp, "brk", n, ES)
                            c.hold(sp)
                            sp.dma_start(dh[s][:, :], dsthead[bass.ds(n * HR, HR), :]).then_inc(landed[s], 16)

                        pipelined(sp, NB, KS, [(0, load)])
                        for s in range(KS):
                            sp.wait_ge(stored[s], NB // KS * 16)

                    @block.gpsimd
                    def _(pool):
                        def gather(n, s, r):
                            c.ready(pool, "idx", n)
                            c.free(pool, "exv", n)
                            c.hold(pool)
                            for t in range(TB):
                                pool.indirect_dma_start(kv[s][:, t, :], None, kv_table[:, :],
                                                        bass.IndirectOffsetOnAxis(ap=idx[s][:, t:t + 1], axis=0)).then_inc(gathered[s], 16)

                        pipelined(pool, NB, KS, [(0, gather)])

                    @block.tensor
                    def _(pe):
                        def fill(n, s, r):
                            c.ready(pe, "mask", n)
                            pe.wait_ge(landed[s], (r + 1) * 48)
                            c.free(pe, "prod", n, 1)
                            c.free(pe, "wq", n, 1)
                            for t in range(TB):
                                last = nc.tensor.matmul(in_bank(ps_q, t, QW), mask[s][:, t, :], qs[s][:, t, :], start=True, stop=True)
                            last.then_inc(c["fq"], 1)

                        def turn(n, s, r):
                            c.ready(pe, "al", n)
                            c.free(pe, "fs", n, 1)
                            c.hold(pe)
                            nc.tensor.transpose(ps_a[0:HR, 0:P], al[s][:, :], ident[:, :]).then_inc(c["at"], 1)

                        def back(n, s, r):
                            c.ready(pe, "bs", n)
                            c.free(pe, "dif", n, 1)
                            c.free(pe, "m", n, 1)
                            c.hold(pe)
                            nc.tensor.transpose(ps_m[:, 0:HR], bs[s][:, :], ident[0:HR, 0:HR]).then_inc(c["mt"], 1)

                        def total(n, s, r):
                            c.ready(pe, "exv", n)
                            c.ready(pe, "exw", n)
                            c.free(pe, "evp", n, 1)
                            for t in range(TB):
                                last = nc.tensor.matmul(in_bank(ps_p, t, MW), mask[s][:, t, :], msg[s][:, t, :], start=True, stop=True)
                            last.then_inc(c["p"], 1)

                        pipelined(pe, NB, KS, [(4, total), (2, back), (0, fill), (1, turn)])

                    @block.scalar
                    def _(act):
                        def exp(n, s, r):
                            c.ready(act, "dif", n)
                            c.free(act, "p", n, RS)
                            nc.scalar.activation(msg[s][:, :, D:D + H], heads(dif[s][:, :]), ACT.Exp).then_inc(c["ex"], 1)

                        def evac(n, s, r):
                            row_free(act, s, r)
                            c.ready(act, "p", n)
                            nc.scalar.activation(by_bank(row[s])[:, :, :, 0:MW], many(ps_p, MW, 0, MW), ACT.Copy)
                            nc.scalar.activation(row[s][:, TM, 0:MW], one(ps_p, MW, 0, MW), ACT.Copy).then_inc(c["evp"], 1)

                        def store(n, s, r):
                            c.ready(act, "evp", n)
                            c.hold(act)
                            c.ready(act, "m", n)
                            act.dma_start(flat_rows(sums_att, n), row[s][:, :, :]).then_inc(stored[s], 16)

                        pipelined(act, NB, KS, [(0, exp), (1, evac), (1, store)], head=2)

                    @block.vector
                    def _(dve):
                        def message(n, s, r):
                            c.ready(dve, "ex", n)
                            dve.tensor_tensor(msg[s][:, :, D + H:MW], msg[s][:, :, D:D + H], weights(n), ALU.mult).then_inc(c["exw"], 1)
                            c.free(dve, "p", n, RS)
                            dve.tensor_tensor(msg[s][:, :, 0:D].rearrange("p t (h d) -> p t h d", d=HD),
                                              kv[s][:, :, D:2 * D].rearrange("p t (h d) -> p t h d", d=HD),
                                              msg[s][:, :, D:D + H].unsqueeze(3).broadcast_to([P, TB, H, HD]), ALU.mult).then_inc(c["exv"], 1)

                        def differ(n, s, r):
                            c.ready(dve, "mt", n)
                            c.free(dve, "ex", n, ES)
                            dve.tensor_tensor(dif[s][:, :], al[s][:, :], ps_m[:, 0:HR], ALU.subtract).then_inc(c["dif"], 1)
                            row_free(dve, s, r)
                            dve.tensor_copy(row[s][:, :, MW:RW], heads(ps_m[:, 0:HR])).then_inc(c["m"], 1)

                        def maxima(n, s, r):
                            c.ready(dve, "at", n)
                            c.ready(dve, "brk2", n)
                            dve.tensor_tensor_scan(fs[s][:, :], brk[s][:, 0:P], ps_a[0:HR, 0:P], -BIG, ALU.add, ALU.max).then_inc(c["fs"], 1)
                            c.ready(dve, "fs", n)
                            c.free(dve, "mt", n, ES)
                            dve.tensor_tensor_scan(bs[s][:, ::-1], brk[s][:, P:0:-1], fs[s][:, ::-1], -BIG, ALU.add, ALU.max).then_inc(c["bs"], 1)

                        def index(n, s, r):
                            nc.vector.tensor_copy(idx[s][:, :], src_i[:, bass.ds(n * TB, TB)].bitcast(U32)).then_inc(c["idx"], 1)

                        def masks(n, s, r):
                            dve.wait_ge(landed[s], (r + 1) * 48)
                            c.free(dve, "p", n)
                            mask_tile(dve, mask[s], drow[s], n).then_inc(c["mask"], 1)
                            c.free(dve, "bs", n, ES)
                            dve.tensor_tensor(brk[s][:, :], dh[s][:, 0:P + 1], dh[s][:, 1:P + 2], ALU.not_equal).then_inc(c["brk"], 1)
                            c.ready(dve, "brk", n)
                            dve.tensor_scalar(brk[s][:, :], brk[s][:, :], -BIG, None, ALU.mult).then_inc(c["brk2"], 1)

                        def scores(n, s, r):
                            c.ready(dve, "fq", n)
                            wait_rows(dve, s, r, TB)
                            c.free(dve, "red", n, 1)
                            dve.tensor_tensor(by_bank(prod), many(ps_q, QW, 0, D), by_bank(kv[s])[:, :, :, 0:D], ALU.mult)
                            dve.tensor_tensor(prod[:, TM, :], one(ps_q, QW, 0, D), kv[s][:, TM, 0:D], ALU.mult).then_inc(c["prod"], 1)
                            dve.tensor_tensor(by_bank(heads(wq[s][:, :])), many(ps_q, QW, D, QW), by_bank(weights(n)), ALU.mult)
                            dve.tensor_tensor(heads(wq[s][:, :])[:, TM, :], one(ps_q, QW, D, QW), weights(n)[:, TM, :], ALU.mult).then_inc(c["wq"], 1)
                            c.ready(dve, "prod", n)
                            dve.tensor_reduce(red[s][:, :], prod[:, :, :].rearrange("p t (h d) -> p (t h) d", d=HD), AX.X, ALU.add).then_inc(c["red"], 1)
                            c.ready(dve, "red", n)
                            c.free(dve, "dif", n, ES)
                            dve.tensor_tensor(al[s][:, :], red[s][:, :], wq[s][:, :], ALU.add).then_inc(c["al"], 1)

                        pipelined(dve, NB, KS, [(7, message), (6, differ), (5, maxima), (0, index), (3, masks), (4, scores)], head=2)
            count_rows(KS, NB, TB)

        def join_tails(scaled):
            with ExitStack() as st:
                def tmp(name, shape, dt=F32):
                    return st.enter_context(nc.sbuf_tensor(f"j_{name}", shape, dt))

                loaded, dv, pe_s, ac, masked = sem("j_loaded"), sem("j_dve"), sem("j_pe"), sem("j_act"), sem("j_masked")
                tail, head = tmp("tail", [TP, TK, RW]), tmp("head", [TP, TK, H])
                ht, lastrow = tmp("ht", [TP, TK, 5], I32), tmp("lastrow", [H, ET + 2], I32)
                same, twice, both, lastf = (tmp(k, [TP, TK]) for k in "same twice both lastf".split())
                mm, dif, sc = tmp("mm", [TP, TK, H]), tmp("dif", [TP, 2, TK, H]), tmp("sc", [TP, 2, TK, H])
                brk, fs, bs = tmp("brk", [H, ET + 1]), tmp("fs", [H, ET]), tmp("bs", [H, ET])
                ps = [st.enter_context(nc.psum_tensor(f"j_ps{s}", [P, 512], F32)) for s in range(2)]
                with nc.Block() as block:
                    @block.sync
                    def _(sp):
                        sp.dma_start(tail[:, :, :], tails(sums_att, RW)).then_inc(loaded, 16)
                        with nc.allow_non_contiguous_dma(reason="one maximum per head and edge tile"):
                            sp.dma_start(head[:, :, :], sums_att[P:EP + P, :].rearrange("(k p e) f -> p k e f", e=P, p=TP)[:, :, 0, MW:RW]).then_inc(loaded, 16)
                        sp.dma_start(ht[:, :, :], headtail).then_inc(loaded, 16)
                        sp.dma_start(lastrow[:, :], lasthead).then_inc(loaded, 16)

                    @block.tensor
                    def _(pe):
                        pe.wait_ge(dv, 7)
                        for k in range(TK):
                            last = nc.tensor.transpose(ps[0][0:H, k * TP:(k + 1) * TP], mm[:, k, :], ident[0:TP, 0:TP])
                        last.then_inc(pe_s, 1)
                        pe.wait_ge(dv, 11)
                        for k in range(TK):
                            last = nc.tensor.transpose(ps[1][0:TP, k * H:(k + 1) * H], bs[:, k * TP:(k + 1) * TP], ident[0:H, 0:H])
                        last.then_inc(pe_s, 1)

                    @block.scalar
                    def _(act):
                        act.wait_ge(dv, 13)
                        nc.scalar.activation(sc[:, :, :, :], dif[:, :, :, :], ACT.Exp).then_inc(ac, 1)

                    @block.vector
                    def _(dve):
                        n = [0]

                        def after(ins):
                            n[0] += 1
                            ins.then_inc(dv, 1)
                            dve.wait_ge(dv, n[0])

                        dve.wait_ge(loaded, 64)
                        after(dve.tensor_tensor(same[:, :], ht[:, :, 0], ht[:, :, 1], ALU.is_equal))
                        after(dve.tensor_tensor(twice[:, :], ht[:, :, 2], ht[:, :, 3], ALU.is_equal))
                        after(dve.tensor_tensor(both[:, :], ht[:, :, 0], ht[:, :, 2], ALU.is_equal))
                        after(dve.tensor_tensor(both[:, :], both[:, :], twice[:, :], ALU.mult))
                        after(dve.tensor_scalar(lastf[:, :], both[:, :], -1.0, 1.0, ALU.mult, ALU.add))
                        after(dve.tensor_scalar(twice[:, :], same[:, :], 1.0, BIG, ALU.subtract, ALU.mult))
                        dve.tensor_tensor(head[:, :, :], head[:, :, :], twice[:, :].unsqueeze(2).broadcast_to([TP, TK, H]), ALU.add).then_inc(masked, 1)
                        dve.wait_ge(masked, 1)
                        after(dve.tensor_tensor(mm[:, :, :], tail[:, :, MW:RW], head[:, :, :], ALU.max))
                        after(dve.tensor_tensor(brk[:, :], lastrow[:, 0:ET + 1], lastrow[:, 1:ET + 2], ALU.not_equal))
                        after(dve.tensor_scalar(brk[:, :], brk[:, :], -BIG, None, ALU.mult))
                        dve.wait_ge(pe_s, 1)
                        after(dve.tensor_tensor_scan(fs[:, :], brk[:, 0:ET], ps[0][0:H, 0:ET], -BIG, ALU.add, ALU.max))
                        after(dve.tensor_tensor_scan(bs[:, ::-1], brk[:, ET:0:-1], fs[:, ::-1], -BIG, ALU.add, ALU.max))
                        dve.wait_ge(pe_s, 2)
                        m_all = ps[1][0:TP, 0:TK * H].rearrange("p (k h) -> p k h", h=H)
                        after(dve.tensor_tensor(dif[:, 0, :, :], tail[:, :, MW:RW], m_all, ALU.subtract))
                        after(dve.tensor_tensor(dif[:, 1, :, :], head[:, :, :], m_all, ALU.subtract))
                        dve.wait_ge(ac, 1)
                        for k in range(TK):
                            dve.tensor_tensor(scaled[:, k, 0:D].rearrange("p (h d) -> p h d", d=HD),
                                              tail[:, k, 0:D].rearrange("p (h d) -> p h d", d=HD),
                                              sc[:, 0, k, :].unsqueeze(2).broadcast_to([TP, H, HD]), ALU.mult)
                            dve.tensor_tensor(scaled[:, k, D:MW].rearrange("p (a h) -> p a h", h=H),
                                              tail[:, k, D:MW].rearrange("p (a h) -> p a h", h=H),
                                              sc[:, 0, k, :].unsqueeze(1).broadcast_to([TP, 2, H]), ALU.mult)
                        dve.tensor_tensor(scaled[:, :, MW:RW], sc[:, 1, :, :], lastf[:, :].unsqueeze(2).broadcast_to([TP, TK, H]), ALU.mult)
                        dve.tensor_copy(scaled[:, :, RW:SW], lastf[:, :].unsqueeze(2))

        def nodes_attention(scaled, att):
            with ExitStack() as st:
                def ring(name, shape, dt=F32, slots=NS):
                    return [st.enter_context(nc.sbuf_tensor(f"n4_{name}{s}", shape, dt)) for s in range(slots)]

                c = Products(sem, "n4", NS, "idx z zt nl en t1 t2 sum")
                idx, g, z = ring("idx", [P, 1], U32), ring("g", [P, RW]), ring("z", [TP, TK, P])
                nl, en = ring("nl", [P, 1]), ring("en", [P, H])
                ps = [st.enter_context(nc.psum_tensor(f"n4_ps{s}", [P, 512], F32)) for s in range(NS)]
                with nc.Block() as block:
                    @block.sync
                    def _(sp):
                        c.credit(sp)

                    @block.gpsimd
                    def _(pool):
                        def gather(n, s, r):
                            c.ready(pool, "idx", n)
                            c.free(pool, "sum", n)
                            c.hold(pool)
                            pool.indirect_dma_start(g[s][:, :], None, sums_att[:, :],
                                                    bass.IndirectOffsetOnAxis(ap=idx[s][:, :], axis=0)).then_inc(gathered[s], 16)

                        pipelined(pool, NT, NS, [(0, gather)])

                    @block.tensor
                    def _(pe):
                        def earlier(n, s, r):
                            c.ready(pe, "z", n)
                            c.free(pe, "sum", n)
                            for k in range(TK):
                                last = nc.tensor.matmul(ps[s][:, 0:SW], z[s][:, k, :], scaled[:, k, :], start=(k == 0), stop=(k == TK - 1))
                            last.then_inc(c["zt"], 1)

                        pipelined(pe, NT, NS, [(0, earlier)])

                    @block.vector
                    def _(dve):
                        def index(n, s, r):
                            c.free(dve, "sum", n)
                            nc.vector.tensor_copy(idx[s][:, :], col(end_row, n)).then_inc(c["idx"], 1)
                            c.free(dve, "zt", n)
                            pick(dve, z[s], n).then_inc(c["z"], 1)

                        def whole(n, s, r):
                            c.ready(dve, "zt", n)
                            dve.tensor_scalar(nl[s][:, :], ps[s][:, RW:SW], -1.0, 1.0, ALU.mult, ALU.add).then_inc(c["nl"], 1)
                            c.ready(dve, "nl", n)
                            dve.tensor_scalar(en[s][:, :], ps[s][:, MW:RW], nl[s][:, 0:1], None, ALU.add).then_inc(c["en"], 1)
                            c.ready(dve, "en", n)
                            wait_rows(dve, s, r)
                            dve.tensor_tensor(g[s][:, 0:D].rearrange("p (h d) -> p h d", d=HD), g[s][:, 0:D].rearrange("p (h d) -> p h d", d=HD),
                                              en[s][:, :].unsqueeze(2).broadcast_to([P, H, HD]), ALU.mult).then_inc(c["t1"], 1)
                            dve.tensor_tensor(g[s][:, D:MW].rearrange("p (a h) -> p a h", h=H), g[s][:, D:MW].rearrange("p (a h) -> p a h", h=H),
                                              en[s][:, :].unsqueeze(1).broadcast_to([P, 2, H]), ALU.mult).then_inc(c["t2"], 1)
                            c.ready(dve, "t1", n)
                            c.ready(dve, "t2", n)
                            dve.tensor_tensor(tile_of(att, n), g[s][:, 0:MW], ps[s][:, 0:MW], ALU.add).then_inc(c["sum"], 1)

                        pipelined(dve, NT, NS, [(0, index), (1, whole)])
            count_rows(NS, NT)

        def layer3_nodes():
            with ExitStack() as st:
                scaled = st.enter_context(nc.sbuf_tensor("scaled", [TP, TK, SW], F32))
                att = st.enter_context(nc.sbuf_tensor("att", [P, NT, MW], F32))
                join_tails(scaled)
                nodes_attention(scaled, att)
                finish(att)

        def finish(att):
            with ExitStack() as st:
                k = Steps("fin")
                c = Products(sem, "fo", NS, "xs tr at mm res stat")
                norm = RowNorm(st, "fin_rows", h_now)
                with_beta, scaled, added, skipped = (sem(f"fin_{k}") for k in "with_beta scaled added skipped".split())
                sq = st.enter_context(nc.sbuf_tensor("fin_sq", [P, NT, D], F32))
                den = st.enter_context(nc.sbuf_tensor("fin_den", [P, NT, H], F32))
                xs = [st.enter_context(nc.sbuf_tensor(f"fin_xs{s}", [P, D], F32)) for s in range(NS)]
                xT = [st.enter_context(nc.sbuf_tensor(f"fin_xT{s}", [P, P], F32)) for s in range(NS)]
                ps = [st.enter_context(nc.psum_tensor(f"fin_ps{s}", [P, 512], F32)) for s in range(2)]
                dv, stored = k.sem["dve"], k.sem["dma"]
                with nc.Block() as block:
                    @block.sync
                    def _(sp):
                        c.credit(sp)
                        half, full = norm.HALF, N // P
                        sp.wait_ge(norm.first_done, 2)
                        sp.dma_start(out[0:half * P, :].rearrange("(j p) f -> p j f", p=P), h_now[:, 0:half, :]).then_inc(stored, 16)
                        sp.wait_ge(norm.others_done, 2)
                        sp.dma_start(out[half * P:full * P, :].rearrange("(j p) f -> p j f", p=P), h_now[:, half:full, :]).then_inc(stored, 16)
                        sp.dma_start(out[full * P:N, :], h_now[0:N - full * P, full, :]).then_inc(stored, 16)
                        sp.wait_ge(stored, 48)

                    @block.gpsimd
                    def _(pool):
                        pool.wait_ge(dv, 5)
                        pool.tensor_tensor(h_now[:, MINE:NT, :], sq[:, MINE:NT, :], h_now[:, MINE:NT, :], ALU.add).then_inc(skipped, 1)
                        pool.wait_ge(dv, 6)
                        pool.wait_ge(skipped, 1)
                        pool.tensor_tensor(sq[:, :, :], x_now[:, :, :], cols(bc[:, B_B3:B_B3 + 1, :]), ALU.add).then_inc(with_beta, 1)
                        pool.wait_ge(norm.others_done, 1)
                        pool.tensor_tensor(h_now[:, MINE:NT, :], h_now[:, MINE:NT, :],
                                           bc[:, B_G3:B_G3 + 1, :].broadcast_to([P, NT - MINE, D]), ALU.mult).then_inc(scaled, 1)
                        pool.wait_ge(scaled, 1)
                        pool.wait_ge(with_beta, 1)
                        pool.tensor_tensor(h_now[:, MINE:NT, :], h_now[:, MINE:NT, :], sq[:, MINE:NT, :], ALU.add).then_inc(added, 1)

                    @block.tensor
                    def _(pe):
                        def turn(n, s, r):
                            c.ready(pe, "xs", n)
                            c.free(pe, "at", n, 1)
                            c.hold(pe)
                            nc.tensor.transpose(ps[0][:, 0:P], xs[s][:, :], ident[:, :]).then_inc(c["tr"], 1)

                        def product(n, s, r):
                            c.ready(pe, "at", n)
                            c.free(pe, "res", n, 1)
                            nc.tensor.matmul(ps[1][:, 0:D], ones[0:1, :], wr[:, R_O, :], start=True, stop=False)
                            nc.tensor.matmul(ps[1][:, 0:D], xT[s][:, :], wm[:, W_O, :], start=False, stop=True).then_inc(c["mm"], 1)

                        pipelined(pe, NT, NS, [(0, turn), (1, product)])

                    @block.scalar
                    def _(act):
                        act.wait_ge(dv, 6)
                        act.wait_ge(skipped, 1)

                        def own(n, s, r):
                            c.free(act, "tr", n)
                            nc.scalar.activation(xs[s][:, :], tile_of(h_now, n), ACT.Copy).then_inc(c["xs"], 1)

                        def move(n, s, r):
                            c.ready(act, "tr", n)
                            c.free(act, "mm", n)
                            nc.scalar.activation(xT[s][:, :], ps[0][:, 0:P], ACT.Copy).then_inc(c["at"], 1)

                        pipelined(act, NT, NS, [(0, own), (1, move)])
                        norm.root(act, 1)
                        norm.root(act, 2)

                    @block.vector
                    def _(dve):
                        dve.tensor_scalar(den[:, :, :], att[:, :, D:D + H], 1e-16, None, ALU.max).then_inc(dv, 1)
                        dve.tensor_tensor(sq[:, :, :].rearrange("p j (h d) -> p j h d", d=HD),
                                          bc[:, B_WE, :].rearrange("p (h d) -> p h d", d=HD).unsqueeze(1).broadcast_to([P, NT, H, HD]),
                                          att[:, :, D + H:MW].unsqueeze(3).broadcast_to([P, NT, H, HD]), ALU.mult).then_inc(dv, 1)
                        dve.wait_ge(dv, 1)
                        dve.reciprocal(den[:, :, :], den[:, :, :]).then_inc(dv, 1)
                        dve.wait_ge(dv, 2)
                        dve.tensor_tensor(sq[:, :, :], sq[:, :, :], att[:, :, 0:D], ALU.add).then_inc(dv, 1)
                        dve.wait_ge(dv, 4)
                        dve.tensor_tensor(sq[:, :, :].rearrange("p j (h d) -> p (j h) d", d=HD), sq[:, :, :].rearrange("p j (h d) -> p (j h) d", d=HD),
                                          den[:, :, :].rearrange("p j h -> p (j h)").unsqueeze(2).broadcast_to([P, NT * H, HD]), ALU.mult).then_inc(dv, 1)
                        dve.wait_ge(dv, 5)
                        dve.tensor_tensor(h_now[:, 0:MINE, :], sq[:, 0:MINE, :], h_now[:, 0:MINE, :], ALU.add).then_inc(dv, 1)

                        def residual(n, s, r):
                            c.ready(dve, "mm", n)
                            dve.tensor_tensor(tile_of(h_now, n), ps[1][:, 0:D], tile_of(x_now, n), ALU.add).then_inc(c["res"], 1)

                            c.ready(dve, "res", n)
                            dve.bn_stats(tile_of(norm.stat, n), tile_of(h_now, n)).then_inc(c["stat"], 1)

                        pipelined(dve, NT, NS, [(0, residual)])
                        dve.wait_ge(c["stat"], NT + NS)
                        norm.aggregate(dve)
                        norm.apply(dve, 1)
                        dve.wait_ge(norm.first_done, 1)
                        dve.wait_ge(norm.others_done, 1)
                        dve.tensor_tensor(h_now[:, 0:MINE, :], h_now[:, 0:MINE, :],
                                          bc[:, B_G3:B_G3 + 1, :].broadcast_to([P, MINE, D]), ALU.mult).then_inc(dv, 1)
                        dve.wait_ge(dv, 7)
                        dve.wait_ge(with_beta, 1)
                        dve.tensor_tensor(h_now[:, 0:MINE, :], h_now[:, 0:MINE, :], sq[:, 0:MINE, :], ALU.add).then_inc(dv, 1)
                        dve.wait_ge(dv, 8)
                        dve.wait_ge(added, 1)
                        norm.stats(dve)
                        norm.apply(dve, 2)

        stages = [
            prepare,
            edges_layer0,
            lambda: degrees("d0", deg_in, True),
            hidden_bias,
            nodes_layer0,
            lambda: edges_sum("e1", tab[1], sums[1], count_src=True),
            lambda: degrees("d1", deg_out, False),
            lambda: nodes_sage("n1a", sums[1], tab[2], x_now, W_S0, W_N0, R_S0, False),
            lambda: edges_sum("e2", tab[2], sums[2], clear=q_starts),
            lambda: nodes_sage("n1b", sums[2], tab[3], h_now, W_S1, W_N1, R_S1, True),
            lambda: edges_sum("e3", tab[3], sums[3]),
            nodes_gcn,
            batch_norm,
            project,
            edges_attention,
            layer3_nodes,
        ]
        for stage in stages:
            stage()
            end_stage()


def kernel(**inputs):
    import numpy as np
    import concourse.bacc as bacc
    from concourse.bass_utils import run_bass_kernel_spmd as run

    a = {k: np.ascontiguousarray(v) for k, v in inputs.items()}
    f4 = np.float32

    def heads_last(w):
        return w.transpose(1, 0, 2).reshape(D, H * HD)

    def cut(w):
        return [w[i:i + P, j:j + P] for i in range(0, w.shape[0], P) for j in range(0, w.shape[1], P)]

    x = np.zeros((NP, D), f4)
    x[:N] = a["x"]
    src = np.full((EP,), N, np.int32)
    src[:E] = a["src"]
    dst = np.full((EP,), NP, np.int32)
    dst[:E] = a["dst"]
    flat = np.full((EP + 2,), -1, np.int32)
    flat[1:EP + 1] = dst
    wts = np.zeros((EP,), f4)
    wts[:E] = a["edge_weight"]
    edges = np.zeros((D, EP), f4)
    edges[:, :E] = a["edge_attr_128"].T
    first, last = dst[0::P], dst[P - 1::P]
    after = [np.append(v[1:], np.int32(-1)) for v in (first, last)]
    after2 = np.append(after[0][1:], np.int32(-1))
    headtail = np.stack([last, after[0], after[1], after2, first], -1).reshape(TK, TP, 5).transpose(1, 0, 2)
    window = np.lib.stride_tricks.sliding_window_view(flat, P + 2)[::P]
    dsthead = np.repeat(window.reshape(ET, 1, P + 2), H, 1).reshape(ET * H, P + 2)
    lastrow = np.full((ET + 2,), -1, np.int32)
    lastrow[1:ET + 1] = last
    mats = cut(a["L0_gnn_W_e_k"]) + cut(a["L0_gnn_W1"]) + cut(a["L0_gnn_W2"])
    for k in ("L1_gnn_W_self0", "L1_gnn_W_neigh0", "L1_gnn_W_self1", "L1_gnn_W_neigh1", "L2_gnn_W"):
        mats += cut(a[k])
    mats += [heads_last(a[f"L3_gnn_W{k}"]) for k in ("q", "k", "v", "skip")] + [a["L3_gnn_Wo"]]
    rows = [a["L0_gnn_b2"], a["L1_gnn_b0"], a["L1_gnn_b1"]] + [a["L3_gnn_bo"]]
    wide = [a["L0_gnn_W_e_b"], a["L2_gnn_gamma"], a["L2_gnn_beta"], a["L3_gnn_We"].reshape(-1), a["L3_gnn_gamma"], a["L3_gnn_beta"]]
    wide += [a[f"L3_gnn_b{k}"].reshape(-1) for k in ("q", "k", "v", "skip")]
    gvec = np.concatenate([a["L0_gnn_globals_g"].reshape(P, 1), np.broadcast_to(a["L0_gnn_eps"], (P, 1)), a["L0_gnn_b1"].reshape(4, P).T], 1)

    def per_partition(v):
        return v.reshape(ET, P).T

    given = {
        "xp": x, "srccol": per_partition(src), "dstcol": per_partition(dst), "dstflat": flat, "dsthead": dsthead,
        "lasthead": np.broadcast_to(lastrow, (H, ET + 2)), "headtail": headtail, "wcol": per_partition(wts),
        "edgesT": edges, "wmat": np.stack(mats, 1), "wrow": np.stack(rows)[None], "wbc": np.stack(wide), "gvec": gvec,
    }
    nc = bacc.Bacc("TRN2", target_bir_lowering=False, num_devices=1)
    arrays, args = {}, {}
    for name, v in given.items():
        v = np.ascontiguousarray(v)
        arrays[f"in_{name}"] = v
        args[name] = nc.dram_tensor(f"in_{name}", v.shape, mybir.dt.from_np(v.dtype), kind="ExternalInput").ap()
    args["out"] = nc.dram_tensor("out", (N, D), F32, kind="ExternalOutput").ap()
    gnn_kernel(nc, **args)
    return run(nc, [arrays], core_ids=[0]).results[0]["out"]
```
